# Optimizing a Trainium2 kernel written in Bass

```python
import numpy as np
import jax
import jax.numpy as jnp

def _softmax(x, axis=-1):
    return jax.nn.softmax(x, axis=axis)

def _gelu(x):
    return jax.nn.gelu(x, approximate=True)

def _silu(x):
    return jax.nn.silu(x)

def _sigmoid(x):
    return jax.nn.sigmoid(x)

def _layernorm(x, axis=-1, eps=1e-05):
    m = jnp.mean(x, axis=axis, keepdims=True)
    v = jnp.var(x, axis=axis, keepdims=True)
    return (x - m) / jnp.sqrt(v + eps)

def _scatter_add(tgt, idx, src, axis=0):
    return tgt.at[idx].add(src)

def _segment_sum(src, seg, n):
    return jax.ops.segment_sum(src, seg, n)
kernel_name = 'mk_decoder_preln_d1_seqx_r4_3ccc3a'

def setup_inputs(seed: int=0):
    np.random.seed(seed)
    _w = jnp.asarray

    def _rec_inputs():
        import jax
        import jax.numpy as jnp
        _rk = jax.random.key(seed)
        x = -7.109e-05 + 0.9999 * jax.random.normal(jax.random.fold_in(_rk, 1), (16, 128, 1024), jnp.float32)
        _lenS = 128 - jax.random.randint(jax.random.fold_in(_rk, 7), (16,), 0, max(1, 128 // 4) + 1, jnp.int32)
        _lenS2 = 128 - jax.random.randint(jax.random.fold_in(_rk, 8), (16,), 0, max(1, 128 // 4) + 1, jnp.int32)
        _ctx_4096P = jax.random.normal(jax.random.fold_in(_rk, 11), (16, 16, 1024), jnp.float32)
        _ctx_4096c = jax.random.dirichlet(jax.random.fold_in(_rk, 511), 0.3 * jnp.ones((16,), jnp.float32), (16, 128))
        _ctx_4096t = jnp.einsum('bsk,bkd->bsd', _ctx_4096c, _ctx_4096P)
        _ctx_4096t = _ctx_4096t * jax.lax.rsqrt(jnp.mean(jnp.square(_ctx_4096t)) + 1e-12) * 0.953939
        ctx_4096 = -0.00010331 + 0.999899 * (_ctx_4096t + 0.3 * jax.random.normal(jax.random.fold_in(_rk, 611), (16, 128, 1024), jnp.float32))
        return (x, ctx_4096)
    x, ctx_4096 = _rec_inputs()

    def _L0_attn_setup():
        import jax, jax.numpy as jnp
        import numpy as np
        B, S, D = (1, 512, 1024)
        H = 32
        QL = 384
        KVL = 128
        DN = 128
        DR = 64
        DV = 128
        BASE = 10000.0
        FACTOR = 40.0
        BFAST, BSLOW = (32.0, 1.0)
        OLD_CTX = 4096.0
        MSCALE = 1.0

        def _yarn_inv_freq():
            freqs = 1.0 / BASE ** (jnp.arange(0, DR, 2, dtype=jnp.float32) / DR)
            wavelengths = 2.0 * jnp.pi / freqs
            ramp = jnp.clip((wavelengths / OLD_CTX - BSLOW) / (BFAST - BSLOW), 0.0, 1.0)
            scale = 1.0 - ramp + ramp * FACTOR
            return (freqs / scale, MSCALE)

        def _apply_rope(x, inv_freq, mscale):
            seq = x.shape[-2]
            pos = jnp.arange(seq, dtype=jnp.float32)
            f = jnp.concatenate([pos[:, None] * inv_freq[None, :]] * 2, axis=-1)
            cos = jnp.cos(f) * mscale
            sin = jnp.sin(f) * mscale
            half = DR // 2
            x1, x2 = (x[..., :half], x[..., half:])
            c1, c2 = (cos[:, :half], cos[:, half:])
            s2 = sin[:, half:]
            return jnp.concatenate([x1 * c1 - x2 * s2, x1 * s2 + x2 * c2], axis=-1)
        key = jax.random.key(seed)
        ks = jax.random.split(key, 10)

        def glorot(k, shape):
            lim = np.sqrt(6.0 / (shape[0] + shape[1])).astype(np.float32)
            return jax.random.uniform(k, shape, jnp.float32, -lim, lim)
        return {'hidden_states': jax.random.normal(ks[0], (B, S, D), jnp.float32), 'w_q_down': glorot(ks[1], (D, QL)), 'w_q_up_nope': glorot(ks[2], (QL, H * DN)), 'w_q_up_rope': glorot(ks[3], (QL, H * DR)), 'w_kv_down': glorot(ks[4], (D, KVL)), 'w_k_rope': glorot(ks[5], (D, DR)), 'w_uk': glorot(ks[6], (H * DN, KVL)), 'w_uv': glorot(ks[7], (H * DV, KVL)), 'w_out': glorot(ks[8], (H * DV, D))}
    _L0_attn_all = _L0_attn_setup()
    _L0_attn_in = {k: v for k, v in _L0_attn_all.items() if k in ('w_q_down', 'w_q_up_nope', 'w_q_up_rope', 'w_kv_down', 'w_k_rope', 'w_uk', 'w_uv', 'w_out')}
    del _L0_attn_all

    def _L0_xattn_setup():
        import jax, jax.numpy as jnp
        import numpy as np
        key = jax.random.key(seed)
        k1, k2 = jax.random.split(key)
        B, Lq, Lk, D = (16, 256, 512, 1024)
        query = jax.random.normal(k1, (B, Lq, D), dtype=jnp.float32)
        key_t = jax.random.normal(k2, (B, Lk, D), dtype=jnp.float32)
        return {'query': query, 'key': key_t}
    _L0_xattn_all = _L0_xattn_setup()
    _L0_xattn_in = {k: v for k, v in _L0_xattn_all.items() if k in ()}
    del _L0_xattn_all

    def _L0_ffn_setup():
        import jax, jax.numpy as jnp
        import numpy as np
        import math
        D = 1024
        TOKENS = (4, 512)
        P = 0.8

        def conn_dense(kernel, x):
            w = jnp.where(kernel, jnp.asarray(1.0, x.dtype), jnp.asarray(-1.0, x.dtype))
            return x @ w

        def ei_dense(x, kernel, scale, p):
            in_dim = x.shape[-1]
            ne = round(in_dim * p)
            x_exc = x[..., :ne]
            x_inh = x[..., ne:]
            xx = jnp.concatenate([x_exc, -p / (1.0 - p) * x_inh], axis=-1)
            return scale * conn_dense(kernel, xx)
        key = jax.random.key(seed)
        ks = jax.random.split(key, 4)
        x = jax.random.normal(ks[0], (*TOKENS, D), dtype=jnp.float32)
        k0 = jax.random.bernoulli(ks[1], 0.5, (D, D))
        k1 = jax.random.bernoulli(ks[2], 0.5, (D, D))
        k2 = jax.random.bernoulli(ks[3], 0.5, (D, D))
        s = jnp.asarray(1.0 / math.sqrt(D), dtype=jnp.float32)
        return {'x': x, 'k0': k0, 's0': s, 'k1': k1, 's1': s, 'k2': k2, 's2': s}
    _L0_ffn_all = _L0_ffn_setup()
    _L0_ffn_in = {k: v for k, v in _L0_ffn_all.items() if k in ('k0', 's0', 'k1', 's1', 'k2', 's2')}
    del _L0_ffn_all
    return {'x': x, 'ctx_4096': ctx_4096, 'L0_attn_w_q_down': _L0_attn_in['w_q_down'], 'L0_attn_w_q_up_nope': _L0_attn_in['w_q_up_nope'], 'L0_attn_w_q_up_rope': _L0_attn_in['w_q_up_rope'], 'L0_attn_w_kv_down': _L0_attn_in['w_kv_down'], 'L0_attn_w_k_rope': _L0_attn_in['w_k_rope'], 'L0_attn_w_uk': _L0_attn_in['w_uk'], 'L0_attn_w_uv': _L0_attn_in['w_uv'], 'L0_attn_w_out': _L0_attn_in['w_out'], 'L0_ffn_k0': _L0_ffn_in['k0'], 'L0_ffn_s0': _L0_ffn_in['s0'], 'L0_ffn_k1': _L0_ffn_in['k1'], 'L0_ffn_s1': _L0_ffn_in['s1'], 'L0_ffn_k2': _L0_ffn_in['k2'], 'L0_ffn_s2': _L0_ffn_in['s2']}

def reference(x, ctx_4096, L0_attn_w_q_down, L0_attn_w_q_up_nope, L0_attn_w_q_up_rope, L0_attn_w_kv_down, L0_attn_w_k_rope, L0_attn_w_uk, L0_attn_w_uv, L0_attn_w_out, L0_ffn_k0, L0_ffn_s0, L0_ffn_k1, L0_ffn_s1, L0_ffn_k2, L0_ffn_s2):
    import jax
    import jax.numpy as jnp

    def _L0_attn_ref(hidden_states, w_q_down, w_q_up_nope, w_q_up_rope, w_kv_down, w_k_rope, w_uk, w_uv, w_out):
        import jax, jax.numpy as jnp
        import numpy as np
        B, S, D = (1, 512, 1024)
        H = 32
        QL = 384
        KVL = 128
        DN = 128
        DR = 64
        DV = 128
        BASE = 10000.0
        FACTOR = 40.0
        BFAST, BSLOW = (32.0, 1.0)
        OLD_CTX = 4096.0
        MSCALE = 1.0

        def _yarn_inv_freq():
            freqs = 1.0 / BASE ** (jnp.arange(0, DR, 2, dtype=jnp.float32) / DR)
            wavelengths = 2.0 * jnp.pi / freqs
            ramp = jnp.clip((wavelengths / OLD_CTX - BSLOW) / (BFAST - BSLOW), 0.0, 1.0)
            scale = 1.0 - ramp + ramp * FACTOR
            return (freqs / scale, MSCALE)

        def _apply_rope(x, inv_freq, mscale):
            seq = x.shape[-2]
            pos = jnp.arange(seq, dtype=jnp.float32)
            f = jnp.concatenate([pos[:, None] * inv_freq[None, :]] * 2, axis=-1)
            cos = jnp.cos(f) * mscale
            sin = jnp.sin(f) * mscale
            half = DR // 2
            x1, x2 = (x[..., :half], x[..., half:])
            c1, c2 = (cos[:, :half], cos[:, half:])
            s2 = sin[:, half:]
            return jnp.concatenate([x1 * c1 - x2 * s2, x1 * s2 + x2 * c2], axis=-1)
        b, s, _ = hidden_states.shape
        c_q = hidden_states @ w_q_down
        q_nope = (c_q @ w_q_up_nope).reshape(b, s, H, DN).transpose(0, 2, 1, 3)
        q_rope = (c_q @ w_q_up_rope).reshape(b, s, H, DR).transpose(0, 2, 1, 3)
        c_kv = hidden_states @ w_kv_down
        k_rope = (hidden_states @ w_k_rope)[:, None]
        inv_freq, mscale = _yarn_inv_freq()
        q_rope = _apply_rope(q_rope, inv_freq, mscale)
        k_rope = _apply_rope(k_rope, inv_freq, mscale)
        wuk = w_uk.reshape(H, DN, KVL)
        q_lat = jnp.einsum('bhsd,hdr->bhsr', q_nope, wuk)
        scores = jnp.einsum('bhsr,btr->bhst', q_lat, c_kv) + jnp.einsum('bhsd,btd->bhst', q_rope, k_rope[:, 0])
        scores = scores / jnp.sqrt(jnp.float32(DN + DR))
        causal = jnp.tril(jnp.ones((s, s), dtype=bool))
        scores = jnp.where(causal, scores, jnp.finfo(scores.dtype).min)
        probs = jax.nn.softmax(scores, axis=-1)
        out_lat = jnp.einsum('bhst,btr->bhsr', probs, c_kv)
        wuv = w_uv.reshape(H, DV, KVL)
        out = jnp.einsum('bhsr,hdr->bhsd', out_lat, wuv)
        out = out.transpose(0, 2, 1, 3).reshape(b, s, H * DV)
        return out @ w_out

    def _L0_xattn_ref(query, key):
        import jax, jax.numpy as jnp
        import numpy as np
        a = jnp.einsum('bqd,bkd->bqk', query, key)
        e = jax.nn.softmax(a, axis=-1)
        c = jnp.einsum('bqk,bkd->bqd', e, key)
        return c

    def _L0_ffn_ref(x, k0, s0, k1, s1, k2, s2):
        import jax, jax.numpy as jnp
        import numpy as np
        import math
        D = 1024
        TOKENS = (4, 512)
        P = 0.8

        def conn_dense(kernel, x):
            w = jnp.where(kernel, jnp.asarray(1.0, x.dtype), jnp.asarray(-1.0, x.dtype))
            return x @ w

        def ei_dense(x, kernel, scale, p):
            in_dim = x.shape[-1]
            ne = round(in_dim * p)
            x_exc = x[..., :ne]
            x_inh = x[..., ne:]
            xx = jnp.concatenate([x_exc, -p / (1.0 - p) * x_inh], axis=-1)
            return scale * conn_dense(kernel, xx)
        h = s0 * conn_dense(k0, x)
        h = jax.nn.relu(h) * 2.0
        h = ei_dense(h, k1, s1, P)
        h = jax.nn.relu(h) * 2.0
        return ei_dense(h, k2, s2, P)
    x = x + _L0_attn_ref(_layernorm(x, axis=-1), L0_attn_w_q_down, L0_attn_w_q_up_nope, L0_attn_w_q_up_rope, L0_attn_w_kv_down, L0_attn_w_k_rope, L0_attn_w_uk, L0_attn_w_uv, L0_attn_w_out)
    x = x + _L0_xattn_ref(_layernorm(x, axis=-1), ctx_4096)
    x = x + _L0_ffn_ref(_layernorm(x, axis=-1), L0_ffn_k0, L0_ffn_s0, L0_ffn_k1, L0_ffn_s1, L0_ffn_k2, L0_ffn_s2)
    return x

_drawn_inputs = setup_inputs


def setup_inputs(seed=0):
    import zlib

    import numpy as np

    out = dict(_drawn_inputs(seed))
    spreads = {}
    factors = {}
    for name, (base, spread) in spreads.items():
        noise = np.random.default_rng([zlib.crc32(name.encode()), seed]).standard_normal(out[name].shape)
        drawn = base * np.exp(spread * noise) if base else spread * noise
        out[name] = jnp.asarray(drawn.astype(out[name].dtype))
    for name, factor in factors.items():
        out[name] = (out[name] * factor).astype(out[name].dtype)
    return out
```

```python
from contextlib import ExitStack

import numpy as np

import concourse.bass as bass
from concourse import mybir

F32 = mybir.dt.float32
F32R = mybir.dt.float32r
BF16 = mybir.dt.bfloat16
U8 = mybir.dt.uint8
I32 = mybir.dt.int32
ACT = mybir.ActivationFunctionType
ALU = mybir.AluOpType
AX_X = mybir.AxisListType.X

P = 128
BATCHES, SEQ, D = 16, 128, 1024
TOKENS = BATCHES * SEQ
KT = D // P
HEADS, QL, KVL, DN, DR, DV = 32, 384, 128, 128, 64, 128
QT = QL // P
HALF = DR // 2
QUAD = P // HALF
QUADS = HEADS // QUAD
PAIR = 2
PAIRS = HEADS // PAIR
CH = 512
CHUNKS = TOKENS // CH
BPC = CH // SEQ
GROUPS = 2
CPG = CHUNKS // GROUPS
BPG = BATCHES // GROUPS
EPS = 1e-5
SCORE_SCALE = float(1.0 / np.sqrt(np.float32(DN + DR)))
MASKED = -1e30
HEAD_W = QL + KVL + KVL + D

CQ_HI, CQ_LO = 0, QT * CH
KT_HI, KT_LO = 2 * QT * CH, 2 * QT * CH + CH
KV_HI, KV_LO = KT_LO + CH, KT_LO + 2 * CH
KR_HI, KR_LO = KT_LO + 3 * CH, KT_LO + 4 * CH
PACK = KR_LO + CH


def as_f32(ap):
    return ap.bitcast(F32)


def three_passes(pe, out, w_hi, w_lo, x_hi, x_lo, first, last):
    pe.matmul(out, w_hi, x_hi, start=first, stop=False)
    pe.matmul(out, w_hi, x_lo, start=False, stop=False)
    return pe.matmul(out, w_lo, x_hi, start=False, stop=last)


def project(nc, x, w_down, consts, tok_d):
    WC = 5 * P
    ctx = ExitStack()
    with ctx:
        def sb(name, shape, dt=F32):
            return ctx.enter_context(nc.sbuf_tensor(name, shape, dt))

        def bank(name):
            return ctx.enter_context(nc.psum_tensor(name, [P, CH], F32))

        def sem(name):
            return ctx.enter_context(nc.semaphore(name))

        w_raw = sb("pj_w_raw", [P, KT, WC])
        w_hi = sb("pj_w_hi", [P, KT, WC], F32R)
        w_lo = sb("pj_w_lo", [P, KT, WC], F32R)
        ident = sb("pj_ident", [P, P])
        k_tab = sb("pj_k_tab", [P, SEQ])
        eps = sb("pj_eps", [P, 1])
        xin = sb("pj_x", [P, BPC, D])
        hn = sb("pj_hn", [P, BPC, D])
        stats = sb("pj_stats", [P, BPC, 2, 6])
        mv = sb("pj_mv", [P, BPC, 2])
        std = sb("pj_std", [P, BPC])
        rstd = sb("pj_rstd", [P, BPC])
        hT_hi = sb("pj_hT_hi", [P, KT, CH], F32R)
        hT_lo = sb("pj_hT_lo", [P, KT, CH], F32R)
        pack = sb("pj_pack", [P, PACK], F32R)
        kv_raw = sb("pj_kv_raw", [P, CH])
        k_cos = sb("pj_k_cos", [DR, CH])
        k_sin = sb("pj_k_sin", [DR, CH])
        k_rot = sb("pj_k_rot", [DR, CH])

        turned = [bank(f"pj_turned{i}") for i in range(2)]
        down = [bank(f"pj_down{m}") for m in range(5)]
        kv_turned = bank("pj_kv_turned")

        w_in, const_in, x_in = sem("pj_w_in"), sem("pj_const_in"), sem("pj_x_in")
        w_hi_done, w_lo_done = sem("pj_w_hi_done"), sem("pj_w_lo_done")
        rstd_done, sin_done = sem("pj_rstd_done"), sem("pj_sin_done")
        var_ready, std_ready, hn_ready = sem("pj_var_ready"), sem("pj_std_ready"), sem("pj_hn_ready")
        turn_ready, turn_hi, turn_lo = sem("pj_turn_ready"), sem("pj_turn_hi"), sem("pj_turn_lo")
        down_ready, cq_hi, cq_lo = sem("pj_down_ready"), sem("pj_cq_hi"), sem("pj_cq_lo")
        kt_hi, kt_lo, kv_raw_ready = sem("pj_kt_hi"), sem("pj_kt_lo"), sem("pj_kv_raw_ready")
        kv_turn_ready, kv_hi, kv_lo = sem("pj_kv_turn_ready"), sem("pj_kv_hi"), sem("pj_kv_lo")
        rot_ready, kr_hi, kr_lo = sem("pj_rot_ready"), sem("pj_kr_hi"), sem("pj_kr_lo")
        zeroed, stored = sem("pj_zeroed"), sem("pj_stored")

        x_chunks = x.rearrange("(c b p) d -> c p b d", c=CHUNKS, p=P)
        block = ctx.enter_context(nc.Block())

        @block.sync
        def _(sp):
            sp.dma_start(ident[:], consts["ident"]).then_inc(const_in, 16)
            sp.dma_start(k_tab[:], consts["k_tab"]).then_inc(const_in, 16)
            sp.dma_start(xin[:], x_chunks[0]).then_inc(x_in, 16)
            sp.dma_start(w_raw[:], w_down).then_inc(w_in, 16)

            def store(c):
                sp.wait_ge(kr_hi, c + 1)
                sp.wait_ge(kr_lo, c + 1)
                sp.wait_ge(zeroed, 1)
                sp.dma_start(tok_d[c], as_f32(pack[:])).then_inc(stored, 16)

            with sp.Fori(0, CHUNKS - 1) as c:
                sp.wait_ge(hn_ready, BPC * (c + 1))
                sp.dma_start(xin[:], x_chunks[c + 1]).then_inc(x_in, 16)
                store(c)
            store(CHUNKS - 1)
            sp.wait_ge(stored, 16 * CHUNKS)

        @block.gpsimd
        def _(pool):
            pool.memset(as_f32(pack[DR:P, KR_LO:KR_LO + CH]), 0.0).then_inc(zeroed, 1)

        @block.scalar
        def _(act):
            act.wait_ge(w_in, 16)
            act.activation(w_hi[:], w_raw[:], ACT.Copy).then_inc(w_hi_done, 1)

            def root():
                act.activation(std[:], mv[:, :, 1], ACT.Sqrt, bias=eps[:, 0:1]).then_inc(std_ready, 1)

            act.wait_ge(var_ready, 1)
            root()

            def chunk(c, last):
                for z in range(2 * BPC):
                    t, half = z // 2, z % 2
                    act.wait_ge(turn_ready, 2 * BPC * c + z + 1)
                    act.activation(hT_hi[:, half * 4:half * 4 + 4, t * P:(t + 1) * P],
                                   turned[z % 2][:].rearrange("p (k s) -> p k s", k=4),
                                   ACT.Copy).then_inc(turn_hi, 1)
                if not last:
                    act.wait_ge(var_ready, c + 2)
                    root()
                act.wait_ge(stored, 16 * c)
                for m in range(QT):
                    act.wait_ge(down_ready, 5 * c + m + 1)
                    act.activation(pack[:, CQ_HI + m * CH:CQ_HI + (m + 1) * CH], down[m][:],
                                   ACT.Copy).then_inc(cq_hi, 1)
                act.wait_ge(down_ready, 5 * c + 4)
                act.activation(kv_raw[:], down[3][:], ACT.Copy).then_inc(kv_raw_ready, 1)
                act.activation(pack[:, KT_HI:KT_HI + CH], down[3][:], ACT.Copy,
                               scale=SCORE_SCALE).then_inc(kt_hi, 1)
                act.wait_ge(kv_turn_ready, c + 1)
                act.activation(pack[:, KV_HI:KV_HI + CH], kv_turned[:], ACT.Copy).then_inc(kv_hi, 1)
                act.wait_ge(rot_ready, c + 1)
                act.activation(pack[0:DR, KR_HI:KR_HI + CH], k_rot[:], ACT.Copy)
                act.activation(pack[DR:P, KR_HI:KR_HI + CH], k_rot[:], ACT.Copy).then_inc(kr_hi, 1)

            with act.Fori(0, CHUNKS - 1) as c:
                chunk(c, False)
            chunk(CHUNKS - 1, True)

        @block.vector
        def _(dve):
            def normalise(c):
                dve.wait_ge(x_in, 16 * (c + 1))
                for t in range(BPC):
                    for h in range(2):
                        dve.bn_stats(stats[:, t, h, :], xin[:, t, h * 512:(h + 1) * 512])
                dve.drain()
                for t in range(BPC):
                    ins = dve.bn_aggr(mv[:, t, :], stats[:, t].rearrange("p h s -> p (h s)"))
                ins.then_inc(var_ready, 1)
                dve.wait_ge(std_ready, c + 1)
                dve.reciprocal(rstd[:], std[:]).then_inc(rstd_done, 1)
                dve.wait_ge(rstd_done, c + 1)
                for t in range(BPC):
                    dve.tensor_scalar(hn[:, t, :], xin[:, t, :], mv[:, t, 0:1], rstd[:, t:t + 1],
                                      ALU.subtract, ALU.mult).then_inc(hn_ready, 1)

            dve.memset(eps[:], EPS)
            normalise(0)
            dve.wait_ge(w_hi_done, 1)
            dve.tensor_tensor(w_lo[:], w_raw[:], as_f32(w_hi[:]), ALU.subtract).then_inc(w_lo_done, 1)

            def chunk(c, last):
                for z in range(2 * BPC):
                    t, half = z // 2, z % 2
                    dve.wait_ge(turn_hi, 2 * BPC * c + z + 1)
                    at = (slice(None), slice(half * 4, half * 4 + 4), slice(t * P, (t + 1) * P))
                    dve.tensor_tensor(hT_lo[at], turned[z % 2][:].rearrange("p (k s) -> p k s", k=4),
                                      as_f32(hT_hi[at]), ALU.subtract).then_inc(turn_lo, 1)
                if not last:
                    normalise(c + 1)
                for m in range(QT):
                    dve.wait_ge(cq_hi, QT * c + m + 1)
                    dve.tensor_tensor(pack[:, CQ_LO + m * CH:CQ_LO + (m + 1) * CH], down[m][:],
                                      as_f32(pack[:, CQ_HI + m * CH:CQ_HI + (m + 1) * CH]),
                                      ALU.subtract).then_inc(cq_lo, 1)
                dve.wait_ge(kt_hi, c + 1)
                dve.scalar_tensor_tensor(out=pack[:, KT_LO:KT_LO + CH], in0=down[3][:], scalar=SCORE_SCALE,
                                         in1=as_f32(pack[:, KT_HI:KT_HI + CH]), op0=ALU.mult,
                                         op1=ALU.subtract).then_inc(kt_lo, 1)
                dve.wait_ge(kv_turn_ready, c + 1)
                dve.wait_ge(kv_hi, c + 1)
                dve.tensor_tensor(pack[:, KV_LO:KV_LO + CH], kv_turned[:],
                                  as_f32(pack[:, KV_HI:KV_HI + CH]), ALU.subtract).then_inc(kv_lo, 1)
                dve.wait_ge(down_ready, 5 * c + 5)

                def times_table(out, rows):
                    return dve.tensor_tensor(
                        out.rearrange("p (b s) -> p b s", b=BPC),
                        down[4][rows, :].rearrange("p (b s) -> p b s", b=BPC),
                        k_tab[rows, :].unsqueeze(1).to_broadcast([DR, BPC, SEQ]), ALU.mult)

                dve.wait_ge(const_in, 32)
                times_table(k_cos[:], slice(0, DR))
                times_table(k_sin[:], slice(DR, P)).then_inc(sin_done, 1)
                dve.wait_ge(sin_done, c + 1)
                dve.tensor_tensor(k_rot[:], k_cos[:], k_sin[:], ALU.add).then_inc(rot_ready, 1)
                dve.wait_ge(rot_ready, c + 1)
                dve.wait_ge(kr_hi, c + 1)
                dve.tensor_tensor(pack[0:DR, KR_LO:KR_LO + CH], k_rot[:],
                                  as_f32(pack[0:DR, KR_HI:KR_HI + CH]), ALU.subtract).then_inc(kr_lo, 1)

            with dve.Fori(0, CHUNKS - 1) as c:
                chunk(c, False)
            chunk(CHUNKS - 1, True)

        @block.tensor
        def _(pe):
            pe.wait_ge(const_in, 32)

            def chunk(c):
                for z in range(2 * BPC):
                    t, half = z // 2, z % 2
                    pe.wait_ge(hn_ready, BPC * c + t + 1)
                    if z >= 2:
                        pe.wait_ge(turn_lo, 2 * BPC * c + z - 1)
                    else:
                        pe.wait_ge(turn_lo, 2 * BPC * c)
                    for j in range(4):
                        k = half * 4 + j
                        ins = pe.transpose(turned[z % 2][:, j * P:(j + 1) * P],
                                           hn[:, t, k * P:(k + 1) * P], ident[:])
                    ins.then_inc(turn_ready, 1)
                pe.wait_ge(turn_lo, 2 * BPC * (c + 1))
                pe.wait_ge(w_lo_done, 1)
                for m in range(5):
                    if m < QT:
                        pe.wait_ge(cq_lo, QT * c)
                    elif m == 3:
                        pe.wait_ge(kt_lo, c)
                    else:
                        pe.wait_ge(rot_ready, c)
                    cols = slice(m * P, (m + 1) * P)
                    for k in range(KT):
                        ins = three_passes(pe, down[m][:], w_hi[:, k, cols], w_lo[:, k, cols],
                                           hT_hi[:, k, :], hT_lo[:, k, :], k == 0, k == KT - 1)
                    ins.then_inc(down_ready, 1)
                pe.wait_ge(kv_raw_ready, c + 1)
                pe.wait_ge(kv_lo, c)
                for b in range(BPC):
                    ins = pe.transpose(kv_turned[:, b * P:(b + 1) * P], kv_raw[:, b * P:(b + 1) * P], ident[:])
                ins.then_inc(kv_turn_ready, 1)

            with pe.Fori(0, CHUNKS) as c:
                chunk(c)


def absorb(nc, w_heads, w_rope, wabs_d, wvo_d, wqr_d):
    ctx = ExitStack()
    with ctx:
        def sb(name, shape, dt=F32):
            return ctx.enter_context(nc.sbuf_tensor(name, shape, dt))

        def sem(name):
            return ctx.enter_context(nc.semaphore(name))

        UK, UV, OUT = QL, QL + KVL, QL + 2 * KVL
        raw = [sb(f"ab_raw{i}", [P, PAIR, HEAD_W]) for i in range(2)]
        hi = [sb(f"ab_hi{i}", [P, PAIR, HEAD_W], F32R) for i in range(2)]
        lo = [sb(f"ab_lo{i}", [P, PAIR, HEAD_W], F32R) for i in range(2)]
        wabs = [sb(f"ab_wabs{i}", [P, 2, QT, PAIR * P], F32R) for i in range(2)]
        wvo = [sb(f"ab_wvo{i}", [P, 2, PAIR, D], F32R) for i in range(2)]
        rope_raw = sb("ab_rope_raw", [P, QT, 2, P])
        rope = sb("ab_rope", [P, 2, QT, 2, P], F32R)
        abs_bank = [ctx.enter_context(nc.psum_tensor(f"ab_abs{i}", [P, QT, P], F32)) for i in range(2)]
        vo_bank = [ctx.enter_context(nc.psum_tensor(f"ab_vo{i}", [P, CH], F32)) for i in range(4)]

        raw_in = [sem(f"ab_raw_in{i}") for i in range(2)]
        rope_in, rope_hi, rope_lo, rope_out = (sem(f"ab_rope_{n}") for n in ("in", "hi", "lo", "out"))
        split_hi, split_lo = sem("ab_split_hi"), sem("ab_split_lo")
        abs_ready, abs_hi, abs_lo = sem("ab_abs_ready"), sem("ab_abs_hi"), sem("ab_abs_lo")
        vo_ready, vo_hi, vo_lo = sem("ab_vo_ready"), sem("ab_vo_hi"), sem("ab_vo_lo")
        out_done = [sem(f"ab_out_done{i}") for i in range(2)]
        PPQ = 2
        block = ctx.enter_context(nc.Block())

        @block.sync
        def _(sp):
            with sp.Fori(0, QUADS) as q:
                sp.wait_ge(rope_lo, q)
                sp.dma_start(rope_raw[:], w_rope[q]).then_inc(rope_in, 16)
                for i in range(PPQ):
                    sp.wait_ge(split_lo, PPQ * q)
                    sp.dma_start(raw[i][:], w_heads[PPQ * q + i]).then_inc(raw_in[i], 16)

        @block.gpsimd
        def _(pool):
            with pool.Fori(0, QUADS) as q:
                pool.wait_ge(rope_lo, q + 1)
                pool.dma_start(wqr_d[q], as_f32(rope[:])).then_inc(rope_out, 16)
                for i in range(PPQ):
                    pool.wait_ge(abs_lo, PAIR * (PPQ * q + i + 1))
                    pool.dma_start(wabs_d[PPQ * q + i], as_f32(wabs[i][:])).then_inc(out_done[i], 16)
                    pool.wait_ge(vo_lo, 2 * PAIR * (PPQ * q + i + 1))
                    pool.dma_start(wvo_d[PPQ * q + i], as_f32(wvo[i][:])).then_inc(out_done[i], 16)
            pool.wait_ge(rope_out, 16 * QUADS)
            for i in range(PPQ):
                pool.wait_ge(out_done[i], 32 * QUADS)

        @block.scalar
        def _(act):
            with act.Fori(0, QUADS) as q:
                act.wait_ge(rope_in, 16 * (q + 1))
                act.wait_ge(rope_out, 16 * q)
                act.activation(rope[:, 0], rope_raw[:], ACT.Copy).then_inc(rope_hi, 1)
                for i in range(PPQ):
                    act.wait_ge(raw_in[i], 16 * (q + 1))
                    act.wait_ge(vo_ready, 2 * PAIR * PPQ * q)
                    act.activation(hi[i][:], raw[i][:], ACT.Copy).then_inc(split_hi, 1)
                for i in range(PPQ):
                    act.wait_ge(out_done[i], 32 * q)
                    for h in range(PAIR):
                        n = PAIR * i + h
                        act.wait_ge(abs_ready, PAIR * PPQ * q + n + 1)
                        act.activation(wabs[i][:, 0, :, h * P:(h + 1) * P], abs_bank[h][:],
                                       ACT.Copy).then_inc(abs_hi, 1)
                        for c in range(2):
                            act.wait_ge(vo_ready, 2 * (PAIR * PPQ * q + n) + c + 1)
                            act.activation(wvo[i][:, 0, h, c * CH:(c + 1) * CH], vo_bank[2 * h + c][:],
                                           ACT.Copy).then_inc(vo_hi, 1)

        @block.vector
        def _(dve):
            with dve.Fori(0, QUADS) as q:
                dve.wait_ge(rope_hi, q + 1)
                dve.tensor_tensor(rope[:, 1], rope_raw[:], as_f32(rope[:, 0]), ALU.subtract).then_inc(rope_lo, 1)
                for i in range(PPQ):
                    dve.wait_ge(split_hi, PPQ * q + i + 1)
                    dve.tensor_tensor(lo[i][:], raw[i][:], as_f32(hi[i][:]), ALU.subtract).then_inc(split_lo, 1)
                for i in range(PPQ):
                    for h in range(PAIR):
                        n = PAIR * i + h
                        cols = slice(h * P, (h + 1) * P)
                        dve.wait_ge(abs_hi, PAIR * PPQ * q + n + 1)
                        dve.tensor_tensor(wabs[i][:, 1, :, cols], abs_bank[h][:],
                                          as_f32(wabs[i][:, 0, :, cols]), ALU.subtract).then_inc(abs_lo, 1)
                        for c in range(2):
                            cols = slice(c * CH, (c + 1) * CH)
                            dve.wait_ge(vo_hi, 2 * (PAIR * PPQ * q + n) + c + 1)
                            dve.tensor_tensor(wvo[i][:, 1, h, cols], vo_bank[2 * h + c][:],
                                              as_f32(wvo[i][:, 0, h, cols]), ALU.subtract).then_inc(vo_lo, 1)

        @block.tensor
        def _(pe):
            with pe.Fori(0, QUADS) as q:
                for i in range(PPQ):
                    pe.wait_ge(split_lo, PPQ * q + i + 1)
                    for h in range(PAIR):
                        n = PAIR * i + h
                        if i == 0:
                            pe.wait_ge(abs_lo, PAIR * PPQ * q)
                            pe.wait_ge(vo_lo, 2 * PAIR * PPQ * q)
                        else:
                            pe.wait_ge(abs_lo, PAIR * PPQ * q + n - 1)
                            pe.wait_ge(vo_lo, 2 * (PAIR * PPQ * q + n - 1))
                        for k in range(QT):
                            ins = three_passes(pe, abs_bank[h][:, k, :],
                                               hi[i][:, h, k * P:(k + 1) * P], lo[i][:, h, k * P:(k + 1) * P],
                                               hi[i][:, h, UK:UV], lo[i][:, h, UK:UV], True, True)
                        ins.then_inc(abs_ready, 1)
                        for c in range(2):
                            cols = slice(OUT + c * CH, OUT + (c + 1) * CH)
                            ins = three_passes(pe, vo_bank[2 * h + c][:], hi[i][:, h, UV:OUT], lo[i][:, h, UV:OUT],
                                               hi[i][:, h, cols], lo[i][:, h, cols], True, True)
                            ins.then_inc(vo_ready, 1)


def attend(nc, x, tok_d, wabs_d, wvo_d, wqr_d, consts, x1_d):
    STEPS, UNITS, ROPES = 8, 4, CPG
    PARTS = 2 * PAIR
    USE = [0, 1, 2, 3, 4, 7, 8, 11]
    ctx = ExitStack()
    with ctx:
        def sb(name, shape, dt=F32):
            return ctx.enter_context(nc.sbuf_tensor(name, shape, dt))

        def bank(name):
            return ctx.enter_context(nc.psum_tensor(name, [P, CH], F32))

        def sem(name):
            return ctx.enter_context(nc.semaphore(name))

        tok = sb("at_tok", [P, CPG, PACK], F32R)
        acc = sb("at_acc", [P, BPG, D])
        wabs = [sb(f"at_wabs{i}", [P, 2, QT, PAIR * P], F32R) for i in range(2)]
        wvo = [sb(f"at_wvo{i}", [P, 2, PAIR, D], F32R) for i in range(2)]
        wqr = sb("at_wqr", [P, 2, QT, 2, P], F32R)
        qlat = [sb(f"at_qlat{i}", [P, 2, PAIR, CH], F32R) for i in range(2)]
        qrope = [sb(f"at_qrope{c}", [P, QUAD, CH], F32R) for c in range(CPG)]
        rope_tmp = sb("at_rope_tmp", [P, 4, CH])
        rope_parts = sb("at_rope_parts", [P, 4, CH], F32R)
        probs = [sb(f"at_probs{i}", [P, PARTS, SEQ]) for i in range(2)]
        nmax = [sb(f"at_nmax{i}", [P, PARTS]) for i in range(2)]
        sums = [sb(f"at_sums{i}", [P, PARTS]) for i in range(2)]
        rsum = [sb(f"at_rsum{i}", [P, PARTS]) for i in range(2)]
        pT_hi = sb("at_pT_hi", [P, CH], F32R)
        pT_lo = sb("at_pT_lo", [P, CH], F32R)
        val_hi = [sb(f"at_val_hi{i}", [P, CH], F32R) for i in range(2)]
        val_lo = [sb(f"at_val_lo{i}", [P, CH], F32R) for i in range(2)]
        ident = sb("at_ident", [P, P])
        ident_b = sb("at_ident_b", [P, P], BF16)
        mask = sb("at_mask", [P, SEQ])
        mask_b = sb("at_mask_b", [P, SEQ], BF16)
        cos = sb("at_cos", [P, SEQ])
        sin = sb("at_sin", [P, SEQ])

        qbank = [bank(f"at_qbank{i}") for i in range(2)]
        score = [bank(f"at_score{i}") for i in range(2)]
        turned, value = bank("at_turned"), bank("at_value")
        outb = [bank(f"at_out{i}") for i in range(2)]

        const_in, tok_in, acc_in, x1_out = (sem(f"at_{n}") for n in ("const_in", "tok_in", "acc_in", "x1_out"))
        wabs_in = [sem(f"at_wabs_in{i}") for i in range(2)]
        wvo_in = [sem(f"at_wvo_in{i}") for i in range(2)]
        wqr_in = sem("at_wqr_in")
        qrope_in = [sem(f"at_qrope_in{c}") for c in range(CPG)]
        const_cast = sem("at_const_cast")
        ql_mm, ql_hi, ql_lo = sem("at_ql_mm"), sem("at_ql_hi"), sem("at_ql_lo")
        rope_mm, rope_cs, rope_sum = sem("at_rope_mm"), sem("at_rope_cs"), sem("at_rope_sum")
        rope_hi, rope_lo = sem("at_rope_hi"), sem("at_rope_lo")
        score_ready, max_ready, exp_ready = sem("at_score_ready"), sem("at_max_ready"), sem("at_exp_ready")
        rsum_ready, probs_ready = sem("at_rsum_ready"), sem("at_probs_ready")
        turn_ready, pT_hi_done, pT_lo_done = sem("at_turn_ready"), sem("at_pT_hi_done"), sem("at_pT_lo_done")
        value_ready, val_hi_done, val_lo_done = (sem(f"at_{n}") for n in ("value_ready", "val_hi_done", "val_lo_done"))
        out_ready = sem("at_out_ready")
        added = sem("at_added")

        def batch_cols(s, bl):
            b = 2 * (s % 2) + bl
            return slice(b * SEQ, (b + 1) * SEQ)

        def place(s):
            return (s // 2) // CPG % 2, (s // 2) % CPG

        def slots(one_slot, m, ahead):
            for s in range(STEPS):
                one_slot(m, s, STEPS * (1 + ahead))

        x_groups = x.rearrange("(g b p) d -> g p b d", g=GROUPS, p=P)
        x1_groups = x1_d.rearrange("(g b p) d -> g p b d", g=GROUPS, p=P)
        tok_groups = tok_d.rearrange("(g c) p n -> g p c n", g=GROUPS)
        block = ctx.enter_context(nc.Block())

        def groups(eng, opening, quad, closing=None):
            with eng.Fori(0, GROUPS) as g:
                opening(g)
                with eng.Fori(0, QUADS - 1) as q:
                    quad(g * QUADS + q, q, 1)
                quad(g * QUADS + (QUADS - 1), QUADS - 1, 0)
                if closing:
                    closing(g)

        @block.sync
        def _(sp):
            for to, name in ((ident, "ident"), (mask, "mask"), (cos, "cos"), (sin, "sin")):
                sp.dma_start(to[:], consts[name]).then_inc(const_in, 16)

            def load_wabs(i, q):
                sp.dma_start(as_f32(wabs[i][:]), wabs_d[2 * q + i]).then_inc(wabs_in[i], 16)

            def load_wvo(i, q):
                sp.dma_start(as_f32(wvo[i][:]), wvo_d[2 * q + i]).then_inc(wvo_in[i], 16)

            def load_wqr(q):
                sp.dma_start(as_f32(wqr[:]), wqr_d[q]).then_inc(wqr_in, 16)

            def relayout(m, c):
                sp.wait_ge(rope_lo, 2 * (ROPES * m + c + 1))
                for h in range(QUAD):
                    for j in range(4):
                        sp.dma_start(as_f32(qrope[c][j * HALF:(j + 1) * HALF, h, :]),
                                     as_f32(rope_parts[h * HALF:(h + 1) * HALF, j, :])).then_inc(qrope_in[c], 16)

            def opening(g):
                sp.wait_ge(out_ready, 4 * STEPS * QUADS * g)
                load_wqr(0)
                sp.dma_start(as_f32(tok[:]), tok_groups[g]).then_inc(tok_in, 16)
                load_wabs(0, 0)
                sp.wait_ge(x1_out, 16 * g)
                sp.dma_start(acc[:], x_groups[g]).then_inc(acc_in, 16)
                load_wvo(0, 0)
                load_wabs(1, 0)
                load_wvo(1, 0)
                for c in range(ROPES):
                    relayout(g * QUADS, c)

            def quad(m, q, ahead):
                if not ahead:
                    return
                sp.wait_ge(ql_mm, PAIR * (UNITS * m + 2))
                load_wabs(0, q + 1)
                sp.wait_ge(rope_mm, ROPES * (m + 1))
                load_wqr(q + 1)
                sp.wait_ge(ql_mm, PAIR * (UNITS * m + 4))
                load_wabs(1, q + 1)
                sp.wait_ge(out_ready, 4 * (STEPS * m + 4))
                load_wvo(0, q + 1)
                for c in range(ROPES):
                    relayout(m + 1, c)
                sp.wait_ge(out_ready, 4 * STEPS * (m + 1))
                load_wvo(1, q + 1)

            def closing(g):
                sp.wait_ge(added, 4 * STEPS * QUADS * (g + 1) + 2)
                sp.dma_start(x1_groups[g], acc[:]).then_inc(x1_out, 16)

            groups(sp, opening, quad, closing)
            sp.wait_ge(x1_out, 16 * GROUPS)

        @block.tensor
        def _(pe):
            pe.wait_ge(const_cast, 2)

            def latent(m, u, h, n, ropes, after_rope):
                pair, c = place(2 * u)
                before = PAIR * (m * UNITS + u) + h
                if h == 0:
                    pe.wait_ge(wabs_in[pair], 16 * (m + u // UNITS + 1))
                pe.wait_ge(rope_cs, ropes)
                pe.wait_ge(ql_lo, before if after_rope else before - 1)
                cols = slice(h * P, (h + 1) * P)
                for k in range(QT):
                    ins = three_passes(pe, qbank[n % 2][:], wabs[pair][:, 0, k, cols], wabs[pair][:, 1, k, cols],
                                       tok[:, c, CQ_HI + k * CH:CQ_HI + (k + 1) * CH],
                                       tok[:, c, CQ_LO + k * CH:CQ_LO + (k + 1) * CH], k == 0, k == QT - 1)
                ins.then_inc(ql_mm, 1)

            def rope(m, c, n, latents):
                pe.wait_ge(wqr_in, 16 * (m + 1))
                pe.wait_ge(rope_cs, ROPES * m + c)
                pe.wait_ge(ql_lo, latents)
                for half in range(2):
                    for k in range(QT):
                        ins = three_passes(pe, qbank[(n + half) % 2][:], wqr[:, 0, k, half], wqr[:, 1, k, half],
                                           tok[:, c, CQ_HI + k * CH:CQ_HI + (k + 1) * CH],
                                           tok[:, c, CQ_LO + k * CH:CQ_LO + (k + 1) * CH], k == 0, k == QT - 1)
                ins.then_inc(rope_mm, 1)

            def scores(m, s):
                pair, c = place(s)
                u = s // 2
                pe.wait_ge(ql_lo, PAIR * (UNITS * m + u + 1))
                if pair == 0 and s % 2 == 0:
                    pe.wait_ge(qrope_in[c], 16 * 16 * (m + s // STEPS + 1))
                sc = score[s % 2]
                pe.matmul(sc[:], ident_b[:], mask_b[:].unsqueeze(1).to_broadcast([P, PARTS, SEQ]),
                          start=True, stop=False)
                for bl in range(2):
                    cols = batch_cols(s, bl)

                    def key(part):
                        return tok[:, c, part + cols.start:part + cols.stop]

                    for h in range(PAIR):
                        j = bl * PAIR + h
                        out = sc[:, j * SEQ:(j + 1) * SEQ]
                        last = j == PARTS - 1
                        q_hi, q_lo = (qlat[u % 2][:, i, h, cols] for i in range(2))
                        q_rope = qrope[c][:, pair * PAIR + h, cols]
                        pe.matmul(out, q_hi, key(KT_HI), start=False, stop=False)
                        pe.matmul(out, q_hi, key(KT_LO), start=False, stop=False)
                        pe.matmul(out, q_lo, key(KT_HI), start=False, stop=False)
                        pe.matmul(out, q_rope, key(KR_HI), start=False, stop=False)
                        ins = pe.matmul(out, q_rope, key(KR_LO), start=False, stop=last)
                ins.then_inc(score_ready, 1)

            def turn(m, s):
                pe.wait_ge(probs_ready, STEPS * m + s + 1)
                for j in range(PARTS):
                    ins = pe.transpose(turned[:, j * SEQ:(j + 1) * SEQ], probs[s % 2][:, j, :], ident[:])
                ins.then_inc(turn_ready, 1)

            def values(m, s):
                _, c = place(s)
                pe.wait_ge(pT_lo_done, STEPS * m + s + 1)
                for bl in range(2):
                    cols = batch_cols(s, bl)
                    at = slice(bl * PAIR * SEQ, (bl + 1) * PAIR * SEQ)
                    ins = three_passes(pe, value[:, at], tok[:, c, KV_HI + cols.start:KV_HI + cols.stop],
                                       tok[:, c, KV_LO + cols.start:KV_LO + cols.stop],
                                       pT_hi[:, at], pT_lo[:, at], True, True)
                ins.then_inc(value_ready, 1)

            def output(m, s, bl):
                pair, _ = place(s)
                if bl == 0:
                    pe.wait_ge(val_lo_done, STEPS * m + s + 1)
                    pe.wait_ge(wvo_in[pair], 16 * (m + 1))
                for n in range(2):
                    pe.wait_ge(added, 4 * (STEPS * m + s) + 2 * bl + n + 1)
                    for h in range(PAIR):
                        at = slice((bl * PAIR + h) * SEQ, (bl * PAIR + h + 1) * SEQ)
                        cols = slice(n * CH, (n + 1) * CH)
                        ins = three_passes(pe, outb[n][:], val_hi[s % 2][:, at], val_lo[s % 2][:, at],
                                           wvo[pair][:, 0, h, cols], wvo[pair][:, 1, h, cols],
                                           h == 0, h == PAIR - 1)
                    ins.then_inc(out_ready, 1)

            def opening(g):
                m = g * QUADS
                pe.wait_ge(tok_in, 16 * (g + 1))
                rope(m, 0, 0, PAIR * UNITS * m)
                for u in range(2):
                    for h in range(PAIR):
                        latent(m, u, h, PAIR * u + h, ROPES * m + 1, u + h == 0)
                rope(m, 1, 0, PAIR * (UNITS * m + 2))
                scores(m, 0)
                scores(m, 1)
                turn(m, 0)
                values(m, 0)

            def slot(m, s, end):
                if s + 1 < end:
                    turn(m, s + 1)
                if s + 2 < end:
                    scores(m, s + 2)
                output(m, s, 0)
                if s + 1 < end:
                    values(m, s + 1)
                output(m, s, 1)
                if s // 2 + 2 < end // 2:
                    ropes = ROPES * (m + 1) + (s > 4) + (s > 6)
                    latent(m, s // 2 + 2, s % 2, USE[s], ropes, s in (0, 5, 7))
                    if s in (4, 6):
                        rope(m + 1, (s - 4) // 2, USE[s] + 1, PAIR * (UNITS * m + 2) + s + 1)

            groups(pe, opening, lambda m, q, ahead: slots(slot, m, ahead))

        @block.scalar
        def _(act):
            act.wait_ge(const_in, 64)
            act.activation(ident_b[:], ident[:], ACT.Copy).then_inc(const_cast, 1)
            act.activation(mask_b[:], mask[:], ACT.Copy).then_inc(const_cast, 1)

            def latent(m, u, h, n):
                act.wait_ge(ql_mm, PAIR * (UNITS * m + u) + h + 1)
                act.activation(qlat[u % 2][:, 0, h, :], qbank[n % 2][:], ACT.Copy).then_inc(ql_hi, 1)

            def rope(m, c):
                at = ROPES * m + c
                if c == 0:
                    act.wait_ge(qrope_in[1], 256 * m)
                else:
                    act.wait_ge(qrope_in[0], 256 * (m + 1))
                for half in range(2):
                    act.wait_ge(rope_sum, 2 * at + half + 1)
                    act.activation(rope_parts[:, half, :], rope_tmp[:, 2 * half, :], ACT.Copy).then_inc(rope_hi, 1)

            def exps(m, s):
                i = s % 2
                act.wait_ge(max_ready, STEPS * m + s + 1)
                for j in range(PARTS):
                    ins = act.activation(probs[i][:, j, :], score[i][:, j * SEQ:(j + 1) * SEQ], ACT.Exp,
                                         bias=nmax[i][:, j:j + 1], accum_out=sums[i][:, j:j + 1])
                ins.then_inc(exp_ready, 1)

            def turn(m, s):
                act.wait_ge(turn_ready, STEPS * m + s + 1)
                act.activation(pT_hi[:], turned[:], ACT.Copy).then_inc(pT_hi_done, 1)

            def values(m, s):
                act.wait_ge(value_ready, STEPS * m + s + 1)
                act.activation(val_hi[s % 2][:], value[:], ACT.Copy).then_inc(val_hi_done, 1)

            def opening(g):
                m = g * QUADS
                rope(m, 0)
                for u in range(2):
                    for h in range(PAIR):
                        latent(m, u, h, PAIR * u + h)
                rope(m, 1)
                exps(m, 0)
                exps(m, 1)
                turn(m, 0)
                values(m, 0)

            def slot(m, s, end):
                if s + 1 < end:
                    turn(m, s + 1)
                if s + 2 < end:
                    exps(m, s + 2)
                if s + 1 < end:
                    values(m, s + 1)
                if s // 2 + 2 < end // 2:
                    latent(m, s // 2 + 2, s % 2, USE[s])
                    if s in (4, 6):
                        rope(m + 1, (s - 4) // 2)

            groups(act, opening, lambda m, q, ahead: slots(slot, m, ahead))

        @block.gpsimd
        def _(pool):
            def normalise(m, s):
                i = s % 2
                pool.wait_ge(rsum_ready, STEPS * m + s + 1)
                pool.tensor_tensor(probs[i][:], probs[i][:], rsum[i][:].unsqueeze(2).to_broadcast([P, PARTS, SEQ]),
                                   ALU.mult).then_inc(probs_ready, 1)

            def rope(m, c):
                at = ROPES * m + c
                pool.wait_ge(rope_cs, at + 1)
                for half, op in ((0, ALU.subtract), (1, ALU.add)):
                    pool.tensor_tensor(rope_tmp[:, 2 * half, :], rope_tmp[:, 2 * half, :],
                                       rope_tmp[:, 2 * half + 1, :], op).then_inc(rope_sum, 1)
                for half in range(2):
                    pool.wait_ge(rope_hi, 2 * at + half + 1)
                    pool.tensor_tensor(rope_parts[:, 2 + half, :], rope_tmp[:, 2 * half, :],
                                       as_f32(rope_parts[:, half, :]), ALU.subtract).then_inc(rope_lo, 1)

            def opening(g):
                m = g * QUADS
                rope(m, 0)
                rope(m, 1)
                normalise(m, 0)
                normalise(m, 1)

            def slot(m, s, end):
                if s + 2 < end:
                    normalise(m, s + 2)
                if s in (4, 6) and s + 2 < end and end > STEPS:
                    rope(m + 1, (s - 4) // 2)

            groups(pool, opening, lambda m, q, ahead: slots(slot, m, ahead))

        @block.vector
        def _(dve):
            dve.sem_inc(added, 2)
            dve.wait_ge(const_in, 64)

            def latent(m, u, h, n):
                dve.wait_ge(ql_hi, PAIR * (UNITS * m + u) + h + 1)
                dve.tensor_tensor(qlat[u % 2][:, 1, h, :], qbank[n % 2][:], as_f32(qlat[u % 2][:, 0, h, :]),
                                  ALU.subtract).then_inc(ql_lo, 1)

            def rope(m, c, n):
                at = ROPES * m + c
                dve.wait_ge(rope_mm, at + 1)
                dve.wait_ge(rope_lo, 2 * at)

                def times(out, half, table):
                    return dve.tensor_tensor(rope_tmp[:, out, :].rearrange("p (b s) -> p b s", b=BPC),
                                             qbank[(n + half) % 2][:].rearrange("p (b s) -> p b s", b=BPC),
                                             table[:].unsqueeze(1).to_broadcast([P, BPC, SEQ]), ALU.mult)

                times(0, 0, cos)
                times(1, 1, sin)
                times(2, 0, sin)
                times(3, 1, cos).then_inc(rope_cs, 1)

            def largest(m, s):
                i = s % 2
                dve.wait_ge(score_ready, STEPS * m + s + 1)
                dve.tensor_reduce(nmax[i][:], score[i][:].rearrange("p (j t) -> p j t", j=PARTS), AX_X, ALU.max,
                                  negate=True).then_inc(max_ready, 1)

            def recip(m, s):
                i = s % 2
                dve.wait_ge(exp_ready, STEPS * m + s + 1)
                dve.reciprocal(rsum[i][:], sums[i][:]).then_inc(rsum_ready, 1)

            def turn(m, s):
                dve.wait_ge(pT_hi_done, STEPS * m + s + 1)
                dve.tensor_tensor(pT_lo[:], turned[:], as_f32(pT_hi[:]), ALU.subtract).then_inc(pT_lo_done, 1)

            def values(m, s):
                dve.wait_ge(val_hi_done, STEPS * m + s + 1)
                dve.tensor_tensor(val_lo[s % 2][:], value[:], as_f32(val_hi[s % 2][:]),
                                  ALU.subtract).then_inc(val_lo_done, 1)

            def add(m, s, bl, n):
                _, c = place(s)
                at = acc[:, BPC * c + 2 * (s % 2) + bl, n * CH:(n + 1) * CH]
                dve.wait_ge(out_ready, 4 * (STEPS * m + s) + 2 * bl + n + 1)
                dve.tensor_tensor(at, outb[n][:], at, ALU.add).then_inc(added, 1)

            def opening(g):
                m = g * QUADS
                rope(m, 0, 0)
                for u in range(2):
                    for h in range(PAIR):
                        latent(m, u, h, PAIR * u + h)
                rope(m, 1, 0)
                largest(m, 0)
                largest(m, 1)
                recip(m, 0)
                recip(m, 1)
                turn(m, 0)
                dve.wait_ge(acc_in, 16 * (g + 1))
                values(m, 0)

            def slot(m, s, end):
                if s + 1 < end:
                    turn(m, s + 1)
                if s + 2 < end:
                    largest(m, s + 2)
                add(m, s, 0, 0)
                if s + 2 < end:
                    recip(m, s + 2)
                add(m, s, 0, 1)
                if s + 1 < end:
                    values(m, s + 1)
                add(m, s, 1, 0)
                add(m, s, 1, 1)
                if s // 2 + 2 < end // 2:
                    latent(m, s // 2 + 2, s % 2, USE[s])
                    if s in (4, 6):
                        rope(m + 1, (s - 4) // 2, USE[s] + 1)

            groups(dve, opening, lambda m, q, ahead: slots(slot, m, ahead))


def cross(nc, x1_d, context, consts, x2_d):
    SETS = 4
    ctx = ExitStack()
    with ctx:
        def sb(name, shape, dt=F32):
            return ctx.enter_context(nc.sbuf_tensor(name, shape, dt))

        def many(n, name, shape, dt=F32):
            return [sb(f"{name}{i}", shape, dt) for i in range(n)]

        def banks(name, n=2):
            return [ctx.enter_context(nc.psum_tensor(f"{name}{i}", [P, CH], F32)) for i in range(n)]

        def sem(name):
            return ctx.enter_context(nc.semaphore(name))

        CUT = ((D, 2 * D), (0, D))
        xt = many(SETS, "cr_x", [P, D])
        ctx_raw = many(2, "cr_ctx_raw", [P, 2 * D])
        ctx_hi = many(SETS, "cr_ctx_hi", [P, 2 * D], F32R)
        ctx_lo = many(SETS, "cr_ctx_lo", [P, 2 * D], F32R)
        hn = many(2, "cr_hn", [P, D])
        qT_hi = many(2, "cr_qT_hi", [P, KT, P], F32R)
        qT_lo = many(2, "cr_qT_lo", [P, KT, P], F32R)
        probs = many(2, "cr_probs", [P, SEQ])
        pT_hi = many(2, "cr_pT_hi", [P, SEQ], F32R)
        pT_lo = many(2, "cr_pT_lo", [P, SEQ], F32R)
        stats = many(2, "cr_stats", [P, 2, 6])
        mv = many(2, "cr_mv", [P, 2])
        var = many(2, "cr_var", [P, 1])
        rstd = many(2, "cr_rstd", [P, 1])
        nmax = many(2, "cr_nmax", [P, 1])
        total = many(2, "cr_total", [P, 1])
        rtotal = many(2, "cr_rtotal", [P, 1])
        power = sb("cr_power", [P, 1])
        ident = sb("cr_ident", [P, P])
        turned, score, out = banks("cr_turned"), banks("cr_score"), banks("cr_out")
        pT = banks("cr_pT", 1)[0]

        const_in, power_set = sem("cr_const_in"), sem("cr_power_set")
        x_in = [sem(f"cr_x_in{i}") for i in range(SETS)]
        c_in = [sem(f"cr_c_in{i}") for i in range(2)]
        x2_out = [sem(f"cr_x2_out{i}") for i in range(SETS)]
        names = ("mv_done", "var_done", "rstd_done", "hn_ready", "turn_ready", "turn_hi", "turn_lo",
                 "ctx_hi_done", "ctx_lo_done", "score_ready", "max_ready", "exp_ready", "rtotal_ready", "pT_ready",
                 "pT_hi_done", "pT_lo_done", "out_ready")
        s = {n: sem(f"cr_{n}") for n in names}
        summed = sem("cr_summed")
        x1_b = x1_d.rearrange("(b p) d -> b p d", p=P)
        x2_b = x2_d.rearrange("(b p) d -> b p d", p=P)
        block = ctx.enter_context(nc.Block())

        def batches(eng, opening, turn):
            opening()
            with eng.Fori(0, BATCHES // SETS - 1) as n:
                for i in range(SETS):
                    turn(SETS * n + i, i, n, SETS)
            for i in range(SETS):
                turn(BATCHES - SETS + i, i, BATCHES // SETS - 1, SETS - 1 - i)

        @block.sync
        def _(sp):
            sp.sem_inc(x2_out[SETS - 1], 16)

            def load_x(b, i):
                sp.dma_start(xt[i][:], x1_b[b]).then_inc(x_in[i], 16)

            def load_context(b, i):
                sp.dma_start(ctx_raw[i][:], context[b]).then_inc(c_in[i], 16)

            def opening():
                load_x(0, 0)
                load_context(0, 0)
                sp.dma_start(ident[:], consts["ident"]).then_inc(const_in, 16)
                for b in range(1, SETS):
                    if b < SETS - 1:
                        load_x(b, b)
                    if b < 2:
                        load_context(b, b)
                for b in range(2, SETS):
                    sp.wait_ge(s["ctx_lo_done"], 2 * (b - 1))
                    load_context(b, b % 2)

            def turn(b, i, n, follow):
                if follow >= SETS - 1:
                    sp.wait_ge(x2_out[(i - 1) % SETS], 16 * (n + 1))
                    load_x(b + SETS - 1, (i - 1) % SETS)
                sp.wait_ge(summed, 2 * (b + 1) + 2)
                sp.dma_start(x2_b[b], xt[i][:]).then_inc(x2_out[i], 16)
                if follow >= SETS:
                    sp.wait_ge(s["ctx_lo_done"], 2 * (b + 3))
                    load_context(b + SETS, i % 2)

            batches(sp, opening, turn)
            for i in range(SETS):
                sp.wait_ge(x2_out[i], 16 * (BATCHES // SETS) + (16 if i == SETS - 1 else 0))

        @block.gpsimd
        def _(pool):
            pool.memset(power[:], -0.5).then_inc(power_set, 1)
            pool.wait_ge(power_set, 1)

            def prepare(b, i):
                pool.wait_ge(s["var_done"], b + 1)
                pool.tensor_tensor(rstd[i % 2][:], var[i % 2][:], power[:], ALU.pow).then_inc(s["rstd_done"], 1)
                for part, (lo, hi) in enumerate(CUT):
                    pool.wait_ge(s["ctx_hi_done"], 2 * b + part + 1)
                    pool.tensor_tensor(ctx_lo[i][:, lo:hi], ctx_raw[i % 2][:, lo:hi], as_f32(ctx_hi[i][:, lo:hi]),
                                       ALU.subtract).then_inc(s["ctx_lo_done"], 1)

            def opening():
                prepare(0, 0)
                prepare(1, 1)

            def turn(b, i, n, follow):
                if follow >= 2:
                    prepare(b + 2, (i + 2) % SETS)

            batches(pool, opening, turn)

        @block.scalar
        def _(act):
            def cut(b, i, n):
                act.wait_ge(c_in[i % 2], 16 * n)
                for lo, hi in CUT:
                    act.activation(ctx_hi[i][:, lo:hi], ctx_raw[i % 2][:, lo:hi],
                                   ACT.Copy).then_inc(s["ctx_hi_done"], 1)

            def turn_hi(b, i):
                for half in range(2):
                    act.wait_ge(s["turn_ready"], 2 * b + half + 1)
                    act.activation(qT_hi[i][:, half * 4:half * 4 + 4, :],
                                   turned[half][:].rearrange("p (k s) -> p k s", k=4), ACT.Copy).then_inc(s["turn_hi"], 1)

            def opening():
                cut(0, 0, 1)
                turn_hi(0, 0)
                cut(1, 1, 1)

            def turn(b, i, n, follow):
                act.wait_ge(s["max_ready"], b + 1)
                act.activation(probs[i % 2][:], score[i % 2][:, 0:SEQ], ACT.Exp, bias=nmax[i % 2][:, 0:1],
                               accum_out=total[i % 2][:, 0:1]).then_inc(s["exp_ready"], 1)
                if follow >= 1:
                    turn_hi(b + 1, (i + 1) % 2)
                act.wait_ge(s["pT_ready"], b + 1)
                act.activation(pT_hi[i % 2][:], pT[:, 0:SEQ], ACT.Copy).then_inc(s["pT_hi_done"], 1)
                if follow >= 2:
                    cut(b + 2, (i + 2) % SETS, 2 * n + i // 2 + 2)

            batches(act, opening, turn)

        @block.vector
        def _(dve):
            dve.sem_inc(summed, 2)

            def moments(b, i, n):
                dve.wait_ge(x_in[i], 16 * n)
                for h in range(2):
                    dve.bn_stats(stats[i % 2][:, h, :], xt[i][:, h * 512:(h + 1) * 512])
                dve.drain()
                dve.bn_aggr(mv[i % 2][:], stats[i % 2][:].rearrange("p h s -> p (h s)")).then_inc(s["mv_done"], 1)
                dve.wait_ge(s["mv_done"], b + 1)
                dve.tensor_scalar(var[i % 2][:], mv[i % 2][:, 1:2], EPS, None, ALU.add).then_inc(s["var_done"], 1)

            def normalise(b, i):
                dve.wait_ge(s["rstd_done"], b + 1)
                dve.tensor_scalar(hn[i % 2][:], xt[i][:], mv[i % 2][:, 0:1], rstd[i % 2][:, 0:1],
                                  ALU.subtract, ALU.mult).then_inc(s["hn_ready"], 1)

            def turn_lo(b, i):
                for half in range(2):
                    ks = slice(half * 4, half * 4 + 4)
                    dve.wait_ge(s["turn_hi"], 2 * b + half + 1)
                    dve.tensor_tensor(qT_lo[i][:, ks, :], turned[half][:].rearrange("p (k s) -> p k s", k=4),
                                      as_f32(qT_hi[i][:, ks, :]), ALU.subtract).then_inc(s["turn_lo"], 1)

            def opening():
                moments(0, 0, 1)
                normalise(0, 0)
                moments(1, 1, 1)
                turn_lo(0, 0)
                normalise(1, 1)

            def turn(b, i, n, follow):
                dve.wait_ge(s["score_ready"], b + 1)
                dve.tensor_reduce(nmax[i % 2][:], score[i % 2][:, 0:SEQ], AX_X, ALU.max,
                                  negate=True).then_inc(s["max_ready"], 1)
                if follow >= 1:
                    turn_lo(b + 1, (i + 1) % 2)
                dve.wait_ge(s["pT_hi_done"], b + 1)
                dve.tensor_tensor(pT_lo[i % 2][:], pT[:, 0:SEQ], as_f32(pT_hi[i % 2][:]),
                                  ALU.subtract).then_inc(s["pT_lo_done"], 1)
                dve.wait_ge(s["exp_ready"], b + 1)
                dve.reciprocal(rtotal[i % 2][:], total[i % 2][:]).then_inc(s["rtotal_ready"], 1)
                if follow >= 2:
                    moments(b + 2, (i + 2) % SETS, n + (i + 2) // SETS + 1)
                dve.wait_ge(s["rtotal_ready"], b + 1)
                for c in range(2):
                    cols = slice(c * CH, (c + 1) * CH)
                    dve.wait_ge(s["out_ready"], 2 * b + c + 1)
                    dve.scalar_tensor_tensor(out=xt[i][:, cols], in0=out[c][:], scalar=rtotal[i % 2][:, 0:1],
                                             in1=xt[i][:, cols], op0=ALU.mult, op1=ALU.add).then_inc(summed, 1)
                if follow >= 2:
                    normalise(b + 2, (i + 2) % SETS)

            batches(dve, opening, turn)

        @block.tensor
        def _(pe):
            pe.wait_ge(const_in, 16)

            def turn_hn(b, i, free):
                pe.wait_ge(s["hn_ready"], b + 1)
                for half in range(2):
                    if free is not None:
                        pe.wait_ge(s["turn_lo"], free + half)
                    for j in range(4):
                        k = half * 4 + j
                        ins = pe.transpose(turned[half][:, j * P:(j + 1) * P], hn[i][:, k * P:(k + 1) * P], ident[:])
                    ins.then_inc(s["turn_ready"], 1)

            def scores(b, i):
                pe.wait_ge(s["turn_lo"], 2 * (b + 1))
                pe.wait_ge(s["ctx_lo_done"], 2 * b + 1)
                for k in range(KT):
                    cols = slice(D + k * P, D + (k + 1) * P)
                    ins = three_passes(pe, score[i % 2][:, 0:SEQ], qT_hi[i % 2][:, k, :], qT_lo[i % 2][:, k, :],
                                       ctx_hi[i][:, cols], ctx_lo[i][:, cols], k == 0, k == KT - 1)
                ins.then_inc(s["score_ready"], 1)

            def opening():
                turn_hn(0, 0, None)
                scores(0, 0)

            def turn(b, i, n, follow):
                if follow >= 1:
                    turn_hn(b + 1, (i + 1) % 2, 2 * b + 1)
                pe.wait_ge(s["exp_ready"], b + 1)
                pe.transpose(pT[:, 0:SEQ], probs[i % 2][:], ident[:]).then_inc(s["pT_ready"], 1)
                if follow >= 1:
                    scores(b + 1, (i + 1) % SETS)
                pe.wait_ge(s["pT_lo_done"], b + 1)
                pe.wait_ge(s["ctx_lo_done"], 2 * (b + 1))
                for c in range(2):
                    cols = slice(c * CH, (c + 1) * CH)
                    pe.wait_ge(summed, 2 * b + c + 1)
                    three_passes(pe, out[c][:], pT_hi[i % 2][:], pT_lo[i % 2][:], ctx_hi[i][:, cols],
                                 ctx_lo[i][:, cols], True, True).then_inc(s["out_ready"], 1)

            batches(pe, opening, turn)


def feed(nc, x2_d, signs, scales, consts, out_d):
    LAYERS = 3
    HID = 2 * KT
    ctx = ExitStack()
    with ctx:
        def sb(name, shape, dt=F32):
            return ctx.enter_context(nc.sbuf_tensor(name, shape, dt))

        def banks(name, n=2):
            return [ctx.enter_context(nc.psum_tensor(f"{name}{i}", [P, CH], F32)) for i in range(n)]

        def sem(name):
            return ctx.enter_context(nc.semaphore(name))

        w = [sb(f"ff_w{l}", [P, KT, D], F32R) for l in range(LAYERS)]
        xt = [sb(f"ff_x{i}", [P, BPC, D]) for i in range(2)]
        hn = sb("ff_hn", [P, 2, D])
        act_hi = [sb(f"ff_act_hi{i}", [P, KT, CH], F32R) for i in range(2)]
        act_lo = [sb(f"ff_act_lo{i}", [P, KT, CH], F32R) for i in range(2)]
        hid = sb("ff_hid", [P, 2, CH])
        stats = sb("ff_stats", [P, BPC, 2, 6])
        mv = sb("ff_mv", [P, BPC, 2])
        var = sb("ff_var", [P, BPC])
        rstd = sb("ff_rstd", [P, BPC])
        power = sb("ff_power", [P, BPC])
        ident = sb("ff_ident", [P, P])
        sign_mul = sb("ff_sign_mul", [P, KT])
        sign_add = sb("ff_sign_add", [P, KT])
        scale = sb("ff_scale", [P, LAYERS])
        scale2 = sb("ff_scale2", [P, LAYERS])
        bit_words = xt[1][:].rearrange("p b d -> p (b d)").bitcast(I32).rearrange("p (l k m) -> p l k m", l=2, k=KT)
        bits = xt[1][:].rearrange("p b d -> p (b d)").bitcast(U8).rearrange("p (l k m) -> p l k m", l=2, k=KT)

        turned, lin, outb = banks("ff_turned"), banks("ff_lin"), banks("ff_out")
        const_in, power_set = sem("ff_const_in"), sem("ff_power_set")
        bits_in = [sem(f"ff_bits_in{l}") for l in range(LAYERS)]
        w_ready = [sem(f"ff_w_ready{l}") for l in range(LAYERS)]
        x_in = [sem(f"ff_x_in{i}") for i in range(2)]
        y_out = [sem(f"ff_y_out{i}") for i in range(2)]
        names = ("scale2_ready", "mv_done", "var_done", "rstd_done", "hn_ready", "turn_ready", "turn_hi",
                 "turn_lo", "lin_ready", "relu_done", "hid_hi", "hid_lo", "out_ready", "summed")
        s = {n: sem(f"ff_{n}") for n in names}
        x2_c = x2_d.rearrange("(c b p) d -> c p b d", c=CHUNKS, p=P)
        out_c = out_d.rearrange("(c b p) d -> c p b d", c=CHUNKS, p=P)
        block = ctx.enter_context(nc.Block())

        def chunks(eng, body):
            with eng.Fori(0, CHUNKS // 2 - 1) as n:
                body(2 * n, 0, n, False)
                body(2 * n + 1, 1, n + 1, False)
            body(CHUNKS - 2, 0, CHUNKS // 2 - 1, False)
            body(CHUNKS - 1, 1, 0, True)

        @block.sync
        def _(sp):
            sp.dma_start(xt[0][:], x2_c[0]).then_inc(x_in[0], 16)
            for to, name in ((ident, "ident"), (sign_mul, "sign_mul"), (sign_add, "sign_add")):
                sp.dma_start(to[:], consts[name]).then_inc(const_in, 16)
            sp.dma_start(scale[:], scales).then_inc(const_in, 16)
            for l in range(2):
                sp.dma_start(bit_words[:, l], signs[l]).then_inc(bits_in[l], 16)
            sp.wait_ge(w_ready[0], 1)
            sp.dma_start(bit_words[:, 0], signs[2]).then_inc(bits_in[2], 16)
            for l in range(1, LAYERS):
                sp.wait_ge(w_ready[l], 1)
            sp.dma_start(xt[1][:], x2_c[1]).then_inc(x_in[1], 16)

            def store(c, i):
                sp.wait_ge(s["summed"], 2 * BPC * (c + 1))
                sp.dma_start(out_c[c], xt[i][:]).then_inc(y_out[i], 16)

            with sp.Fori(0, CHUNKS // 2 - 1) as n:
                for i in range(2):
                    store(2 * n + i, i)
                    sp.wait_ge(y_out[i], 16 * (n + 1))
                    sp.dma_start(xt[i][:], x2_c[2 * n + 2 + i]).then_inc(x_in[i], 16)
            for i in range(2):
                store(CHUNKS - 2 + i, i)
            for i in range(2):
                sp.wait_ge(y_out[i], 16 * (CHUNKS // 2))

        @block.gpsimd
        def _(pool):
            pool.memset(power[:], -0.5).then_inc(power_set, 1)
            pool.wait_ge(power_set, 1)

            def root(c):
                pool.wait_ge(s["var_done"], c + 1)
                pool.tensor_tensor(rstd[:], var[:], power[:], ALU.pow).then_inc(s["rstd_done"], 1)

            root(0)
            pool.wait_ge(const_in, 64)
            pool.wait_ge(bits_in[2], 16)
            for k in range(KT):
                ins = pool.tensor_scalar(w[2][:, k, :], bits[:, 0, k, :], sign_mul[:, k:k + 1], sign_add[:, k:k + 1],
                                         ALU.mult, ALU.add)
            ins.then_inc(w_ready[2], 1)
            chunks(pool, lambda c, i, n_next, last: None if last else root(c + 1))

        @block.scalar
        def _(act):
            def turn(c, i, t):
                for half in range(2):
                    act.wait_ge(s["turn_ready"], 2 * BPC * c + 2 * t + half + 1)
                    act.activation(act_hi[i][:, half * 4:half * 4 + 4, t * P:(t + 1) * P],
                                   turned[half][:].rearrange("p (k s) -> p k s", k=4), ACT.Copy).then_inc(s["turn_hi"], 1)

            def hidden(c, i, layer):
                to = act_hi[1 - i] if layer == 0 else act_hi[i]
                for m in range(KT):
                    a = HID * c + KT * layer + m
                    act.wait_ge(s["lin_ready"], a + 1)
                    if layer or m >= 2:
                        act.wait_ge(s["hid_lo"], a - 1)
                    act.activation(hid[:, m % 2, :], lin[m % 2][:], ACT.Relu,
                                   scale=scale2[:, layer:layer + 1]).then_inc(s["relu_done"], 1)
                    act.wait_ge(s["relu_done"], a + 1)
                    act.activation(to[:, m, :], hid[:, m % 2, :], ACT.Copy).then_inc(s["hid_hi"], 1)

            def body(c, i, n_next, last):
                hidden(c, i, 0)
                hidden(c, i, 1)
                if not last:
                    for t in range(BPC):
                        turn(c + 1, 1 - i, t)

            act.wait_ge(const_in, 64)
            act.wait_ge(bits_in[1], 16)
            for k in range(KT):
                ins = act.activation(w[1][:, k, :], bits[:, 1, k, :], ACT.Identity, scale=sign_mul[:, k:k + 1],
                                     bias=sign_add[:, k:k + 1])
            ins.then_inc(w_ready[1], 1)
            act.wait_ge(s["scale2_ready"], 1)
            for t in range(BPC):
                turn(0, 0, t)
            chunks(act, body)

        @block.vector
        def _(dve):
            def moments(c, i, n):
                dve.wait_ge(x_in[i], 16 * (n + 1))
                for t in range(BPC):
                    for h in range(2):
                        dve.bn_stats(stats[:, t, h, :], xt[i][:, t, h * 512:(h + 1) * 512])
                dve.drain()
                for t in range(BPC):
                    ins = dve.bn_aggr(mv[:, t, :], stats[:, t].rearrange("p h s -> p (h s)"))
                ins.then_inc(s["mv_done"], 1)
                dve.wait_ge(s["mv_done"], c + 1)
                dve.tensor_scalar(var[:], mv[:, :, 1], EPS, None, ALU.add).then_inc(s["var_done"], 1)

            def normalise(c, i, t):
                if t == 0:
                    dve.wait_ge(s["rstd_done"], c + 1)
                dve.tensor_scalar(hn[:, t % 2, :], xt[i][:, t, :], mv[:, t, 0:1], rstd[:, t:t + 1],
                                  ALU.subtract, ALU.mult).then_inc(s["hn_ready"], 1)

            def turn(c, i, t):
                for half in range(2):
                    at = (slice(None), slice(half * 4, half * 4 + 4), slice(t * P, (t + 1) * P))
                    dve.wait_ge(s["turn_hi"], 2 * BPC * c + 2 * t + half + 1)
                    dve.tensor_tensor(act_lo[i][at], turned[half][:].rearrange("p (k s) -> p k s", k=4),
                                      as_f32(act_hi[i][at]), ALU.subtract).then_inc(s["turn_lo"], 1)

            def hidden(c, i, layer):
                at = 1 - i if layer == 0 else i
                for m in range(KT):
                    dve.wait_ge(s["hid_hi"], HID * c + KT * layer + m + 1)
                    dve.tensor_tensor(act_lo[at][:, m, :], hid[:, m % 2, :], as_f32(act_hi[at][:, m, :]),
                                      ALU.subtract).then_inc(s["hid_lo"], 1)

            def body(c, i, n_next, last):
                hidden(c, i, 0)
                if not last:
                    moments(c + 1, 1 - i, n_next)
                    normalise(c + 1, 1 - i, 0)
                    normalise(c + 1, 1 - i, 1)
                hidden(c, i, 1)
                for t in range(BPC):
                    for n in range(2):
                        cols = slice(n * CH, (n + 1) * CH)
                        dve.wait_ge(s["out_ready"], 2 * BPC * c + 2 * t + n + 1)
                        dve.scalar_tensor_tensor(out=xt[i][:, t, cols], in0=outb[n][:], scalar=scale[:, 2:3],
                                                 in1=xt[i][:, t, cols], op0=ALU.mult, op1=ALU.add).then_inc(s["summed"], 1)
                    if not last:
                        turn(c + 1, 1 - i, t)
                        if t + 2 < BPC:
                            normalise(c + 1, 1 - i, t + 2)

            moments(0, 0, 0)
            normalise(0, 0, 0)
            normalise(0, 0, 1)
            dve.wait_ge(const_in, 64)
            dve.tensor_scalar(scale2[:], scale[:], 2.0, None, ALU.mult).then_inc(s["scale2_ready"], 1)
            dve.wait_ge(bits_in[0], 16)
            for k in range(KT):
                ins = dve.tensor_scalar(w[0][:, k, :], bits[:, 0, k, :], 2.0, -1.0, ALU.mult, ALU.add)
            ins.then_inc(w_ready[0], 1)
            for t in range(BPC):
                turn(0, 0, t)
                if t + 2 < BPC:
                    normalise(0, 0, t + 2)
            chunks(dve, body)

        @block.tensor
        def _(pe):
            def turn(c, i, t):
                pe.wait_ge(s["hn_ready"], BPC * c + t + 1)
                for half in range(2):
                    if t:
                        pe.wait_ge(s["turn_lo"], 2 * BPC * c + 2 * (t - 1) + half + 1)
                    for j in range(4):
                        k = half * 4 + j
                        ins = pe.transpose(turned[half][:, j * P:(j + 1) * P], hn[:, t % 2, k * P:(k + 1) * P], ident[:])
                    ins.then_inc(s["turn_ready"], 1)

            def hidden(c, i, layer):
                at = i if layer == 0 else 1 - i
                if layer == 0:
                    pe.wait_ge(s["turn_lo"], 2 * BPC * (c + 1))
                pe.wait_ge(w_ready[layer], 1)
                for m in range(KT):
                    a = HID * c + KT * layer + m
                    if layer or m >= 2:
                        pe.wait_ge(s["relu_done"], a - 1)
                    for k in range(KT):
                        if layer and m == 0:
                            pe.wait_ge(s["hid_lo"], HID * c + k + 1)
                        wk = w[layer][:, k, m * P:(m + 1) * P]
                        pe.matmul(lin[m % 2][:], wk, act_hi[at][:, k, :], start=k == 0, stop=False)
                        ins = pe.matmul(lin[m % 2][:], wk, act_lo[at][:, k, :], start=False, stop=k == KT - 1)
                    ins.then_inc(s["lin_ready"], 1)

            def body(c, i, n_next, last):
                hidden(c, i, 0)
                hidden(c, i, 1)
                pe.wait_ge(w_ready[2], 1)
                for t in range(BPC):
                    for n in range(2):
                        if t:
                            pe.wait_ge(s["summed"], 2 * BPC * c + 2 * (t - 1) + n + 1)
                        else:
                            pe.wait_ge(s["summed"], 2 * BPC * c)
                        for k in range(KT):
                            if t == 0 and n == 0:
                                pe.wait_ge(s["hid_lo"], HID * c + KT + k + 1)
                            rows = slice(t * P, (t + 1) * P)
                            wk = w[2][:, k, n * CH:(n + 1) * CH]
                            pe.matmul(outb[n][:], act_hi[i][:, k, rows], wk, start=k == 0, stop=False)
                            ins = pe.matmul(outb[n][:], act_lo[i][:, k, rows], wk, start=False, stop=k == KT - 1)
                        ins.then_inc(s["out_ready"], 1)
                    if not last:
                        turn(c + 1, 1 - i, t)

            pe.wait_ge(const_in, 64)
            for t in range(BPC):
                turn(0, 0, t)
            chunks(pe, body)


def build(nc, a, out):
    def scratch(name, shape):
        return nc.dram_tensor(name, shape, F32, kind="Internal").ap()

    tok_d = scratch("tok_d", [CHUNKS, P, PACK])
    wabs_d = scratch("wabs_d", [PAIRS, P, 2, QT, PAIR * P])
    wvo_d = scratch("wvo_d", [PAIRS, P, 2, PAIR, D])
    wqr_d = scratch("wqr_d", [QUADS, P, 2, QT, 2, P])
    x1_d = scratch("x1_d", [TOKENS, D])
    x2_d = scratch("x2_d", [TOKENS, D])
    project(nc, a["x"], a["w_down"], a, tok_d)
    absorb(nc, a["w_heads"], a["w_rope"], wabs_d, wvo_d, wqr_d)
    attend(nc, a["x"], tok_d, wabs_d, wvo_d, wqr_d, a, x1_d)
    cross(nc, x1_d, a["context"], a, x2_d)
    feed(nc, x2_d, a["signs"], a["scales"], a, out)


def constants():
    half = np.arange(0, DR, 2, dtype=np.float32) / np.float32(DR)
    freqs = np.float32(1.0) / np.power(np.float32(10000.0), half)
    wave = np.float32(2.0 * np.pi) / freqs
    ramp = np.clip((wave / np.float32(4096.0) - np.float32(1.0)) / np.float32(31.0), 0, 1).astype(np.float32)
    inv = freqs / (np.float32(1.0) - ramp + ramp * np.float32(40.0))
    angle = (np.arange(SEQ, dtype=np.float32)[None, :] * inv[:, None]).astype(np.float32)
    cos, sin = np.cos(angle).astype(np.float32), np.sin(angle).astype(np.float32)
    sc = np.float32(SCORE_SCALE)
    row = np.arange(KT * P).reshape(KT, P).T
    inhibitory = row >= round(D * 0.8)
    return {
        "ident": np.eye(P, dtype=np.float32),
        "mask": np.where(np.tril(np.ones((SEQ, SEQ), bool)), 0, MASKED).astype(np.float32),
        "cos": np.tile(cos, (QUAD, 1)),
        "sin": np.tile(sin, (QUAD, 1)),
        "k_tab": np.concatenate([cos * sc, cos * sc, -sin * sc, sin * sc]),
        "sign_mul": np.where(inhibitory, -8, 2).astype(np.float32),
        "sign_add": np.where(inhibitory, 4, -1).astype(np.float32),
    }


def kernel(x, ctx_4096, L0_attn_w_q_down, L0_attn_w_q_up_nope, L0_attn_w_q_up_rope, L0_attn_w_kv_down,
           L0_attn_w_k_rope, L0_attn_w_uk, L0_attn_w_uv, L0_attn_w_out, L0_ffn_k0, L0_ffn_s0, L0_ffn_k1,
           L0_ffn_s1, L0_ffn_k2, L0_ffn_s2):
    import concourse.bacc as bacc
    from concourse.bass_utils import run_bass_kernel_spmd

    x, ctx_4096 = np.asarray(x), np.asarray(ctx_4096)
    wkr = np.asarray(L0_attn_w_k_rope)
    w_down = np.concatenate([np.asarray(L0_attn_w_q_down), np.asarray(L0_attn_w_kv_down), wkr,
                             wkr[:, HALF:], wkr[:, :HALF]], axis=1)
    w_down = w_down.reshape(KT, P, 5 * P).transpose(1, 0, 2)
    nope_t = np.asarray(L0_attn_w_q_up_nope).reshape(QL, HEADS, DN).transpose(1, 2, 0)
    heads = np.concatenate([nope_t, np.asarray(L0_attn_w_uk).reshape(HEADS, DN, KVL),
                            np.asarray(L0_attn_w_uv).reshape(HEADS, DV, KVL),
                            np.asarray(L0_attn_w_out).reshape(HEADS, DV, D)], axis=2)
    heads = heads.reshape(PAIRS, PAIR, P, HEAD_W).transpose(0, 2, 1, 3)
    w_rope = np.asarray(L0_attn_w_q_up_rope).reshape(QT, P, QUADS, QUAD, 2, HALF).transpose(2, 1, 0, 4, 3, 5)
    w_rope = w_rope.reshape(QUADS, P, QT, 2, P)
    ctx_t = ctx_4096.reshape(BATCHES, SEQ, KT, P).transpose(0, 3, 2, 1).reshape(BATCHES, P, KT * SEQ)
    context = np.concatenate([ctx_4096, ctx_t], axis=2)
    signs = np.stack([np.asarray(k).reshape(KT, P, D).transpose(1, 0, 2)
                      for k in (L0_ffn_k0, L0_ffn_k1, L0_ffn_k2)]).view(np.int32)
    scales = np.broadcast_to(np.stack([np.asarray(s).reshape(()) for s in (L0_ffn_s0, L0_ffn_s1, L0_ffn_s2)]), (P, 3))
    arrays = {"x": x.reshape(TOKENS, D), "w_down": w_down, "w_heads": heads, "w_rope": w_rope, "context": context,
              "signs": signs, "scales": scales, **constants()}
    arrays = {name: np.ascontiguousarray(v) for name, v in arrays.items()}

    nc = bacc.Bacc("TRN2", target_bir_lowering=False, num_devices=1)
    a = {name: nc.dram_tensor(f"in_{name}", v.shape, mybir.dt.from_np(v.dtype), kind="ExternalInput").ap()
         for name, v in arrays.items()}
    out = nc.dram_tensor("out", [TOKENS, D], F32, kind="ExternalOutput").ap()
    build(nc, a, out)
    r = run_bass_kernel_spmd(nc, [{f"in_{name}": v for name, v in arrays.items()}], core_ids=[0])
    return r.results[0]["out"].reshape(BATCHES, SEQ, D)
```

```python
from contextlib import ExitStack

import numpy as np

import concourse.bass as bass
from concourse import mybir

F32 = mybir.dt.float32
F32R = mybir.dt.float32r
BF16 = mybir.dt.bfloat16
U8 = mybir.dt.uint8
I32 = mybir.dt.int32
ACT = mybir.ActivationFunctionType
ALU = mybir.AluOpType
AX_X = mybir.AxisListType.X

P = 128
BATCHES, SEQ, D = 16, 128, 1024
TOKENS = BATCHES * SEQ
KT = D // P
HEADS, QL, KVL, DN, DR, DV = 32, 384, 128, 128, 64, 128
QT = QL // P
HALF = DR // 2
QUAD = P // HALF
QUADS = HEADS // QUAD
PAIR = 2
PAIRS = HEADS // PAIR
CH = 512
CHUNKS = TOKENS // CH
BPC = CH // SEQ
GROUPS = 2
CPG = CHUNKS // GROUPS
BPG = BATCHES // GROUPS
EPS = 1e-5
SCORE_SCALE = float(1.0 / np.sqrt(np.float32(DN + DR)))
MASKED = -1e30
HEAD_W = QL + KVL + KVL + D

CQ_HI, CQ_LO = 0, QT * CH
KT_HI, KT_LO = 2 * QT * CH, 2 * QT * CH + CH
KV_HI, KV_LO = KT_LO + CH, KT_LO + 2 * CH
KR_HI, KR_LO = KT_LO + 3 * CH, KT_LO + 4 * CH
PACK = KR_LO + CH


def as_f32(ap):
    return ap.bitcast(F32)


def three_passes(pe, out, w_hi, w_lo, x_hi, x_lo, first, last):
    pe.matmul(out, w_hi, x_hi, start=first, stop=False)
    pe.matmul(out, w_hi, x_lo, start=False, stop=False)
    return pe.matmul(out, w_lo, x_hi, start=False, stop=last)


def project(nc, x, w_down, consts, tok_d):
    WC = 5 * P
    ctx = ExitStack()
    with ctx:
        def sb(name, shape, dt=F32):
            return ctx.enter_context(nc.sbuf_tensor(name, shape, dt))

        def bank(name):
            return ctx.enter_context(nc.psum_tensor(name, [P, CH], F32))

        def sem(name):
            return ctx.enter_context(nc.semaphore(name))

        w_raw = sb("pj_w_raw", [P, KT, WC])
        w_hi = sb("pj_w_hi", [P, KT, WC], F32R)
        w_lo = sb("pj_w_lo", [P, KT, WC], F32R)
        ident = sb("pj_ident", [P, P])
        k_tab = sb("pj_k_tab", [P, SEQ])
        eps = sb("pj_eps", [P, 1])
        xin = sb("pj_x", [P, BPC, D])
        hn = sb("pj_hn", [P, BPC, D])
        stats = sb("pj_stats", [P, BPC, 2, 6])
        mv = sb("pj_mv", [P, BPC, 2])
        std = sb("pj_std", [P, BPC])
        rstd = sb("pj_rstd", [P, BPC])
        hT_hi = sb("pj_hT_hi", [P, KT, CH], F32R)
        hT_lo = sb("pj_hT_lo", [P, KT, CH], F32R)
        pack = sb("pj_pack", [P, PACK], F32R)
        kv_raw = sb("pj_kv_raw", [P, CH])
        k_cos = sb("pj_k_cos", [DR, CH])
        k_sin = sb("pj_k_sin", [DR, CH])
        k_rot = sb("pj_k_rot", [DR, CH])

        turned = [bank(f"pj_turned{i}") for i in range(2)]
        down = [bank(f"pj_down{m}") for m in range(5)]
        kv_turned = bank("pj_kv_turned")

        w_in, const_in, x_in = sem("pj_w_in"), sem("pj_const_in"), sem("pj_x_in")
        w_hi_done, w_lo_done = sem("pj_w_hi_done"), sem("pj_w_lo_done")
        rstd_done, sin_done = sem("pj_rstd_done"), sem("pj_sin_done")
        var_ready, std_ready, hn_ready = sem("pj_var_ready"), sem("pj_std_ready"), sem("pj_hn_ready")
        turn_ready, turn_hi, turn_lo = sem("pj_turn_ready"), sem("pj_turn_hi"), sem("pj_turn_lo")
        down_ready, cq_hi, cq_lo = sem("pj_down_ready"), sem("pj_cq_hi"), sem("pj_cq_lo")
        kt_hi, kt_lo, kv_raw_ready = sem("pj_kt_hi"), sem("pj_kt_lo"), sem("pj_kv_raw_ready")
        kv_turn_ready, kv_hi, kv_lo = sem("pj_kv_turn_ready"), sem("pj_kv_hi"), sem("pj_kv_lo")
        rot_ready, kr_hi, kr_lo = sem("pj_rot_ready"), sem("pj_kr_hi"), sem("pj_kr_lo")
        zeroed, stored = sem("pj_zeroed"), sem("pj_stored")

        x_chunks = x.rearrange("(c b p) d -> c p b d", c=CHUNKS, p=P)
        block = ctx.enter_context(nc.Block())

        @block.sync
        def _(sp):
            sp.dma_start(ident[:], consts["ident"]).then_inc(const_in, 16)
            sp.dma_start(k_tab[:], consts["k_tab"]).then_inc(const_in, 16)
            sp.dma_start(xin[:], x_chunks[0]).then_inc(x_in, 16)
            sp.dma_start(w_raw[:], w_down).then_inc(w_in, 16)

            def store(c):
                sp.wait_ge(kr_hi, c + 1)
                sp.wait_ge(kr_lo, c + 1)
                sp.wait_ge(zeroed, 1)
                sp.dma_start(tok_d[c], as_f32(pack[:])).then_inc(stored, 16)

            with sp.Fori(0, CHUNKS - 1) as c:
                sp.wait_ge(hn_ready, BPC * (c + 1))
                sp.dma_start(xin[:], x_chunks[c + 1]).then_inc(x_in, 16)
                store(c)
            store(CHUNKS - 1)
            sp.wait_ge(stored, 16 * CHUNKS)

        @block.gpsimd
        def _(pool):
            pool.memset(as_f32(pack[DR:P, KR_LO:KR_LO + CH]), 0.0).then_inc(zeroed, 1)

        @block.scalar
        def _(act):
            act.wait_ge(w_in, 16)
            act.activation(w_hi[:], w_raw[:], ACT.Copy).then_inc(w_hi_done, 1)

            def root():
                act.activation(std[:], mv[:, :, 1], ACT.Sqrt, bias=eps[:, 0:1]).then_inc(std_ready, 1)

            act.wait_ge(var_ready, 1)
            root()

            def chunk(c, last):
                for z in range(2 * BPC):
                    t, half = z // 2, z % 2
                    act.wait_ge(turn_ready, 2 * BPC * c + z + 1)
                    act.activation(hT_hi[:, half * 4:half * 4 + 4, t * P:(t + 1) * P],
                                   turned[z % 2][:].rearrange("p (k s) -> p k s", k=4),
                                   ACT.Copy).then_inc(turn_hi, 1)
                if not last:
                    act.wait_ge(var_ready, c + 2)
                    root()
                act.wait_ge(stored, 16 * c)
                for m in range(QT):
                    act.wait_ge(down_ready, 5 * c + m + 1)
                    act.activation(pack[:, CQ_HI + m * CH:CQ_HI + (m + 1) * CH], down[m][:],
                                   ACT.Copy).then_inc(cq_hi, 1)
                act.wait_ge(down_ready, 5 * c + 4)
                act.activation(kv_raw[:], down[3][:], ACT.Copy).then_inc(kv_raw_ready, 1)
                act.activation(pack[:, KT_HI:KT_HI + CH], down[3][:], ACT.Copy,
                               scale=SCORE_SCALE).then_inc(kt_hi, 1)
                act.wait_ge(kv_turn_ready, c + 1)
                act.activation(pack[:, KV_HI:KV_HI + CH], kv_turned[:], ACT.Copy).then_inc(kv_hi, 1)
                act.wait_ge(rot_ready, c + 1)
                act.activation(pack[0:DR, KR_HI:KR_HI + CH], k_rot[:], ACT.Copy)
                act.activation(pack[DR:P, KR_HI:KR_HI + CH], k_rot[:], ACT.Copy).then_inc(kr_hi, 1)

            with act.Fori(0, CHUNKS - 1) as c:
                chunk(c, False)
            chunk(CHUNKS - 1, True)

        @block.vector
        def _(dve):
            def normalise(c):
                dve.wait_ge(x_in, 16 * (c + 1))
                for t in range(BPC):
                    for h in range(2):
                        dve.bn_stats(stats[:, t, h, :], xin[:, t, h * 512:(h + 1) * 512])
                dve.drain()
                for t in range(BPC):
                    ins = dve.bn_aggr(mv[:, t, :], stats[:, t].rearrange("p h s -> p (h s)"))
                ins.then_inc(var_ready, 1)
                dve.wait_ge(std_ready, c + 1)
                dve.reciprocal(rstd[:], std[:]).then_inc(rstd_done, 1)
                dve.wait_ge(rstd_done, c + 1)
                for t in range(BPC):
                    dve.tensor_scalar(hn[:, t, :], xin[:, t, :], mv[:, t, 0:1], rstd[:, t:t + 1],
                                      ALU.subtract, ALU.mult).then_inc(hn_ready, 1)

            dve.memset(eps[:], EPS)
            normalise(0)
            dve.wait_ge(w_hi_done, 1)
            dve.tensor_tensor(w_lo[:], w_raw[:], as_f32(w_hi[:]), ALU.subtract).then_inc(w_lo_done, 1)

            def chunk(c, last):
                for z in range(2 * BPC):
                    t, half = z // 2, z % 2
                    dve.wait_ge(turn_hi, 2 * BPC * c + z + 1)
                    at = (slice(None), slice(half * 4, half * 4 + 4), slice(t * P, (t + 1) * P))
                    dve.tensor_tensor(hT_lo[at], turned[z % 2][:].rearrange("p (k s) -> p k s", k=4),
                                      as_f32(hT_hi[at]), ALU.subtract).then_inc(turn_lo, 1)
                if not last:
                    normalise(c + 1)
                for m in range(QT):
                    dve.wait_ge(cq_hi, QT * c + m + 1)
                    dve.tensor_tensor(pack[:, CQ_LO + m * CH:CQ_LO + (m + 1) * CH], down[m][:],
                                      as_f32(pack[:, CQ_HI + m * CH:CQ_HI + (m + 1) * CH]),
                                      ALU.subtract).then_inc(cq_lo, 1)
                dve.wait_ge(kt_hi, c + 1)
                dve.scalar_tensor_tensor(out=pack[:, KT_LO:KT_LO + CH], in0=down[3][:], scalar=SCORE_SCALE,
                                         in1=as_f32(pack[:, KT_HI:KT_HI + CH]), op0=ALU.mult,
                                         op1=ALU.subtract).then_inc(kt_lo, 1)
                dve.wait_ge(kv_turn_ready, c + 1)
                dve.wait_ge(kv_hi, c + 1)
                dve.tensor_tensor(pack[:, KV_LO:KV_LO + CH], kv_turned[:],
                                  as_f32(pack[:, KV_HI:KV_HI + CH]), ALU.subtract).then_inc(kv_lo, 1)
                dve.wait_ge(down_ready, 5 * c + 5)

                def times_table(out, rows):
                    return dve.tensor_tensor(
                        out.rearrange("p (b s) -> p b s", b=BPC),
                        down[4][rows, :].rearrange("p (b s) -> p b s", b=BPC),
                        k_tab[rows, :].unsqueeze(1).to_broadcast([DR, BPC, SEQ]), ALU.mult)

                dve.wait_ge(const_in, 32)
                times_table(k_cos[:], slice(0, DR))
                times_table(k_sin[:], slice(DR, P)).then_inc(sin_done, 1)
                dve.wait_ge(sin_done, c + 1)
                dve.tensor_tensor(k_rot[:], k_cos[:], k_sin[:], ALU.add).then_inc(rot_ready, 1)
                dve.wait_ge(rot_ready, c + 1)
                dve.wait_ge(kr_hi, c + 1)
                dve.tensor_tensor(pack[0:DR, KR_LO:KR_LO + CH], k_rot[:],
                                  as_f32(pack[0:DR, KR_HI:KR_HI + CH]), ALU.subtract).then_inc(kr_lo, 1)

            with dve.Fori(0, CHUNKS - 1) as c:
                chunk(c, False)
            chunk(CHUNKS - 1, True)

        @block.tensor
        def _(pe):
            pe.wait_ge(const_in, 32)

            def chunk(c):
                for z in range(2 * BPC):
                    t, half = z // 2, z % 2
                    pe.wait_ge(hn_ready, BPC * c + t + 1)
                    if z >= 2:
                        pe.wait_ge(turn_lo, 2 * BPC * c + z - 1)
                    else:
                        pe.wait_ge(turn_lo, 2 * BPC * c)
                    for j in range(4):
                        k = half * 4 + j
                        ins = pe.transpose(turned[z % 2][:, j * P:(j + 1) * P],
                                           hn[:, t, k * P:(k + 1) * P], ident[:])
                    ins.then_inc(turn_ready, 1)
                pe.wait_ge(turn_lo, 2 * BPC * (c + 1))
                pe.wait_ge(w_lo_done, 1)
                for m in range(5):
                    if m < QT:
                        pe.wait_ge(cq_lo, QT * c)
                    elif m == 3:
                        pe.wait_ge(kt_lo, c)
                    else:
                        pe.wait_ge(rot_ready, c)
                    cols = slice(m * P, (m + 1) * P)
                    for k in range(KT):
                        ins = three_passes(pe, down[m][:], w_hi[:, k, cols], w_lo[:, k, cols],
                                           hT_hi[:, k, :], hT_lo[:, k, :], k == 0, k == KT - 1)
                    ins.then_inc(down_ready, 1)
                pe.wait_ge(kv_raw_ready, c + 1)
                pe.wait_ge(kv_lo, c)
                for b in range(BPC):
                    ins = pe.transpose(kv_turned[:, b * P:(b + 1) * P], kv_raw[:, b * P:(b + 1) * P], ident[:])
                ins.then_inc(kv_turn_ready, 1)

            with pe.Fori(0, CHUNKS) as c:
                chunk(c)


def absorb(nc, w_heads, w_rope, wabs_d, wvo_d, wqr_d):
    ctx = ExitStack()
    with ctx:
        def sb(name, shape, dt=F32):
            return ctx.enter_context(nc.sbuf_tensor(name, shape, dt))

        def sem(name):
            return ctx.enter_context(nc.semaphore(name))

        UK, UV, OUT = QL, QL + KVL, QL + 2 * KVL
        raw = [sb(f"ab_raw{i}", [P, PAIR, HEAD_W]) for i in range(2)]
        hi = [sb(f"ab_hi{i}", [P, PAIR, HEAD_W], F32R) for i in range(2)]
        lo = [sb(f"ab_lo{i}", [P, PAIR, HEAD_W], F32R) for i in range(2)]
        wabs = [sb(f"ab_wabs{i}", [P, 2, QT, PAIR * P], F32R) for i in range(2)]
        wvo = [sb(f"ab_wvo{i}", [P, 2, PAIR, D], F32R) for i in range(2)]
        rope_raw = sb("ab_rope_raw", [P, QT, 2, P])
        rope = sb("ab_rope", [P, 2, QT, 2, P], F32R)
        abs_bank = [ctx.enter_context(nc.psum_tensor(f"ab_abs{i}", [P, QT, P], F32)) for i in range(2)]
        vo_bank = [ctx.enter_context(nc.psum_tensor(f"ab_vo{i}", [P, CH], F32)) for i in range(4)]

        raw_in = [sem(f"ab_raw_in{i}") for i in range(2)]
        rope_in, rope_hi, rope_lo, rope_out = (sem(f"ab_rope_{n}") for n in ("in", "hi", "lo", "out"))
        split_hi, split_lo = sem("ab_split_hi"), sem("ab_split_lo")
        abs_ready, abs_hi, abs_lo = sem("ab_abs_ready"), sem("ab_abs_hi"), sem("ab_abs_lo")
        vo_ready, vo_hi, vo_lo = sem("ab_vo_ready"), sem("ab_vo_hi"), sem("ab_vo_lo")
        out_done = [sem(f"ab_out_done{i}") for i in range(2)]
        PPQ = 2
        block = ctx.enter_context(nc.Block())

        @block.sync
        def _(sp):
            with sp.Fori(0, QUADS) as q:
                sp.wait_ge(rope_lo, q)
                sp.dma_start(rope_raw[:], w_rope[q]).then_inc(rope_in, 16)
                for i in range(PPQ):
                    sp.wait_ge(split_lo, PPQ * q)
                    sp.dma_start(raw[i][:], w_heads[PPQ * q + i]).then_inc(raw_in[i], 16)

        @block.gpsimd
        def _(pool):
            with pool.Fori(0, QUADS) as q:
                pool.wait_ge(rope_lo, q + 1)
                pool.dma_start(wqr_d[q], as_f32(rope[:])).then_inc(rope_out, 16)
                for i in range(PPQ):
                    pool.wait_ge(abs_lo, PAIR * (PPQ * q + i + 1))
                    pool.dma_start(wabs_d[PPQ * q + i], as_f32(wabs[i][:])).then_inc(out_done[i], 16)
                    pool.wait_ge(vo_lo, 2 * PAIR * (PPQ * q + i + 1))
                    pool.dma_start(wvo_d[PPQ * q + i], as_f32(wvo[i][:])).then_inc(out_done[i], 16)
            pool.wait_ge(rope_out, 16 * QUADS)
            for i in range(PPQ):
                pool.wait_ge(out_done[i], 32 * QUADS)

        @block.scalar
        def _(act):
            with act.Fori(0, QUADS) as q:
                act.wait_ge(rope_in, 16 * (q + 1))
                act.wait_ge(rope_out, 16 * q)
                act.activation(rope[:, 0], rope_raw[:], ACT.Copy).then_inc(rope_hi, 1)
                for i in range(PPQ):
                    act.wait_ge(raw_in[i], 16 * (q + 1))
                    act.wait_ge(vo_ready, 2 * PAIR * PPQ * q)
                    act.activation(hi[i][:], raw[i][:], ACT.Copy).then_inc(split_hi, 1)
                for i in range(PPQ):
                    act.wait_ge(out_done[i], 32 * q)
                    for h in range(PAIR):
                        n = PAIR * i + h
                        act.wait_ge(abs_ready, PAIR * PPQ * q + n + 1)
                        act.activation(wabs[i][:, 0, :, h * P:(h + 1) * P], abs_bank[h][:],
                                       ACT.Copy).then_inc(abs_hi, 1)
                        for c in range(2):
                            act.wait_ge(vo_ready, 2 * (PAIR * PPQ * q + n) + c + 1)
                            act.activation(wvo[i][:, 0, h, c * CH:(c + 1) * CH], vo_bank[2 * h + c][:],
                                           ACT.Copy).then_inc(vo_hi, 1)

        @block.vector
        def _(dve):
            with dve.Fori(0, QUADS) as q:
                dve.wait_ge(rope_hi, q + 1)
                dve.tensor_tensor(rope[:, 1], rope_raw[:], as_f32(rope[:, 0]), ALU.subtract).then_inc(rope_lo, 1)
                for i in range(PPQ):
                    dve.wait_ge(split_hi, PPQ * q + i + 1)
                    dve.tensor_tensor(lo[i][:], raw[i][:], as_f32(hi[i][:]), ALU.subtract).then_inc(split_lo, 1)
                for i in range(PPQ):
                    for h in range(PAIR):
                        n = PAIR * i + h
                        cols = slice(h * P, (h + 1) * P)
                        dve.wait_ge(abs_hi, PAIR * PPQ * q + n + 1)
                        dve.tensor_tensor(wabs[i][:, 1, :, cols], abs_bank[h][:],
                                          as_f32(wabs[i][:, 0, :, cols]), ALU.subtract).then_inc(abs_lo, 1)
                        for c in range(2):
                            cols = slice(c * CH, (c + 1) * CH)
                            dve.wait_ge(vo_hi, 2 * (PAIR * PPQ * q + n) + c + 1)
                            dve.tensor_tensor(wvo[i][:, 1, h, cols], vo_bank[2 * h + c][:],
                                              as_f32(wvo[i][:, 0, h, cols]), ALU.subtract).then_inc(vo_lo, 1)

        @block.tensor
        def _(pe):
            with pe.Fori(0, QUADS) as q:
                for i in range(PPQ):
                    pe.wait_ge(split_lo, PPQ * q + i + 1)
                    for h in range(PAIR):
                        n = PAIR * i + h
                        if i == 0:
                            pe.wait_ge(abs_lo, PAIR * PPQ * q)
                            pe.wait_ge(vo_lo, 2 * PAIR * PPQ * q)
                        else:
                            pe.wait_ge(abs_lo, PAIR * PPQ * q + n - 1)
                            pe.wait_ge(vo_lo, 2 * (PAIR * PPQ * q + n - 1))
                        for k in range(QT):
                            ins = three_passes(pe, abs_bank[h][:, k, :],
                                               hi[i][:, h, k * P:(k + 1) * P], lo[i][:, h, k * P:(k + 1) * P],
                                               hi[i][:, h, UK:UV], lo[i][:, h, UK:UV], True, True)
                        ins.then_inc(abs_ready, 1)
                        for c in range(2):
                            cols = slice(OUT + c * CH, OUT + (c + 1) * CH)
                            ins = three_passes(pe, vo_bank[2 * h + c][:], hi[i][:, h, UV:OUT], lo[i][:, h, UV:OUT],
                                               hi[i][:, h, cols], lo[i][:, h, cols], True, True)
                            ins.then_inc(vo_ready, 1)


def attend(nc, x, tok_d, wabs_d, wvo_d, wqr_d, consts, x1_d):
    STEPS, UNITS, ROPES = 8, 4, CPG
    PARTS = 2 * PAIR
    ROPE_CHUNK = {2: 0, 4: 1}
    USE = [0, 1, 2, 5, 6, 9, 10, 11]
    ctx = ExitStack()
    with ctx:
        def sb(name, shape, dt=F32):
            return ctx.enter_context(nc.sbuf_tensor(name, shape, dt))

        def bank(name):
            return ctx.enter_context(nc.psum_tensor(name, [P, CH], F32))

        def sem(name):
            return ctx.enter_context(nc.semaphore(name))

        tok = sb("at_tok", [P, CPG, PACK], F32R)
        acc = sb("at_acc", [P, BPG, D])
        wabs = [sb(f"at_wabs{i}", [P, 2, QT, PAIR * P], F32R) for i in range(2)]
        wvo = [sb(f"at_wvo{i}", [P, 2, PAIR, D], F32R) for i in range(2)]
        wqr = sb("at_wqr", [P, 2, QT, 2, P], F32R)
        qlat = [sb(f"at_qlat{i}", [P, 2, PAIR, CH], F32R) for i in range(2)]
        qrope = [sb(f"at_qrope{c}", [P, QUAD, CH], F32R) for c in range(CPG)]
        rope_tmp = sb("at_rope_tmp", [P, 4, CH])
        rope_parts = sb("at_rope_parts", [P, 4, CH], F32R)
        probs = [sb(f"at_probs{i}", [P, PARTS, SEQ]) for i in range(2)]
        nmax = [sb(f"at_nmax{i}", [P, PARTS]) for i in range(2)]
        sums = [sb(f"at_sums{i}", [P, PARTS]) for i in range(2)]
        rsum = [sb(f"at_rsum{i}", [P, PARTS]) for i in range(2)]
        pT_hi = sb("at_pT_hi", [P, CH], F32R)
        pT_lo = sb("at_pT_lo", [P, CH], F32R)
        val_hi = [sb(f"at_val_hi{i}", [P, CH], F32R) for i in range(2)]
        val_lo = [sb(f"at_val_lo{i}", [P, CH], F32R) for i in range(2)]
        ident = sb("at_ident", [P, P])
        ident_b = sb("at_ident_b", [P, P], BF16)
        mask = sb("at_mask", [P, SEQ])
        mask_b = sb("at_mask_b", [P, SEQ], BF16)
        cos = sb("at_cos", [P, SEQ])
        sin = sb("at_sin", [P, SEQ])

        qbank = [bank(f"at_qbank{i}") for i in range(2)]
        score = [bank(f"at_score{i}") for i in range(2)]
        turned, value = bank("at_turned"), bank("at_value")
        outb = [bank(f"at_out{i}") for i in range(2)]

        const_in = sem("at_const_in")
        cq_in, key_in, kv_in, acc_in, x1_out = ([sem(f"at_{n}{c}") for c in range(CPG)]
                                                for n in ("cq_in", "key_in", "kv_in", "acc_in", "x1_out"))
        wabs_in = [sem(f"at_wabs_in{i}") for i in range(2)]
        wvo_in = [sem(f"at_wvo_in{i}") for i in range(2)]
        wqr_in = sem("at_wqr_in")
        qrope_in = [sem(f"at_qrope_in{c}") for c in range(CPG)]
        const_cast = sem("at_const_cast")
        ql_mm, ql_hi, ql_lo = sem("at_ql_mm"), sem("at_ql_hi"), sem("at_ql_lo")
        rope_mm, rope_cs, rope_sum = sem("at_rope_mm"), sem("at_rope_cs"), sem("at_rope_sum")
        rope_hi, rope_lo = sem("at_rope_hi"), sem("at_rope_lo")
        score_ready, max_ready, exp_ready = sem("at_score_ready"), sem("at_max_ready"), sem("at_exp_ready")
        rsum_ready, probs_ready = sem("at_rsum_ready"), sem("at_probs_ready")
        turn_ready, pT_hi_done, pT_lo_done = sem("at_turn_ready"), sem("at_pT_hi_done"), sem("at_pT_lo_done")
        value_ready, val_hi_done, val_lo_done = (sem(f"at_{n}") for n in ("value_ready", "val_hi_done", "val_lo_done"))
        out_ready = sem("at_out_ready")
        added = sem("at_added")

        def batch_cols(s, bl):
            b = 2 * (s % 2) + bl
            return slice(b * SEQ, (b + 1) * SEQ)

        def place(s):
            return (s // 2) // CPG % 2, (s // 2) % CPG

        x_chunks = x.rearrange("(c b p) d -> c p b d", c=CHUNKS, p=P)
        x1_chunks = x1_d.rearrange("(c b p) d -> c p b d", c=CHUNKS, p=P)
        block = ctx.enter_context(nc.Block())

        def quads(eng, opening, slot):
            opening()
            for g in range(GROUPS):
                with eng.Fori(0, QUADS - 1) as q:
                    for s in range(STEPS):
                        slot(g * QUADS + q, s, 2 * STEPS, lambda k: g)
                for s in range(STEPS):
                    slot(g * QUADS + QUADS - 1, s, 2 * STEPS if g < GROUPS - 1 else STEPS, lambda k: g + k // STEPS)

        @block.sync
        def _(sp):
            def load_wabs(i, q):
                sp.dma_start(as_f32(wabs[i][:]), wabs_d[2 * q + i]).then_inc(wabs_in[i], 16)

            def load_wvo(i, q):
                sp.dma_start(as_f32(wvo[i][:]), wvo_d[2 * q + i]).then_inc(wvo_in[i], 16)

            def load_wqr(q):
                sp.dma_start(as_f32(wqr[:]), wqr_d[q]).then_inc(wqr_in, 16)

            def load_tokens(g, c, lo, hi, done):
                sp.dma_start(as_f32(tok[:, c, lo:hi]), tok_d[CPG * g + c][:, lo:hi]).then_inc(done[c], 16)

            def load_queries(g, c):
                load_tokens(g, c, CQ_HI, KT_HI, cq_in)

            def load_keys(g, c):
                load_tokens(g, c, KT_HI, KV_HI, key_in)
                load_tokens(g, c, KR_HI, PACK, key_in)

            def load_values(g, c):
                load_tokens(g, c, KV_HI, KR_HI, kv_in)

            def load_x(g, c):
                sp.dma_start(acc[:, BPC * c:BPC * (c + 1), :], x_chunks[CPG * g + c]).then_inc(acc_in[c], 16)

            def store_x1(g, c):
                sp.dma_start(x1_chunks[CPG * g + c], acc[:, BPC * c:BPC * (c + 1), :]).then_inc(x1_out[c], 16)

            def relayout(m, c):
                sp.wait_ge(rope_lo, 2 * (ROPES * m + c + 1))
                for h in range(QUAD):
                    for j in range(4):
                        sp.dma_start(as_f32(qrope[c][j * HALF:(j + 1) * HALF, h, :]),
                                     as_f32(rope_parts[h * HALF:(h + 1) * HALF, j, :])).then_inc(qrope_in[c], 16)

            def quad(m, q1, q2, switch):
                sp.wait_ge(ql_mm, PAIR * (UNITS * m + 2))
                load_wabs(0, q1)
                if switch:
                    sp.wait_ge(ql_mm, PAIR * (UNITS * m + 3))
                    load_queries(switch, 0)
                    sp.wait_ge(score_ready, STEPS * m + 6)
                    load_keys(switch, 0)
                sp.wait_ge(ql_mm, PAIR * (UNITS * m + 4))
                load_wabs(1, q1)
                if switch:
                    load_queries(switch, 1)
                sp.wait_ge(out_ready, 4 * (STEPS * m + 4))
                load_wvo(0, q1)
                relayout(m + 1, 0)
                if switch:
                    sp.wait_ge(value_ready, STEPS * m + 6)
                    load_values(switch, 0)
                sp.wait_ge(score_ready, STEPS * m + 8)
                if q2 is not None:
                    load_wqr(q2)
                if switch:
                    load_keys(switch, 1)
                relayout(m + 1, 1)
                if switch:
                    sp.wait_ge(added, 4 * (STEPS * m + 6) + 2)
                    store_x1(switch - 1, 0)
                    sp.wait_ge(value_ready, STEPS * m + 8)
                    load_values(switch, 1)
                    sp.wait_ge(x1_out[0], 16 * switch)
                    load_x(switch, 0)
                sp.wait_ge(out_ready, 4 * STEPS * (m + 1))
                load_wvo(1, q1)
                if switch:
                    sp.wait_ge(added, 4 * (STEPS * m + 8) + 2)
                    store_x1(switch - 1, 1)
                    sp.wait_ge(x1_out[1], 16 * switch)
                    load_x(switch, 1)

            load_wqr(0)
            load_queries(0, 0)
            for to, name in ((ident, "ident"), (mask, "mask"), (cos, "cos"), (sin, "sin")):
                sp.dma_start(to[:], consts[name]).then_inc(const_in, 16)
            load_wabs(0, 0)
            load_queries(0, 1)
            load_keys(0, 0)
            relayout(0, 0)
            load_values(0, 0)
            sp.wait_ge(rope_mm, ROPES)
            load_wqr(1)
            relayout(0, 1)
            load_wvo(0, 0)
            load_x(0, 0)
            load_wabs(1, 0)
            load_keys(0, 1)
            load_values(0, 1)
            load_x(0, 1)
            load_wvo(1, 0)
            for g in range(GROUPS):
                more = g < GROUPS - 1
                with sp.Fori(0, QUADS - 2) as q:
                    quad(g * QUADS + q, q + 1, q + 2, None)
                quad(g * QUADS + QUADS - 2, QUADS - 1, 0 if more else None, None)
                if more:
                    quad(g * QUADS + QUADS - 1, 0, 1, g + 1)
            for c in range(CPG):
                sp.wait_ge(added, 4 * (STEPS * (GROUPS * QUADS - 1) + 6 + 2 * c) + 2)
                store_x1(GROUPS - 1, c)
            for c in range(CPG):
                sp.wait_ge(x1_out[c], 16 * GROUPS)

        @block.tensor
        def _(pe):
            pe.wait_ge(const_cast, 2)

            def latent(m, u, h, g, n, ropes, latents):
                pair, c = place(2 * u)
                if h == 0:
                    pe.wait_ge(cq_in[c], 16 * (g + 1))
                    pe.wait_ge(wabs_in[pair], 16 * (m + u // UNITS + 1))
                pe.wait_ge(rope_cs, ropes)
                if latents is not None:
                    pe.wait_ge(ql_lo, latents)
                cols = slice(h * P, (h + 1) * P)
                for k in range(QT):
                    ins = three_passes(pe, qbank[n % 2][:], wabs[pair][:, 0, k, cols], wabs[pair][:, 1, k, cols],
                                       tok[:, c, CQ_HI + k * CH:CQ_HI + (k + 1) * CH],
                                       tok[:, c, CQ_LO + k * CH:CQ_LO + (k + 1) * CH], k == 0, k == QT - 1)
                ins.then_inc(ql_mm, 1)

            def rope(m, c, g, n, ropes, latents):
                pe.wait_ge(cq_in[c], 16 * (g + 1))
                pe.wait_ge(wqr_in, 16 * (m + 1))
                if ropes is not None:
                    pe.wait_ge(rope_cs, ropes)
                if latents is not None:
                    pe.wait_ge(ql_lo, latents)
                for half in range(2):
                    for k in range(QT):
                        ins = three_passes(pe, qbank[(n + half) % 2][:], wqr[:, 0, k, half], wqr[:, 1, k, half],
                                           tok[:, c, CQ_HI + k * CH:CQ_HI + (k + 1) * CH],
                                           tok[:, c, CQ_LO + k * CH:CQ_LO + (k + 1) * CH], k == 0, k == QT - 1)
                ins.then_inc(rope_mm, 1)

            def scores(m, s, g):
                pair, c = place(s)
                u = s // 2
                pe.wait_ge(ql_lo, PAIR * (UNITS * m + u + 1))
                if pair == 0 and s % 2 == 0:
                    pe.wait_ge(key_in[c], 2 * 16 * (g + 1))
                    pe.wait_ge(qrope_in[c], 16 * 16 * (m + s // STEPS + 1))
                sc = score[s % 2]
                pe.matmul(sc[:], ident_b[:], mask_b[:].unsqueeze(1).to_broadcast([P, PARTS, SEQ]),
                          start=True, stop=False)
                for bl in range(2):
                    cols = batch_cols(s, bl)

                    def key(part):
                        return tok[:, c, part + cols.start:part + cols.stop]

                    for h in range(PAIR):
                        j = bl * PAIR + h
                        out = sc[:, j * SEQ:(j + 1) * SEQ]
                        last = j == PARTS - 1
                        q_hi, q_lo = (qlat[u % 2][:, i, h, cols] for i in range(2))
                        q_rope = qrope[c][:, pair * PAIR + h, cols]
                        pe.matmul(out, q_hi, key(KT_HI), start=False, stop=False)
                        pe.matmul(out, q_hi, key(KT_LO), start=False, stop=False)
                        pe.matmul(out, q_lo, key(KT_HI), start=False, stop=False)
                        pe.matmul(out, q_rope, key(KR_HI), start=False, stop=False)
                        ins = pe.matmul(out, q_rope, key(KR_LO), start=False, stop=last)
                ins.then_inc(score_ready, 1)

            def turn(m, s):
                pe.wait_ge(probs_ready, STEPS * m + s + 1)
                for j in range(PARTS):
                    ins = pe.transpose(turned[:, j * SEQ:(j + 1) * SEQ], probs[s % 2][:, j, :], ident[:])
                ins.then_inc(turn_ready, 1)

            def values(m, s, g):
                _, c = place(s)
                pe.wait_ge(kv_in[c], 16 * (g + 1))
                pe.wait_ge(pT_lo_done, STEPS * m + s + 1)
                for bl in range(2):
                    cols = batch_cols(s, bl)
                    at = slice(bl * PAIR * SEQ, (bl + 1) * PAIR * SEQ)
                    ins = three_passes(pe, value[:, at], tok[:, c, KV_HI + cols.start:KV_HI + cols.stop],
                                       tok[:, c, KV_LO + cols.start:KV_LO + cols.stop],
                                       pT_hi[:, at], pT_lo[:, at], True, True)
                ins.then_inc(value_ready, 1)

            def output(m, s, bl):
                pair, _ = place(s)
                if bl == 0:
                    pe.wait_ge(val_lo_done, STEPS * m + s + 1)
                    pe.wait_ge(wvo_in[pair], 16 * (m + 1))
                for n in range(2):
                    pe.wait_ge(added, 4 * (STEPS * m + s) + 2 * bl + n + 1)
                    for h in range(PAIR):
                        at = slice((bl * PAIR + h) * SEQ, (bl * PAIR + h + 1) * SEQ)
                        cols = slice(n * CH, (n + 1) * CH)
                        ins = three_passes(pe, outb[n][:], val_hi[s % 2][:, at], val_lo[s % 2][:, at],
                                           wvo[pair][:, 0, h, cols], wvo[pair][:, 1, h, cols],
                                           h == 0, h == PAIR - 1)
                    ins.then_inc(out_ready, 1)

            def opening():
                rope(0, 0, 0, 0, None, None)
                for u in range(2):
                    for h in range(PAIR):
                        n = PAIR * u + h
                        latent(0, u, h, 0, n, 1, n - 1 if n > 1 else None)
                rope(0, 1, 0, 0, 1, 2 * PAIR)
                scores(0, 0, 0)
                scores(0, 1, 0)
                turn(0, 0)
                values(0, 0, 0)

            def slot(m, s, end, of):
                if s + 1 < end:
                    turn(m, s + 1)
                if s + 2 < end:
                    scores(m, s + 2, of(s + 2))
                output(m, s, 0)
                u = s // 2 + 2
                latents = PAIR * (UNITS * m + u) + s % 2
                more = end > STEPS
                if u < end // 2:
                    ropes = ROPES * (m + 1) + (sum(t < s for t in ROPE_CHUNK) if more else 0)
                    latent(m, u, s % 2, of(2 * u), USE[s], ropes, latents)
                if s + 1 < end:
                    values(m, s + 1, of(s + 1))
                output(m, s, 1)
                if s in ROPE_CHUNK and more:
                    c = ROPE_CHUNK[s]
                    rope(m + 1, c, of(STEPS), USE[s] + 1, ROPES * (m + 1) + c, latents + 1)

            quads(pe, opening, slot)

        @block.scalar
        def _(act):
            act.wait_ge(const_in, 64)
            act.activation(ident_b[:], ident[:], ACT.Copy).then_inc(const_cast, 1)
            act.activation(mask_b[:], mask[:], ACT.Copy).then_inc(const_cast, 1)

            def latent(m, u, h, n):
                act.wait_ge(ql_mm, PAIR * (UNITS * m + u) + h + 1)
                act.activation(qlat[u % 2][:, 0, h, :], qbank[n % 2][:], ACT.Copy).then_inc(ql_hi, 1)

            def rope(m, c, moved):
                at = ROPES * m + c
                if moved is not None:
                    act.wait_ge(qrope_in[1 - c], moved)
                for half in range(2):
                    act.wait_ge(rope_sum, 2 * at + half + 1)
                    act.activation(rope_parts[:, half, :], rope_tmp[:, 2 * half, :], ACT.Copy).then_inc(rope_hi, 1)

            def exps(m, s):
                i = s % 2
                act.wait_ge(max_ready, STEPS * m + s + 1)
                for j in range(PARTS):
                    ins = act.activation(probs[i][:, j, :], score[i][:, j * SEQ:(j + 1) * SEQ], ACT.Exp,
                                         bias=nmax[i][:, j:j + 1], accum_out=sums[i][:, j:j + 1])
                ins.then_inc(exp_ready, 1)

            def turn(m, s):
                act.wait_ge(turn_ready, STEPS * m + s + 1)
                act.activation(pT_hi[:], turned[:], ACT.Copy).then_inc(pT_hi_done, 1)

            def values(m, s):
                act.wait_ge(value_ready, STEPS * m + s + 1)
                act.activation(val_hi[s % 2][:], value[:], ACT.Copy).then_inc(val_hi_done, 1)

            def opening():
                rope(0, 0, None)
                for u in range(2):
                    for h in range(PAIR):
                        latent(0, u, h, PAIR * u + h)
                rope(0, 1, 256)
                exps(0, 0)
                exps(0, 1)
                turn(0, 0)
                values(0, 0)

            def slot(m, s, end, of):
                if s + 1 < end:
                    turn(m, s + 1)
                if s + 2 < end:
                    exps(m, s + 2)
                if s // 2 + 2 < end // 2:
                    latent(m, s // 2 + 2, s % 2, USE[s])
                if s + 1 < end:
                    values(m, s + 1)
                if s - 1 in ROPE_CHUNK and end > STEPS:
                    c = ROPE_CHUNK[s - 1]
                    rope(m + 1, c, 256 * (m + 1 + c))

            quads(act, opening, slot)

        @block.gpsimd
        def _(pool):
            def normalise(m, s):
                i = s % 2
                pool.wait_ge(rsum_ready, STEPS * m + s + 1)
                pool.tensor_tensor(probs[i][:], probs[i][:], rsum[i][:].unsqueeze(2).to_broadcast([P, PARTS, SEQ]),
                                   ALU.mult).then_inc(probs_ready, 1)

            def rope_sums(m, c):
                at = ROPES * m + c
                pool.wait_ge(rope_cs, at + 1)
                for half, op in ((0, ALU.subtract), (1, ALU.add)):
                    pool.tensor_tensor(rope_tmp[:, 2 * half, :], rope_tmp[:, 2 * half, :],
                                       rope_tmp[:, 2 * half + 1, :], op).then_inc(rope_sum, 1)

            def rope_low(m, c):
                at = ROPES * m + c
                for half in range(2):
                    pool.wait_ge(rope_hi, 2 * at + half + 1)
                    pool.tensor_tensor(rope_parts[:, 2 + half, :], rope_tmp[:, 2 * half, :],
                                       as_f32(rope_parts[:, half, :]), ALU.subtract).then_inc(rope_lo, 1)

            def opening():
                for c in range(ROPES):
                    rope_sums(0, c)
                    rope_low(0, c)
                normalise(0, 0)
                normalise(0, 1)

            def slot(m, s, end, of):
                finish = s - 1 in ROPE_CHUNK and end > STEPS
                if finish:
                    rope_sums(m + 1, ROPE_CHUNK[s - 1])
                if s + 2 < end:
                    normalise(m, s + 2)
                if finish:
                    rope_low(m + 1, ROPE_CHUNK[s - 1])

            quads(pool, opening, slot)

        @block.vector
        def _(dve):
            dve.sem_inc(added, 2)
            dve.wait_ge(const_in, 64)

            def latent(m, u, h, n):
                dve.wait_ge(ql_hi, PAIR * (UNITS * m + u) + h + 1)
                dve.tensor_tensor(qlat[u % 2][:, 1, h, :], qbank[n % 2][:], as_f32(qlat[u % 2][:, 0, h, :]),
                                  ALU.subtract).then_inc(ql_lo, 1)

            def rope(m, c, n, used):
                dve.wait_ge(rope_mm, ROPES * m + c + 1)
                if used is not None:
                    dve.wait_ge(rope_lo, used)

                def times(out, half, table):
                    return dve.tensor_tensor(rope_tmp[:, out, :].rearrange("p (b s) -> p b s", b=BPC),
                                             qbank[(n + half) % 2][:].rearrange("p (b s) -> p b s", b=BPC),
                                             table[:].unsqueeze(1).to_broadcast([P, BPC, SEQ]), ALU.mult)

                times(0, 0, cos)
                times(1, 1, sin)
                times(2, 0, sin)
                times(3, 1, cos).then_inc(rope_cs, 1)

            def largest(m, s):
                i = s % 2
                dve.wait_ge(score_ready, STEPS * m + s + 1)
                dve.tensor_reduce(nmax[i][:], score[i][:].rearrange("p (j t) -> p j t", j=PARTS), AX_X, ALU.max,
                                  negate=True).then_inc(max_ready, 1)

            def recip(m, s):
                i = s % 2
                dve.wait_ge(exp_ready, STEPS * m + s + 1)
                dve.reciprocal(rsum[i][:], sums[i][:]).then_inc(rsum_ready, 1)

            def turn(m, s):
                dve.wait_ge(pT_hi_done, STEPS * m + s + 1)
                dve.tensor_tensor(pT_lo[:], turned[:], as_f32(pT_hi[:]), ALU.subtract).then_inc(pT_lo_done, 1)

            def values(m, s):
                dve.wait_ge(val_hi_done, STEPS * m + s + 1)
                dve.tensor_tensor(val_lo[s % 2][:], value[:], as_f32(val_hi[s % 2][:]),
                                  ALU.subtract).then_inc(val_lo_done, 1)

            def add(m, s, bl, n, g):
                _, c = place(s)
                if bl == 0 and n == 0:
                    dve.wait_ge(acc_in[c], 16 * (g + 1))
                at = acc[:, BPC * c + 2 * (s % 2) + bl, n * CH:(n + 1) * CH]
                dve.wait_ge(out_ready, 4 * (STEPS * m + s) + 2 * bl + n + 1)
                dve.tensor_tensor(at, outb[n][:], at, ALU.add).then_inc(added, 1)

            def opening():
                rope(0, 0, 0, None)
                for u in range(2):
                    for h in range(PAIR):
                        latent(0, u, h, PAIR * u + h)
                rope(0, 1, 0, 2)
                largest(0, 0)
                largest(0, 1)
                recip(0, 0)
                recip(0, 1)
                turn(0, 0)
                values(0, 0)

            def slot(m, s, end, of):
                if s + 1 < end:
                    turn(m, s + 1)
                if s + 2 < end:
                    largest(m, s + 2)
                add(m, s, 0, 0, of(s))
                if s + 2 < end:
                    recip(m, s + 2)
                add(m, s, 0, 1, of(s))
                if s // 2 + 2 < end // 2:
                    latent(m, s // 2 + 2, s % 2, USE[s])
                if s + 1 < end:
                    values(m, s + 1)
                add(m, s, 1, 0, of(s))
                add(m, s, 1, 1, of(s))
                if s in ROPE_CHUNK and end > STEPS:
                    c = ROPE_CHUNK[s]
                    rope(m + 1, c, USE[s] + 1, 2 * (ROPES * (m + 1) + c))

            quads(dve, opening, slot)


def cross(nc, x1_d, context, consts, x2_d):
    SETS = 4
    ctx = ExitStack()
    with ctx:
        def sb(name, shape, dt=F32):
            return ctx.enter_context(nc.sbuf_tensor(name, shape, dt))

        def many(n, name, shape, dt=F32):
            return [sb(f"{name}{i}", shape, dt) for i in range(n)]

        def banks(name, n=2):
            return [ctx.enter_context(nc.psum_tensor(f"{name}{i}", [P, CH], F32)) for i in range(n)]

        def sem(name):
            return ctx.enter_context(nc.semaphore(name))

        CUT = ((D, 2 * D), (0, D))
        xt = many(SETS, "cr_x", [P, D])
        ctx_raw = many(2, "cr_ctx_raw", [P, 2 * D])
        ctx_hi = many(SETS, "cr_ctx_hi", [P, 2 * D], F32R)
        ctx_lo = many(SETS, "cr_ctx_lo", [P, 2 * D], F32R)
        hn = many(2, "cr_hn", [P, D])
        qT_hi = many(2, "cr_qT_hi", [P, KT, P], F32R)
        qT_lo = many(2, "cr_qT_lo", [P, KT, P], F32R)
        probs = many(2, "cr_probs", [P, SEQ])
        pT_hi = many(2, "cr_pT_hi", [P, SEQ], F32R)
        pT_lo = many(2, "cr_pT_lo", [P, SEQ], F32R)
        stats = many(2, "cr_stats", [P, 2, 6])
        mv = many(2, "cr_mv", [P, 2])
        var = many(2, "cr_var", [P, 1])
        rstd = many(2, "cr_rstd", [P, 1])
        nmax = many(2, "cr_nmax", [P, 1])
        total = many(2, "cr_total", [P, 1])
        rtotal = many(2, "cr_rtotal", [P, 1])
        power = sb("cr_power", [P, 1])
        ident = sb("cr_ident", [P, P])
        turned, score, out = banks("cr_turned"), banks("cr_score"), banks("cr_out")
        pT = banks("cr_pT", 1)[0]

        const_in, power_set = sem("cr_const_in"), sem("cr_power_set")
        x_in = [sem(f"cr_x_in{i}") for i in range(SETS)]
        c_in = [sem(f"cr_c_in{i}") for i in range(2)]
        x2_out = [sem(f"cr_x2_out{i}") for i in range(SETS)]
        names = ("mv_done", "var_done", "rstd_done", "hn_ready", "turn_ready", "turn_hi", "turn_lo",
                 "ctx_hi_done", "ctx_lo_done", "score_ready", "max_ready", "exp_ready", "rtotal_ready", "pT_ready",
                 "pT_hi_done", "pT_lo_done", "out_ready")
        s = {n: sem(f"cr_{n}") for n in names}
        summed = sem("cr_summed")
        x1_b = x1_d.rearrange("(b p) d -> b p d", p=P)
        x2_b = x2_d.rearrange("(b p) d -> b p d", p=P)
        block = ctx.enter_context(nc.Block())

        def batches(eng, opening, turn):
            opening()
            with eng.Fori(0, BATCHES // SETS - 1) as n:
                for i in range(SETS):
                    turn(SETS * n + i, i, n, SETS)
            for i in range(SETS):
                turn(BATCHES - SETS + i, i, BATCHES // SETS - 1, SETS - 1 - i)

        @block.sync
        def _(sp):
            sp.sem_inc(x2_out[SETS - 1], 16)

            def load_x(b, i):
                sp.dma_start(xt[i][:], x1_b[b]).then_inc(x_in[i], 16)

            def load_context(b, i):
                sp.dma_start(ctx_raw[i][:], context[b]).then_inc(c_in[i], 16)

            def opening():
                load_x(0, 0)
                load_context(0, 0)
                sp.dma_start(ident[:], consts["ident"]).then_inc(const_in, 16)
                for b in range(1, SETS):
                    if b < SETS - 1:
                        load_x(b, b)
                    if b < 2:
                        load_context(b, b)
                for b in range(2, SETS):
                    sp.wait_ge(s["ctx_lo_done"], 2 * (b - 1))
                    load_context(b, b % 2)

            def turn(b, i, n, follow):
                if follow >= SETS - 1:
                    sp.wait_ge(x2_out[(i - 1) % SETS], 16 * (n + 1))
                    load_x(b + SETS - 1, (i - 1) % SETS)
                sp.wait_ge(summed, 2 * (b + 1) + 2)
                sp.dma_start(x2_b[b], xt[i][:]).then_inc(x2_out[i], 16)
                if follow >= SETS:
                    sp.wait_ge(s["ctx_lo_done"], 2 * (b + 3))
                    load_context(b + SETS, i % 2)

            batches(sp, opening, turn)
            for i in range(SETS):
                sp.wait_ge(x2_out[i], 16 * (BATCHES // SETS) + (16 if i == SETS - 1 else 0))

        @block.gpsimd
        def _(pool):
            pool.memset(power[:], -0.5).then_inc(power_set, 1)
            pool.wait_ge(power_set, 1)

            def prepare(b, i):
                pool.wait_ge(s["var_done"], b + 1)
                pool.tensor_tensor(rstd[i % 2][:], var[i % 2][:], power[:], ALU.pow).then_inc(s["rstd_done"], 1)
                for part, (lo, hi) in enumerate(CUT):
                    pool.wait_ge(s["ctx_hi_done"], 2 * b + part + 1)
                    pool.tensor_tensor(ctx_lo[i][:, lo:hi], ctx_raw[i % 2][:, lo:hi], as_f32(ctx_hi[i][:, lo:hi]),
                                       ALU.subtract).then_inc(s["ctx_lo_done"], 1)

            def opening():
                prepare(0, 0)
                prepare(1, 1)

            def turn(b, i, n, follow):
                if follow >= 2:
                    prepare(b + 2, (i + 2) % SETS)

            batches(pool, opening, turn)

        @block.scalar
        def _(act):
            def cut(b, i, n):
                act.wait_ge(c_in[i % 2], 16 * n)
                for lo, hi in CUT:
                    act.activation(ctx_hi[i][:, lo:hi], ctx_raw[i % 2][:, lo:hi],
                                   ACT.Copy).then_inc(s["ctx_hi_done"], 1)

            def turn_hi(b, i):
                for half in range(2):
                    act.wait_ge(s["turn_ready"], 2 * b + half + 1)
                    act.activation(qT_hi[i][:, half * 4:half * 4 + 4, :],
                                   turned[half][:].rearrange("p (k s) -> p k s", k=4), ACT.Copy).then_inc(s["turn_hi"], 1)

            def opening():
                cut(0, 0, 1)
                turn_hi(0, 0)
                cut(1, 1, 1)

            def turn(b, i, n, follow):
                act.wait_ge(s["max_ready"], b + 1)
                act.activation(probs[i % 2][:], score[i % 2][:, 0:SEQ], ACT.Exp, bias=nmax[i % 2][:, 0:1],
                               accum_out=total[i % 2][:, 0:1]).then_inc(s["exp_ready"], 1)
                if follow >= 1:
                    turn_hi(b + 1, (i + 1) % 2)
                act.wait_ge(s["pT_ready"], b + 1)
                act.activation(pT_hi[i % 2][:], pT[:, 0:SEQ], ACT.Copy).then_inc(s["pT_hi_done"], 1)
                if follow >= 2:
                    cut(b + 2, (i + 2) % SETS, 2 * n + i // 2 + 2)

            batches(act, opening, turn)

        @block.vector
        def _(dve):
            dve.sem_inc(summed, 2)

            def moments(b, i, n):
                dve.wait_ge(x_in[i], 16 * n)
                for h in range(2):
                    dve.bn_stats(stats[i % 2][:, h, :], xt[i][:, h * 512:(h + 1) * 512])
                dve.drain()
                dve.bn_aggr(mv[i % 2][:], stats[i % 2][:].rearrange("p h s -> p (h s)")).then_inc(s["mv_done"], 1)
                dve.wait_ge(s["mv_done"], b + 1)
                dve.tensor_scalar(var[i % 2][:], mv[i % 2][:, 1:2], EPS, None, ALU.add).then_inc(s["var_done"], 1)

            def normalise(b, i):
                dve.wait_ge(s["rstd_done"], b + 1)
                dve.tensor_scalar(hn[i % 2][:], xt[i][:], mv[i % 2][:, 0:1], rstd[i % 2][:, 0:1],
                                  ALU.subtract, ALU.mult).then_inc(s["hn_ready"], 1)

            def turn_lo(b, i):
                for half in range(2):
                    ks = slice(half * 4, half * 4 + 4)
                    dve.wait_ge(s["turn_hi"], 2 * b + half + 1)
                    dve.tensor_tensor(qT_lo[i][:, ks, :], turned[half][:].rearrange("p (k s) -> p k s", k=4),
                                      as_f32(qT_hi[i][:, ks, :]), ALU.subtract).then_inc(s["turn_lo"], 1)

            def largest(b, i):
                dve.wait_ge(s["score_ready"], b + 1)
                dve.tensor_reduce(nmax[i][:], score[i][:, 0:SEQ], AX_X, ALU.max, negate=True).then_inc(s["max_ready"], 1)

            def opening():
                moments(0, 0, 1)
                normalise(0, 0)
                moments(1, 1, 1)
                turn_lo(0, 0)
                normalise(1, 1)
                largest(0, 0)

            def turn(b, i, n, follow):
                if follow >= 1:
                    turn_lo(b + 1, (i + 1) % 2)
                dve.wait_ge(s["pT_hi_done"], b + 1)
                dve.tensor_tensor(pT_lo[i % 2][:], pT[:, 0:SEQ], as_f32(pT_hi[i % 2][:]),
                                  ALU.subtract).then_inc(s["pT_lo_done"], 1)
                dve.wait_ge(s["exp_ready"], b + 1)
                dve.reciprocal(rtotal[i % 2][:], total[i % 2][:]).then_inc(s["rtotal_ready"], 1)
                if follow >= 2:
                    moments(b + 2, (i + 2) % SETS, n + (i + 2) // SETS + 1)
                if follow >= 1:
                    largest(b + 1, (i + 1) % 2)
                if follow >= 2:
                    normalise(b + 2, (i + 2) % SETS)
                dve.wait_ge(s["rtotal_ready"], b + 1)
                for c in range(2):
                    cols = slice(c * CH, (c + 1) * CH)
                    dve.wait_ge(s["out_ready"], 2 * b + c + 1)
                    dve.scalar_tensor_tensor(out=xt[i][:, cols], in0=out[c][:], scalar=rtotal[i % 2][:, 0:1],
                                             in1=xt[i][:, cols], op0=ALU.mult, op1=ALU.add).then_inc(summed, 1)

            batches(dve, opening, turn)

        @block.tensor
        def _(pe):
            pe.wait_ge(const_in, 16)

            def turn_hn(b, i, free):
                pe.wait_ge(s["hn_ready"], b + 1)
                for half in range(2):
                    if free is not None:
                        pe.wait_ge(s["turn_lo"], free + half)
                    for j in range(4):
                        k = half * 4 + j
                        ins = pe.transpose(turned[half][:, j * P:(j + 1) * P], hn[i][:, k * P:(k + 1) * P], ident[:])
                    ins.then_inc(s["turn_ready"], 1)

            def scores(b, i):
                pe.wait_ge(s["turn_lo"], 2 * (b + 1))
                pe.wait_ge(s["ctx_lo_done"], 2 * b + 1)
                for k in range(KT):
                    cols = slice(D + k * P, D + (k + 1) * P)
                    ins = three_passes(pe, score[i % 2][:, 0:SEQ], qT_hi[i % 2][:, k, :], qT_lo[i % 2][:, k, :],
                                       ctx_hi[i][:, cols], ctx_lo[i][:, cols], k == 0, k == KT - 1)
                ins.then_inc(s["score_ready"], 1)

            def opening():
                turn_hn(0, 0, None)
                scores(0, 0)

            def turn(b, i, n, follow):
                if follow >= 1:
                    turn_hn(b + 1, (i + 1) % 2, 2 * b + 1)
                pe.wait_ge(s["exp_ready"], b + 1)
                pe.transpose(pT[:, 0:SEQ], probs[i % 2][:], ident[:]).then_inc(s["pT_ready"], 1)
                if follow >= 1:
                    scores(b + 1, (i + 1) % SETS)
                pe.wait_ge(s["pT_lo_done"], b + 1)
                pe.wait_ge(s["ctx_lo_done"], 2 * (b + 1))
                for c in range(2):
                    cols = slice(c * CH, (c + 1) * CH)
                    pe.wait_ge(summed, 2 * b + c + 1)
                    three_passes(pe, out[c][:], pT_hi[i % 2][:], pT_lo[i % 2][:], ctx_hi[i][:, cols],
                                 ctx_lo[i][:, cols], True, True).then_inc(s["out_ready"], 1)

            batches(pe, opening, turn)


def feed(nc, x2_d, signs, scales, consts, out_d):
    LAYERS = 3
    HID = 2 * KT
    ctx = ExitStack()
    with ctx:
        def sb(name, shape, dt=F32):
            return ctx.enter_context(nc.sbuf_tensor(name, shape, dt))

        def banks(name, n=2):
            return [ctx.enter_context(nc.psum_tensor(f"{name}{i}", [P, CH], F32)) for i in range(n)]

        def sem(name):
            return ctx.enter_context(nc.semaphore(name))

        w = [sb(f"ff_w{l}", [P, KT, D], F32R) for l in range(LAYERS)]
        xt = [sb(f"ff_x{i}", [P, BPC, D]) for i in range(2)]
        hn = sb("ff_hn", [P, 2, D])
        act_hi = [sb(f"ff_act_hi{i}", [P, KT, CH], F32R) for i in range(2)]
        act_lo = [sb(f"ff_act_lo{i}", [P, KT, CH], F32R) for i in range(2)]
        hid = sb("ff_hid", [P, 2, CH])
        stats = sb("ff_stats", [P, BPC, 2, 6])
        mv = sb("ff_mv", [P, BPC, 2])
        var = sb("ff_var", [P, BPC])
        rstd = sb("ff_rstd", [P, BPC])
        power = sb("ff_power", [P, BPC])
        ident = sb("ff_ident", [P, P])
        sign_mul = sb("ff_sign_mul", [P, KT])
        sign_add = sb("ff_sign_add", [P, KT])
        scale = sb("ff_scale", [P, LAYERS])
        scale2 = sb("ff_scale2", [P, LAYERS])
        bit_words = xt[1][:].rearrange("p b d -> p (b d)").bitcast(I32).rearrange("p (l k m) -> p l k m", l=2, k=KT)
        bits = xt[1][:].rearrange("p b d -> p (b d)").bitcast(U8).rearrange("p (l k m) -> p l k m", l=2, k=KT)

        turned, lin, outb = banks("ff_turned"), banks("ff_lin"), banks("ff_out")
        const_in, power_set = sem("ff_const_in"), sem("ff_power_set")
        bits_in = [sem(f"ff_bits_in{l}") for l in range(LAYERS)]
        w_ready = [sem(f"ff_w_ready{l}") for l in range(LAYERS)]
        x_in = [sem(f"ff_x_in{i}") for i in range(2)]
        y_out = [sem(f"ff_y_out{i}") for i in range(2)]
        names = ("scale2_ready", "mv_done", "var_done", "rstd_done", "hn_ready", "turn_ready", "turn_hi",
                 "turn_lo", "lin_ready", "relu_done", "hid_hi", "hid_lo", "out_ready", "summed")
        s = {n: sem(f"ff_{n}") for n in names}
        x2_c = x2_d.rearrange("(c b p) d -> c p b d", c=CHUNKS, p=P)
        out_c = out_d.rearrange("(c b p) d -> c p b d", c=CHUNKS, p=P)
        block = ctx.enter_context(nc.Block())

        def chunks(eng, body):
            with eng.Fori(0, CHUNKS // 2 - 1) as n:
                body(2 * n, 0, n, False)
                body(2 * n + 1, 1, n + 1, False)
            body(CHUNKS - 2, 0, CHUNKS // 2 - 1, False)
            body(CHUNKS - 1, 1, 0, True)

        @block.sync
        def _(sp):
            sp.dma_start(xt[0][:], x2_c[0]).then_inc(x_in[0], 16)
            for to, name in ((ident, "ident"), (sign_mul, "sign_mul"), (sign_add, "sign_add")):
                sp.dma_start(to[:], consts[name]).then_inc(const_in, 16)
            sp.dma_start(scale[:], scales).then_inc(const_in, 16)
            for l in range(2):
                sp.dma_start(bit_words[:, l], signs[l]).then_inc(bits_in[l], 16)
            sp.wait_ge(w_ready[0], 1)
            sp.dma_start(bit_words[:, 0], signs[2]).then_inc(bits_in[2], 16)
            for l in range(1, LAYERS):
                sp.wait_ge(w_ready[l], 1)
            sp.dma_start(xt[1][:], x2_c[1]).then_inc(x_in[1], 16)

            def store(c, i):
                sp.wait_ge(s["summed"], 2 * BPC * (c + 1))
                sp.dma_start(out_c[c], xt[i][:]).then_inc(y_out[i], 16)

            with sp.Fori(0, CHUNKS // 2 - 1) as n:
                for i in range(2):
                    store(2 * n + i, i)
                    sp.wait_ge(y_out[i], 16 * (n + 1))
                    sp.dma_start(xt[i][:], x2_c[2 * n + 2 + i]).then_inc(x_in[i], 16)
            for i in range(2):
                store(CHUNKS - 2 + i, i)
            for i in range(2):
                sp.wait_ge(y_out[i], 16 * (CHUNKS // 2))

        @block.gpsimd
        def _(pool):
            pool.memset(power[:], -0.5).then_inc(power_set, 1)
            pool.wait_ge(power_set, 1)

            def root(c):
                pool.wait_ge(s["var_done"], c + 1)
                pool.tensor_tensor(rstd[:], var[:], power[:], ALU.pow).then_inc(s["rstd_done"], 1)

            root(0)
            pool.wait_ge(const_in, 64)
            pool.wait_ge(bits_in[2], 16)
            for k in range(KT):
                ins = pool.tensor_scalar(w[2][:, k, :], bits[:, 0, k, :], sign_mul[:, k:k + 1], sign_add[:, k:k + 1],
                                         ALU.mult, ALU.add)
            ins.then_inc(w_ready[2], 1)
            chunks(pool, lambda c, i, n_next, last: None if last else root(c + 1))

        @block.scalar
        def _(act):
            def turn(c, i, t):
                for half in range(2):
                    act.wait_ge(s["turn_ready"], 2 * BPC * c + 2 * t + half + 1)
                    act.activation(act_hi[i][:, half * 4:half * 4 + 4, t * P:(t + 1) * P],
                                   turned[half][:].rearrange("p (k s) -> p k s", k=4), ACT.Copy).then_inc(s["turn_hi"], 1)

            def hidden(c, i, layer):
                to = act_hi[1 - i] if layer == 0 else act_hi[i]
                for m in range(KT):
                    a = HID * c + KT * layer + m
                    act.wait_ge(s["lin_ready"], a + 1)
                    if layer or m >= 2:
                        act.wait_ge(s["hid_lo"], a - 1)
                    act.activation(hid[:, m % 2, :], lin[m % 2][:], ACT.Relu,
                                   scale=scale2[:, layer:layer + 1]).then_inc(s["relu_done"], 1)
                    act.wait_ge(s["relu_done"], a + 1)
                    act.activation(to[:, m, :], hid[:, m % 2, :], ACT.Copy).then_inc(s["hid_hi"], 1)

            def body(c, i, n_next, last):
                hidden(c, i, 0)
                hidden(c, i, 1)
                if not last:
                    for t in range(BPC):
                        turn(c + 1, 1 - i, t)

            act.wait_ge(const_in, 64)
            act.wait_ge(bits_in[1], 16)
            for k in range(KT):
                ins = act.activation(w[1][:, k, :], bits[:, 1, k, :], ACT.Identity, scale=sign_mul[:, k:k + 1],
                                     bias=sign_add[:, k:k + 1])
            ins.then_inc(w_ready[1], 1)
            act.wait_ge(s["scale2_ready"], 1)
            for t in range(BPC):
                turn(0, 0, t)
            chunks(act, body)

        @block.vector
        def _(dve):
            def moments(c, i, n):
                dve.wait_ge(x_in[i], 16 * (n + 1))
                for t in range(BPC):
                    for h in range(2):
                        dve.bn_stats(stats[:, t, h, :], xt[i][:, t, h * 512:(h + 1) * 512])
                dve.drain()
                for t in range(BPC):
                    ins = dve.bn_aggr(mv[:, t, :], stats[:, t].rearrange("p h s -> p (h s)"))
                ins.then_inc(s["mv_done"], 1)
                dve.wait_ge(s["mv_done"], c + 1)
                dve.tensor_scalar(var[:], mv[:, :, 1], EPS, None, ALU.add).then_inc(s["var_done"], 1)

            def normalise(c, i, t):
                if t == 0:
                    dve.wait_ge(s["rstd_done"], c + 1)
                dve.tensor_scalar(hn[:, t % 2, :], xt[i][:, t, :], mv[:, t, 0:1], rstd[:, t:t + 1],
                                  ALU.subtract, ALU.mult).then_inc(s["hn_ready"], 1)

            def turn(c, i, t):
                for half in range(2):
                    at = (slice(None), slice(half * 4, half * 4 + 4), slice(t * P, (t + 1) * P))
                    dve.wait_ge(s["turn_hi"], 2 * BPC * c + 2 * t + half + 1)
                    dve.tensor_tensor(act_lo[i][at], turned[half][:].rearrange("p (k s) -> p k s", k=4),
                                      as_f32(act_hi[i][at]), ALU.subtract).then_inc(s["turn_lo"], 1)

            def hidden(c, i, layer):
                at = 1 - i if layer == 0 else i
                for m in range(KT):
                    dve.wait_ge(s["hid_hi"], HID * c + KT * layer + m + 1)
                    dve.tensor_tensor(act_lo[at][:, m, :], hid[:, m % 2, :], as_f32(act_hi[at][:, m, :]),
                                      ALU.subtract).then_inc(s["hid_lo"], 1)

            def body(c, i, n_next, last):
                hidden(c, i, 0)
                if not last:
                    moments(c + 1, 1 - i, n_next)
                    normalise(c + 1, 1 - i, 0)
                    normalise(c + 1, 1 - i, 1)
                hidden(c, i, 1)
                for t in range(BPC):
                    for n in range(2):
                        cols = slice(n * CH, (n + 1) * CH)
                        dve.wait_ge(s["out_ready"], 2 * BPC * c + 2 * t + n + 1)
                        dve.scalar_tensor_tensor(out=xt[i][:, t, cols], in0=outb[n][:], scalar=scale[:, 2:3],
                                                 in1=xt[i][:, t, cols], op0=ALU.mult, op1=ALU.add).then_inc(s["summed"], 1)
                    if not last:
                        turn(c + 1, 1 - i, t)
                        if t + 2 < BPC:
                            normalise(c + 1, 1 - i, t + 2)

            moments(0, 0, 0)
            normalise(0, 0, 0)
            normalise(0, 0, 1)
            dve.wait_ge(const_in, 64)
            dve.tensor_scalar(scale2[:], scale[:], 2.0, None, ALU.mult).then_inc(s["scale2_ready"], 1)
            dve.wait_ge(bits_in[0], 16)
            for k in range(KT):
                ins = dve.tensor_scalar(w[0][:, k, :], bits[:, 0, k, :], 2.0, -1.0, ALU.mult, ALU.add)
            ins.then_inc(w_ready[0], 1)
            for t in range(BPC):
                turn(0, 0, t)
                if t + 2 < BPC:
                    normalise(0, 0, t + 2)
            chunks(dve, body)

        @block.tensor
        def _(pe):
            def turn(c, i, t):
                pe.wait_ge(s["hn_ready"], BPC * c + t + 1)
                for half in range(2):
                    if t:
                        pe.wait_ge(s["turn_lo"], 2 * BPC * c + 2 * (t - 1) + half + 1)
                    for j in range(4):
                        k = half * 4 + j
                        ins = pe.transpose(turned[half][:, j * P:(j + 1) * P], hn[:, t % 2, k * P:(k + 1) * P], ident[:])
                    ins.then_inc(s["turn_ready"], 1)

            def hidden(c, i, layer):
                at = i if layer == 0 else 1 - i
                if layer == 0:
                    pe.wait_ge(s["turn_lo"], 2 * BPC * (c + 1))
                pe.wait_ge(w_ready[layer], 1)
                for m in range(KT):
                    a = HID * c + KT * layer + m
                    if layer or m >= 2:
                        pe.wait_ge(s["relu_done"], a - 1)
                    for k in range(KT):
                        if layer and m == 0:
                            pe.wait_ge(s["hid_lo"], HID * c + k + 1)
                        wk = w[layer][:, k, m * P:(m + 1) * P]
                        pe.matmul(lin[m % 2][:], wk, act_hi[at][:, k, :], start=k == 0, stop=False)
                        ins = pe.matmul(lin[m % 2][:], wk, act_lo[at][:, k, :], start=False, stop=k == KT - 1)
                    ins.then_inc(s["lin_ready"], 1)

            def body(c, i, n_next, last):
                hidden(c, i, 0)
                hidden(c, i, 1)
                pe.wait_ge(w_ready[2], 1)
                for t in range(BPC):
                    for n in range(2):
                        if t:
                            pe.wait_ge(s["summed"], 2 * BPC * c + 2 * (t - 1) + n + 1)
                        else:
                            pe.wait_ge(s["summed"], 2 * BPC * c)
                        for k in range(KT):
                            if t == 0 and n == 0:
                                pe.wait_ge(s["hid_lo"], HID * c + KT + k + 1)
                            rows = slice(t * P, (t + 1) * P)
                            wk = w[2][:, k, n * CH:(n + 1) * CH]
                            pe.matmul(outb[n][:], act_hi[i][:, k, rows], wk, start=k == 0, stop=False)
                            ins = pe.matmul(outb[n][:], act_lo[i][:, k, rows], wk, start=False, stop=k == KT - 1)
                        ins.then_inc(s["out_ready"], 1)
                    if not last:
                        turn(c + 1, 1 - i, t)

            pe.wait_ge(const_in, 64)
            for t in range(BPC):
                turn(0, 0, t)
            chunks(pe, body)


def build(nc, a, out):
    def scratch(name, shape):
        return nc.dram_tensor(name, shape, F32, kind="Internal").ap()

    tok_d = scratch("tok_d", [CHUNKS, P, PACK])
    wabs_d = scratch("wabs_d", [PAIRS, P, 2, QT, PAIR * P])
    wvo_d = scratch("wvo_d", [PAIRS, P, 2, PAIR, D])
    wqr_d = scratch("wqr_d", [QUADS, P, 2, QT, 2, P])
    x1_d = scratch("x1_d", [TOKENS, D])
    x2_d = scratch("x2_d", [TOKENS, D])
    project(nc, a["x"], a["w_down"], a, tok_d)
    absorb(nc, a["w_heads"], a["w_rope"], wabs_d, wvo_d, wqr_d)
    attend(nc, a["x"], tok_d, wabs_d, wvo_d, wqr_d, a, x1_d)
    cross(nc, x1_d, a["context"], a, x2_d)
    feed(nc, x2_d, a["signs"], a["scales"], a, out)


def constants():
    half = np.arange(0, DR, 2, dtype=np.float32) / np.float32(DR)
    freqs = np.float32(1.0) / np.power(np.float32(10000.0), half)
    wave = np.float32(2.0 * np.pi) / freqs
    ramp = np.clip((wave / np.float32(4096.0) - np.float32(1.0)) / np.float32(31.0), 0, 1).astype(np.float32)
    inv = freqs / (np.float32(1.0) - ramp + ramp * np.float32(40.0))
    angle = (np.arange(SEQ, dtype=np.float32)[None, :] * inv[:, None]).astype(np.float32)
    cos, sin = np.cos(angle).astype(np.float32), np.sin(angle).astype(np.float32)
    sc = np.float32(SCORE_SCALE)
    row = np.arange(KT * P).reshape(KT, P).T
    inhibitory = row >= round(D * 0.8)
    return {
        "ident": np.eye(P, dtype=np.float32),
        "mask": np.where(np.tril(np.ones((SEQ, SEQ), bool)), 0, MASKED).astype(np.float32),
        "cos": np.tile(cos, (QUAD, 1)),
        "sin": np.tile(sin, (QUAD, 1)),
        "k_tab": np.concatenate([cos * sc, cos * sc, -sin * sc, sin * sc]),
        "sign_mul": np.where(inhibitory, -8, 2).astype(np.float32),
        "sign_add": np.where(inhibitory, 4, -1).astype(np.float32),
    }


def kernel(x, ctx_4096, L0_attn_w_q_down, L0_attn_w_q_up_nope, L0_attn_w_q_up_rope, L0_attn_w_kv_down,
           L0_attn_w_k_rope, L0_attn_w_uk, L0_attn_w_uv, L0_attn_w_out, L0_ffn_k0, L0_ffn_s0, L0_ffn_k1,
           L0_ffn_s1, L0_ffn_k2, L0_ffn_s2):
    import concourse.bacc as bacc
    from concourse.bass_utils import run_bass_kernel_spmd

    x, ctx_4096 = np.asarray(x), np.asarray(ctx_4096)
    wkr = np.asarray(L0_attn_w_k_rope)
    w_down = np.concatenate([np.asarray(L0_attn_w_q_down), np.asarray(L0_attn_w_kv_down), wkr,
                             wkr[:, HALF:], wkr[:, :HALF]], axis=1)
    w_down = w_down.reshape(KT, P, 5 * P).transpose(1, 0, 2)
    nope_t = np.asarray(L0_attn_w_q_up_nope).reshape(QL, HEADS, DN).transpose(1, 2, 0)
    heads = np.concatenate([nope_t, np.asarray(L0_attn_w_uk).reshape(HEADS, DN, KVL),
                            np.asarray(L0_attn_w_uv).reshape(HEADS, DV, KVL),
                            np.asarray(L0_attn_w_out).reshape(HEADS, DV, D)], axis=2)
    heads = heads.reshape(PAIRS, PAIR, P, HEAD_W).transpose(0, 2, 1, 3)
    w_rope = np.asarray(L0_attn_w_q_up_rope).reshape(QT, P, QUADS, QUAD, 2, HALF).transpose(2, 1, 0, 4, 3, 5)
    w_rope = w_rope.reshape(QUADS, P, QT, 2, P)
    ctx_t = ctx_4096.reshape(BATCHES, SEQ, KT, P).transpose(0, 3, 2, 1).reshape(BATCHES, P, KT * SEQ)
    context = np.concatenate([ctx_4096, ctx_t], axis=2)
    signs = np.stack([np.asarray(k).reshape(KT, P, D).transpose(1, 0, 2)
                      for k in (L0_ffn_k0, L0_ffn_k1, L0_ffn_k2)]).view(np.int32)
    scales = np.broadcast_to(np.stack([np.asarray(s).reshape(()) for s in (L0_ffn_s0, L0_ffn_s1, L0_ffn_s2)]), (P, 3))
    arrays = {"x": x.reshape(TOKENS, D), "w_down": w_down, "w_heads": heads, "w_rope": w_rope, "context": context,
              "signs": signs, "scales": scales, **constants()}
    arrays = {name: np.ascontiguousarray(v) for name, v in arrays.items()}

    nc = bacc.Bacc("TRN2", target_bir_lowering=False, num_devices=1)
    a = {name: nc.dram_tensor(f"in_{name}", v.shape, mybir.dt.from_np(v.dtype), kind="ExternalInput").ap()
         for name, v in arrays.items()}
    out = nc.dram_tensor("out", [TOKENS, D], F32, kind="ExternalOutput").ap()
    build(nc, a, out)
    r = run_bass_kernel_spmd(nc, [{f"in_{name}": v for name, v in arrays.items()}], core_ids=[0])
    return r.results[0]["out"].reshape(BATCHES, SEQ, D)
```

```python
from contextlib import ExitStack

import numpy as np

import concourse.bass as bass
from concourse import mybir

F32 = mybir.dt.float32
F32R = mybir.dt.float32r
U8 = mybir.dt.uint8
I32 = mybir.dt.int32
ACT = mybir.ActivationFunctionType
ALU = mybir.AluOpType
AX_X = mybir.AxisListType.X

P = 128
BATCHES, SEQ, D = 16, 128, 1024
TOKENS = BATCHES * SEQ
KT = D // P
HEADS, QL, KVL, DN, DR, DV = 32, 384, 128, 128, 64, 128
QT = QL // P
HALF = DR // 2
QUAD = P // HALF
QUADS = HEADS // QUAD
PAIR = 2
PAIRS = HEADS // PAIR
CH = 512
CHUNKS = TOKENS // CH
BPC = CH // SEQ
GROUPS = 2
CPG = CHUNKS // GROUPS
BPG = BATCHES // GROUPS
EPS = 1e-5
SCORE_SCALE = float(1.0 / np.sqrt(np.float32(DN + DR)))
MASKED = -1e30
HEAD_W = QL + KVL + KVL + D
WH = QL + D

CQ_HI, CQ_LO = 0, QT * CH
KT_HI, KT_LO = 2 * QT * CH, 2 * QT * CH + CH
KV_HI, KV_LO = KT_LO + CH, KT_LO + 2 * CH
KR_HI, KR_LO = KT_LO + 3 * CH, KT_LO + 4 * CH
PACK = KR_LO + CH


def as_f32(ap):
    return ap.bitcast(F32)


def three_passes(pe, out, w_hi, w_lo, x_hi, x_lo, first, last):
    pe.matmul(out, w_hi, x_hi, start=first, stop=False)
    pe.matmul(out, w_hi, x_lo, start=False, stop=False)
    return pe.matmul(out, w_lo, x_hi, start=False, stop=last)


def prepare(nc, x, w_down, w_heads, consts, tok_d, wh_d):
    WC = 5 * P
    HPC = HEADS // CHUNKS
    LOADS = 4
    UK, UV, OUT = QL, QL + KVL, QL + 2 * KVL
    ctx = ExitStack()
    with ctx:
        def sb(name, shape, dt=F32):
            return ctx.enter_context(nc.sbuf_tensor(name, shape, dt))

        def bank(name):
            return ctx.enter_context(nc.psum_tensor(name, [P, CH], F32))

        def sem(name):
            return ctx.enter_context(nc.semaphore(name))

        w_hi = sb("pj_w_hi", [P, KT, WC], F32R)
        w_lo = sb("pj_w_lo", [P, KT, WC], F32R)
        ident = sb("pj_ident", [P, P])
        k_tab = sb("pj_k_tab", [P, SEQ])
        eps = sb("pj_eps", [P, 1])
        xin = sb("pj_x", [P, BPC, D])
        hn = sb("pj_hn", [P, BPC, D])
        stats = sb("pj_stats", [P, BPC, 2, 6])
        mv = sb("pj_mv", [P, BPC, 2])
        std = sb("pj_std", [P, BPC])
        rstd = sb("pj_rstd", [P, BPC])
        hT_hi = sb("pj_hT_hi", [P, KT, CH], F32R)
        hT_lo = sb("pj_hT_lo", [P, KT, CH], F32R)
        pack = sb("pj_pack", [P, PACK], F32R)
        w_raw = as_f32(pack[:, 0:KT * WC]).rearrange("p (k n) -> p k n", k=KT)
        kv_raw = sb("pj_kv_raw", [P, CH])
        k_cos = sb("pj_k_cos", [DR, CH])
        k_sin = sb("pj_k_sin", [DR, CH])
        k_rot = sb("pj_k_rot", [DR, CH])
        head_raw = [sb(f"ab_raw{i}", [P, HEAD_W]) for i in range(LOADS)]
        head_hi = [sb(f"ab_hi{i}", [P, HEAD_W], F32R) for i in range(2)]
        head_lo = [sb(f"ab_lo{i}", [P, HEAD_W], F32R) for i in range(2)]
        head = [sb(f"ab_out{i}", [P, WH]) for i in range(2)]

        turned = [bank(f"pj_turned{i}") for i in range(2)]
        down = [bank(f"pj_down{i}") for i in range(2)]
        kv_turned = bank("pj_kv_turned")
        products = [bank(f"ab_product{i}") for i in range(3)]

        w_in, const_in, x_in = sem("pj_w_in"), sem("pj_const_in"), sem("pj_x_in")
        first_in = [sem(f"pj_first_in{t}") for t in range(BPC)]
        w_hi_done, w_lo_done = sem("pj_w_hi_done"), sem("pj_w_lo_done")
        rstd_done = sem("pj_rstd_done")
        sin_done = sem("pj_sin_done")
        var_ready, std_ready, hn_ready = sem("pj_var_ready"), sem("pj_std_ready"), sem("pj_hn_ready")
        turn_ready, turn_hi, turn_lo = sem("pj_turn_ready"), sem("pj_turn_hi"), sem("pj_turn_lo")
        down_ready, cq_hi, cq_lo = sem("pj_down_ready"), sem("pj_cq_hi"), sem("pj_cq_lo")
        kt_hi, kv_raw_ready = sem("pj_kt_hi"), sem("pj_kv_raw_ready")
        kt_lo, kv_lo = sem("pj_kt_lo"), sem("pj_kv_lo")
        kv_turn_ready, kv_hi = sem("pj_kv_turn_ready"), sem("pj_kv_hi")
        rot_ready, kr_hi, kr_lo = sem("pj_rot_ready"), sem("pj_kr_hi"), sem("pj_kr_lo")
        zeroed = sem("pj_zeroed")
        cq_out, key_out = sem("pj_cq_out"), sem("pj_key_out")
        head_in = [sem(f"ab_in{i}") for i in range(LOADS)]
        head_hi_done, head_lo_done, product_ready = sem("ab_hi_done"), sem("ab_lo_done"), sem("ab_product_ready")
        taken = sem("ab_taken")
        head_out = [sem(f"ab_head_out{i}") for i in range(2)]

        x_chunks = x.rearrange("(c b p) d -> c p b d", c=CHUNKS, p=P)
        block = ctx.enter_context(nc.Block())

        def chunks(eng, body):
            with eng.Fori(0, CHUNKS - 1) as c:
                body(c, False)
            body(CHUNKS - 1, True)

        @block.sync
        def _(sp):
            for i in range(2):
                sp.sem_inc(head_out[i], 16)
            sp.sem_inc(cq_out, 16)
            sp.sem_inc(key_out, 16)

            def load_head(n, i):
                sp.dma_start(head_raw[i][:], w_heads[n]).then_inc(head_in[i], 16)

            for t in range(BPC):
                sp.dma_start(xin[:, t, :], x_chunks[0][:, t, :]).then_inc(first_in[t], 16)
            sp.dma_start(ident[:], consts["ident"]).then_inc(const_in, 16)
            sp.dma_start(k_tab[:], consts["k_tab"]).then_inc(const_in, 16)
            load_head(0, 0)
            sp.dma_start(w_raw, w_down).then_inc(w_in, 16)
            for i in range(1, LOADS):
                load_head(i, i)

            def body(c, last):
                if not last:
                    sp.wait_ge(hn_ready, BPC * (c + 1))
                    sp.dma_start(xin[:], x_chunks[c + 1]).then_inc(x_in, 16)
                for j in range(HPC):
                    sp.wait_ge(taken, 3 * (HPC * c + j + 1) + 3)
                    sp.dma_start(wh_d[HPC // 2 * c + j // 2][:, j % 2, :], head[j % 2][:]).then_inc(head_out[j % 2], 16)
                    if not (last and j + LOADS >= HPC):
                        load_head(HPC * c + j + LOADS, j % LOADS)
                    if j == 4:
                        sp.wait_ge(cq_lo, QT * (c + 1))
                        sp.dma_start(tok_d[c][:, 0:KT_HI], as_f32(pack[:, 0:KT_HI])).then_inc(cq_out, 16)
                sp.wait_ge(kr_lo, c + 1)
                sp.dma_start(tok_d[c][:, KT_HI:PACK], as_f32(pack[:, KT_HI:PACK])).then_inc(key_out, 16)

            sp.wait_ge(zeroed, 1)
            chunks(sp, body)
            sp.wait_ge(cq_out, 16 * CHUNKS + 16)
            sp.wait_ge(key_out, 16 * CHUNKS + 16)
            for i in range(2):
                sp.wait_ge(head_out[i], 16 * (HEADS // 2) + 16)

        @block.gpsimd
        def _(pool):
            pool.memset(as_f32(pack[DR:P, KR_LO:KR_LO + CH]), 0.0).then_inc(zeroed, 1)
            pool.wait_ge(zeroed, 1)

            def cut(n, i):
                pool.wait_ge(head_hi_done, n + 1)
                pool.tensor_tensor(head_lo[i % 2][:], head_raw[i][:], as_f32(head_hi[i % 2][:]),
                                   ALU.subtract).then_inc(head_lo_done, 1)

            cut(0, 0)
            pool.wait_ge(w_hi_done, 1)
            pool.tensor_tensor(w_lo[:], w_raw, as_f32(w_hi[:]), ALU.subtract).then_inc(w_lo_done, 1)
            for i in range(1, LOADS):
                cut(i, i)
            with pool.Fori(1, HEADS // LOADS) as n:
                for i in range(LOADS):
                    cut(LOADS * n + i, i)

        @block.scalar
        def _(act):
            def cut(c, j):
                act.wait_ge(head_in[j % LOADS], 16 * (HPC // LOADS * c + j // LOADS + 1))
                act.activation(head_hi[j % 2][:], head_raw[j % LOADS][:], ACT.Copy).then_inc(head_hi_done, 1)

            def root(c):
                act.wait_ge(var_ready, c + 1)
                act.activation(std[:], mv[:, :, 1], ACT.Sqrt, bias=eps[:, 0:1]).then_inc(std_ready, 1)

            def body(c, last):
                def turns(tiles):
                    for z in tiles:
                        t, half = z // 2, z % 2
                        act.wait_ge(turn_ready, 2 * BPC * c + z + 1)
                        act.activation(hT_hi[:, half * 4:half * 4 + 4, t * P:(t + 1) * P],
                                       turned[z % 2][:].rearrange("p (k s) -> p k s", k=4),
                                       ACT.Copy).then_inc(turn_hi, 1)

                def query(m):
                    act.wait_ge(down_ready, 5 * c + m + 1)
                    act.activation(pack[:, CQ_HI + m * CH:CQ_HI + (m + 1) * CH], down[m % 2][:],
                                   ACT.Copy).then_inc(cq_hi, 1)

                def ahead(j):
                    if not (last and j + 2 >= HPC):
                        act.wait_ge(product_ready, 3 * (HPC * c + j + 1))
                        cut(c, j + 2)

                turns(range(4))
                ahead(0)
                turns(range(4, 8))
                ahead(1)
                act.wait_ge(cq_out, 16 * c + 16)
                query(0)
                ahead(2)
                query(1)
                ahead(3)
                query(2)
                if not last:
                    root(c + 1)
                ahead(4)
                act.wait_ge(down_ready, 5 * c + 4)
                act.activation(kv_raw[:], down[1][:], ACT.Copy).then_inc(kv_raw_ready, 1)
                act.wait_ge(key_out, 16 * c + 16)
                act.activation(pack[:, KT_HI:KT_HI + CH], down[1][:], ACT.Copy,
                               scale=SCORE_SCALE).then_inc(kt_hi, 1)
                ahead(5)
                ahead(6)
                act.wait_ge(kv_turn_ready, c + 1)
                act.activation(pack[:, KV_HI:KV_HI + CH], kv_turned[:], ACT.Copy).then_inc(kv_hi, 1)
                act.wait_ge(rot_ready, c + 1)
                act.activation(pack[0:DR, KR_HI:KR_HI + CH], k_rot[:], ACT.Copy)
                act.activation(pack[DR:P, KR_HI:KR_HI + CH], k_rot[:], ACT.Copy).then_inc(kr_hi, 1)
                ahead(7)

            cut(0, 0)
            root(0)
            act.wait_ge(w_in, 16)
            act.activation(w_hi[:], w_raw, ACT.Copy).then_inc(w_hi_done, 1)
            cut(0, 1)
            chunks(act, body)

        @block.vector
        def _(dve):
            dve.sem_inc(sin_done, 1)
            dve.sem_inc(kt_lo, 1)
            dve.sem_inc(kv_lo, 1)
            dve.sem_inc(taken, 3)

            def moments(c, first):
                if not first:
                    dve.wait_ge(x_in, 16 * c)
                for t in range(BPC):
                    if first:
                        dve.wait_ge(first_in[t], 16)
                    for h in range(2):
                        dve.bn_stats(stats[:, t, h, :], xin[:, t, h * 512:(h + 1) * 512])
                dve.drain()
                for t in range(BPC):
                    ins = dve.bn_aggr(mv[:, t, :], stats[:, t].rearrange("p h s -> p (h s)"))
                ins.then_inc(var_ready, 1)

            def normalise(c):
                dve.wait_ge(std_ready, c + 1)
                dve.reciprocal(rstd[:], std[:]).then_inc(rstd_done, 1)
                dve.wait_ge(rstd_done, c + 1)
                for t in range(BPC):
                    dve.tensor_scalar(hn[:, t, :], xin[:, t, :], mv[:, t, 0:1], rstd[:, t:t + 1],
                                      ALU.subtract, ALU.mult).then_inc(hn_ready, 1)

            def body(c, last):
                def turns(tiles):
                    for z in tiles:
                        t, half = z // 2, z % 2
                        dve.wait_ge(turn_hi, 2 * BPC * c + z + 1)
                        at = (slice(None), slice(half * 4, half * 4 + 4), slice(t * P, (t + 1) * P))
                        dve.tensor_tensor(hT_lo[at], turned[z % 2][:].rearrange("p (k s) -> p k s", k=4),
                                          as_f32(hT_hi[at]), ALU.subtract).then_inc(turn_lo, 1)

                def take(j):
                    n = HPC * c + j
                    dve.wait_ge(head_out[j % 2], 16 * (HPC // 2 * c + j // 2) + 16)
                    for i, (lo, width) in enumerate(((0, QL), (QL, CH), (QL + CH, CH))):
                        dve.wait_ge(product_ready, 3 * n + i + 1)
                        dve.tensor_copy(head[j % 2][:, lo:lo + width], products[i][:, 0:width]).then_inc(taken, 1)

                def query(m):
                    dve.wait_ge(cq_hi, QT * c + m + 1)
                    dve.tensor_tensor(pack[:, CQ_LO + m * CH:CQ_LO + (m + 1) * CH], down[m % 2][:],
                                      as_f32(pack[:, CQ_HI + m * CH:CQ_HI + (m + 1) * CH]),
                                      ALU.subtract).then_inc(cq_lo, 1)

                def times_table(out, rows):
                    return dve.tensor_tensor(
                        out.rearrange("p (b s) -> p b s", b=BPC),
                        down[0][rows, :].rearrange("p (b s) -> p b s", b=BPC),
                        k_tab[rows, :].unsqueeze(1).to_broadcast([DR, BPC, SEQ]), ALU.mult)

                turns(range(4))
                take(0)
                turns(range(4, 8))
                take(1)
                query(0)
                take(2)
                query(1)
                take(3)
                if not last:
                    moments(c + 1, False)
                query(2)
                take(4)
                if not last:
                    normalise(c + 1)
                dve.wait_ge(kt_hi, c + 1)
                dve.scalar_tensor_tensor(out=pack[:, KT_LO:KT_LO + CH], in0=down[1][:], scalar=SCORE_SCALE,
                                         in1=as_f32(pack[:, KT_HI:KT_HI + CH]), op0=ALU.mult,
                                         op1=ALU.subtract).then_inc(kt_lo, 1)
                take(5)
                dve.wait_ge(down_ready, 5 * c + 5)
                times_table(k_cos[:], slice(0, DR))
                times_table(k_sin[:], slice(DR, P)).then_inc(sin_done, 1)
                dve.wait_ge(sin_done, c + 2)
                dve.tensor_tensor(k_rot[:], k_cos[:], k_sin[:], ALU.add).then_inc(rot_ready, 1)
                take(6)
                dve.wait_ge(kv_hi, c + 1)
                dve.tensor_tensor(pack[:, KV_LO:KV_LO + CH], kv_turned[:],
                                  as_f32(pack[:, KV_HI:KV_HI + CH]), ALU.subtract).then_inc(kv_lo, 1)
                dve.wait_ge(kr_hi, c + 1)
                dve.tensor_tensor(pack[0:DR, KR_LO:KR_LO + CH], k_rot[:],
                                  as_f32(pack[0:DR, KR_HI:KR_HI + CH]), ALU.subtract).then_inc(kr_lo, 1)
                take(7)

            dve.memset(eps[:], EPS)
            moments(0, True)
            normalise(0)
            dve.wait_ge(const_in, 32)
            chunks(dve, body)

        @block.tensor
        def _(pe):
            pe.wait_ge(const_in, 32)

            def body(c, last):
                def turns(tiles):
                    for z in tiles:
                        t, half = z // 2, z % 2
                        pe.wait_ge(hn_ready, BPC * c + t + 1)
                        if z >= 2:
                            pe.wait_ge(turn_lo, 2 * BPC * c + z - 1)
                        for j in range(4):
                            k = half * 4 + j
                            ins = pe.transpose(turned[z % 2][:, j * P:(j + 1) * P],
                                               hn[:, t, k * P:(k + 1) * P], ident[:])
                        ins.then_inc(turn_ready, 1)

                def project(m):
                    if m == 0:
                        pe.wait_ge(turn_lo, 2 * BPC * (c + 1))
                        pe.wait_ge(w_lo_done, 1)
                        pe.wait_ge(sin_done, c + 1)
                    elif m == 1:
                        pe.wait_ge(kt_lo, c + 1)
                    else:
                        pe.wait_ge(cq_lo, QT * c + m - 1)
                    cols = slice(m * P, (m + 1) * P)
                    for k in range(KT):
                        ins = three_passes(pe, down[m % 2][:], w_hi[:, k, cols], w_lo[:, k, cols],
                                           hT_hi[:, k, :], hT_lo[:, k, :], k == 0, k == KT - 1)
                    ins.then_inc(down_ready, 1)

                def absorb(j):
                    n = HPC * c + j
                    hi, lo = head_hi[j % 2], head_lo[j % 2]
                    pe.wait_ge(head_lo_done, n + 1)
                    pe.wait_ge(taken, 3 * n + 1)
                    for k in range(QT):
                        ins = three_passes(pe, products[0][:, k * P:(k + 1) * P], hi[:, k * P:(k + 1) * P],
                                           lo[:, k * P:(k + 1) * P], hi[:, UK:UV], lo[:, UK:UV], True, True)
                    ins.then_inc(product_ready, 1)
                    for i in range(2):
                        cols = slice(OUT + i * CH, OUT + (i + 1) * CH)
                        pe.wait_ge(taken, 3 * n + i + 2)
                        three_passes(pe, products[1 + i][:], hi[:, UV:OUT], lo[:, UV:OUT],
                                     hi[:, cols], lo[:, cols], True, True).then_inc(product_ready, 1)

                turns(range(4))
                absorb(0)
                turns(range(4, 8))
                absorb(1)
                for m in range(5):
                    project(m)
                    if m == 4:
                        pe.wait_ge(kv_raw_ready, c + 1)
                        pe.wait_ge(kv_lo, c + 1)
                        for b in range(BPC):
                            ins = pe.transpose(kv_turned[:, b * P:(b + 1) * P], kv_raw[:, b * P:(b + 1) * P], ident[:])
                        ins.then_inc(kv_turn_ready, 1)
                    absorb(m + 2)
                absorb(7)

            chunks(pe, body)


def attend(nc, x, tok_d, wh_d, w_rope, consts, x1_d):
    STEPS, UNITS, ROPES = 8, 4, CPG
    PARTS = 2 * PAIR
    ROPE_CHUNK = {2: 0, 4: 1}
    USE = [0, 1, 2, 5, 6, 9, 10, 11]
    ctx = ExitStack()
    with ctx:
        def sb(name, shape, dt=F32):
            return ctx.enter_context(nc.sbuf_tensor(name, shape, dt))

        def bank(name):
            return ctx.enter_context(nc.psum_tensor(name, [P, CH], F32))

        def sem(name):
            return ctx.enter_context(nc.semaphore(name))

        tok = sb("at_tok", [P, CPG, PACK], F32R)
        acc = sb("at_acc", [P, BPG, D])
        w_raw = sb("at_w_raw", [P, PAIR * D])
        wabs = [sb(f"at_wabs{i}", [P, 2, PAIR * QL], F32R) for i in range(2)]
        wvo = [sb(f"at_wvo{i}", [P, 2, PAIR * D], F32R) for i in range(2)]
        wqr = sb("at_wqr", [P, 2, QT * 2 * P], F32R)
        weights = [wqr, wabs[0], wabs[1], wvo[0], wvo[1]]
        WQR, WABS, WVO, LOADS = 0, 1, 3, 5
        CUT_NEXT = {1: WQR, 3: WABS, 5: WABS + 1, 6: WVO}
        qlat = [sb(f"at_qlat{i}", [P, 2, PAIR, CH], F32R) for i in range(2)]
        qrope = [sb(f"at_qrope{c}", [P, QUAD, CH], F32R) for c in range(CPG)]
        rope_tmp = sb("at_rope_tmp", [P, 4, CH])
        rope_parts = sb("at_rope_parts", [P, 4, CH], F32R)
        probs = [sb(f"at_probs{i}", [P, PARTS, SEQ]) for i in range(2)]
        nmax = [sb(f"at_nmax{i}", [P, PARTS]) for i in range(2)]
        sums = [sb(f"at_sums{i}", [P, PARTS]) for i in range(2)]
        rsum = [sb(f"at_rsum{i}", [P, PARTS]) for i in range(2)]
        pT_hi = sb("at_pT_hi", [P, CH], F32R)
        pT_lo = sb("at_pT_lo", [P, CH], F32R)
        val_hi = [sb(f"at_val_hi{i}", [P, CH], F32R) for i in range(2)]
        val_lo = [sb(f"at_val_lo{i}", [P, CH], F32R) for i in range(2)]
        ident = sb("at_ident", [P, P])
        mask = sb("at_mask", [P, SEQ])
        cross_sum = sb("at_cross_sum", [P, PARTS, SEQ])
        cos = sb("at_cos", [P, SEQ])
        sin = sb("at_sin", [P, SEQ])

        qbank = [bank(f"at_qbank{i}") for i in range(2)]
        score = ctx.enter_context(nc.psum_tensor("at_score", [P, PARTS, 2, SEQ], F32))
        turned, value = bank("at_turned"), bank("at_value")
        outb = [bank(f"at_out{i}") for i in range(2)]

        const_in, x1_last = sem("at_const_in"), sem("at_x1_last")
        cq_in, key_in, kv_in, acc_in, x1_out = ([sem(f"at_{n}{c}") for c in range(CPG)]
                                                for n in ("cq_in", "key_in", "kv_in", "acc_in", "x1_out"))
        weights_in, weights_hi, weights_lo = (sem(f"at_weights_{n}") for n in ("in", "hi", "lo"))
        qrope_in = [sem(f"at_qrope_in{c}") for c in range(CPG)]
        ql_mm, ql_hi, ql_lo = sem("at_ql_mm"), sem("at_ql_hi"), sem("at_ql_lo")
        rope_mm, rope_cs, rope_sum = sem("at_rope_mm"), sem("at_rope_cs"), sem("at_rope_sum")
        rope_hi, rope_lo = sem("at_rope_hi"), sem("at_rope_lo")
        score_ready, crossed, score_taken = sem("at_score_ready"), sem("at_crossed"), sem("at_score_taken")
        max_ready, exp_ready = sem("at_max_ready"), sem("at_exp_ready")
        rsum_ready, probs_ready = sem("at_rsum_ready"), sem("at_probs_ready")
        turn_ready, pT_hi_done, pT_lo_done = sem("at_turn_ready"), sem("at_pT_hi_done"), sem("at_pT_lo_done")
        value_ready, val_hi_done, val_lo_done = (sem(f"at_{n}") for n in ("value_ready", "val_hi_done", "val_lo_done"))
        out_ready = sem("at_out_ready")
        added = sem("at_added")

        def batch_cols(s, bl):
            b = 2 * (s % 2) + bl
            return slice(b * SEQ, (b + 1) * SEQ)

        def place(s):
            return (s // 2) // CPG % 2, (s // 2) % CPG

        x_chunks = x.rearrange("(c b p) d -> c p b d", c=CHUNKS, p=P)
        x1_chunks = x1_d.rearrange("(c b p) d -> c p b d", c=CHUNKS, p=P)
        block = ctx.enter_context(nc.Block())

        def quads(eng, opening, slot):
            opening()
            for g in range(GROUPS):
                with eng.Fori(0, QUADS - 1) as q:
                    for s in range(STEPS):
                        slot(g * QUADS + q, s, 2 * STEPS, lambda k: g)
                for s in range(STEPS):
                    slot(g * QUADS + QUADS - 1, s, 2 * STEPS if g < GROUPS - 1 else STEPS, lambda k: g + k // STEPS)

        def cuts(cut, m, s, end):
            if s == 0:
                cut(WVO + 1, m)
            elif s in CUT_NEXT and end > STEPS:
                cut(CUT_NEXT[s], m + 1)

        @block.sync
        def _(sp):
            def load(k, m, q):
                if not (isinstance(m, int) and LOADS * m + k == 0):
                    sp.wait_ge(weights_lo, LOADS * m + k)
                if k == WQR:
                    of, to = w_rope[q], w_raw[:, 0:QT * 2 * P]
                elif k < WVO:
                    of = wh_d[2 * q + k - WABS][:, :, 0:QL]
                    to = w_raw[:, 0:PAIR * QL].rearrange("p (h n) -> p h n", h=PAIR)
                else:
                    of, to = wh_d[2 * q + k - WVO][:, :, QL:WH], w_raw[:].rearrange("p (h n) -> p h n", h=PAIR)
                sp.dma_start(to, of).then_inc(weights_in, 16)

            def load_tokens(g, c, lo, hi, done):
                sp.dma_start(as_f32(tok[:, c, lo:hi]), tok_d[CPG * g + c][:, lo:hi]).then_inc(done[c], 16)

            def load_queries(g, c):
                load_tokens(g, c, CQ_HI, KT_HI, cq_in)

            def load_keys(g, c):
                load_tokens(g, c, KT_HI, KV_HI, key_in)
                load_tokens(g, c, KR_HI, PACK, key_in)

            def load_values(g, c):
                load_tokens(g, c, KV_HI, KR_HI, kv_in)

            def load_x(g, c):
                sp.dma_start(acc[:, BPC * c:BPC * (c + 1), :], x_chunks[CPG * g + c]).then_inc(acc_in[c], 16)

            def store_x1(g, c):
                sp.dma_start(x1_chunks[CPG * g + c], acc[:, BPC * c:BPC * (c + 1), :]).then_inc(x1_out[c], 16)

            def relayout(m, c):
                sp.wait_ge(rope_lo, 2 * (ROPES * m + c + 1))
                for h in range(QUAD):
                    for j in range(4):
                        sp.dma_start(as_f32(qrope[c][j * HALF:(j + 1) * HALF, h, :]),
                                     as_f32(rope_parts[h * HALF:(h + 1) * HALF, j, :])).then_inc(qrope_in[c], 16)

            def quad(m, q1, switch):
                load(WQR, m + 1, q1)
                if switch:
                    sp.wait_ge(ql_mm, PAIR * (UNITS * m + 3))
                    load_queries(switch, 0)
                load(WABS, m + 1, q1)
                if switch:
                    sp.wait_ge(ql_mm, PAIR * (UNITS * m + 4))
                    load_queries(switch, 1)
                load(WABS + 1, m + 1, q1)
                if switch:
                    sp.wait_ge(score_ready, STEPS * m + 6)
                    load_keys(switch, 0)
                relayout(m + 1, 0)
                load(WVO, m + 1, q1)
                if switch:
                    sp.wait_ge(value_ready, STEPS * m + 6)
                    load_values(switch, 0)
                    sp.wait_ge(score_ready, STEPS * m + 8)
                    load_keys(switch, 1)
                    sp.wait_ge(added, 4 * (STEPS * m + 6) + 2)
                    store_x1(switch - 1, 0)
                relayout(m + 1, 1)
                if switch:
                    sp.wait_ge(value_ready, STEPS * m + 8)
                    load_values(switch, 1)
                    sp.wait_ge(x1_out[0], 16 * switch)
                    load_x(switch, 0)
                load(WVO + 1, m + 1, q1)
                if switch:
                    sp.wait_ge(added, 4 * (STEPS * m + 8) + 2)
                    store_x1(switch - 1, 1)
                    sp.wait_ge(x1_out[1], 16 * switch)
                    load_x(switch, 1)

            load(WQR, 0, 0)
            load_queries(0, 0)
            for to, name in ((ident, "ident"), (mask, "mask"), (cos, "cos"), (sin, "sin")):
                sp.dma_start(to[:], consts[name]).then_inc(const_in, 16)
            load(WABS, 0, 0)
            load_queries(0, 1)
            load_keys(0, 0)
            load_values(0, 0)
            load(WABS + 1, 0, 0)
            relayout(0, 0)
            load_x(0, 0)
            load_keys(0, 1)
            load(WVO, 0, 0)
            relayout(0, 1)
            load_values(0, 1)
            load(WVO + 1, 0, 0)
            load_x(0, 1)
            for g in range(GROUPS):
                with sp.Fori(0, QUADS - 1) as q:
                    quad(g * QUADS + q, q + 1, None)
                if g < GROUPS - 1:
                    quad(g * QUADS + QUADS - 1, 0, g + 1)
            last = GROUPS * QUADS - 1
            for step in range(UNITS, STEPS):
                c, b = place(step)[1], 2 * (step % 2)
                sp.wait_ge(added, 4 * (STEPS * last + step + 1) + 2)
                sp.dma_start(x1_chunks[CPG * (GROUPS - 1) + c][:, b:b + 2, :],
                             acc[:, BPC * c + b:BPC * c + b + 2, :]).then_inc(x1_last, 16)
            sp.wait_ge(x1_last, 16 * (STEPS - UNITS))

        @block.tensor
        def _(pe):
            pe.wait_ge(const_in, 64)

            def latent(m, u, h, g, n, ropes, latents):
                pair, c = place(2 * u)
                if h == 0:
                    pe.wait_ge(cq_in[c], 16 * (g + 1))
                    pe.wait_ge(weights_lo, LOADS * (m + u // UNITS) + WABS + pair + 1)
                pe.wait_ge(rope_cs, ropes)
                if latents is not None:
                    pe.wait_ge(ql_lo, latents)
                for k in range(QT):
                    cols = slice(h * QL + k * P, h * QL + (k + 1) * P)
                    ins = three_passes(pe, qbank[n % 2][:], wabs[pair][:, 0, cols], wabs[pair][:, 1, cols],
                                       tok[:, c, CQ_HI + k * CH:CQ_HI + (k + 1) * CH],
                                       tok[:, c, CQ_LO + k * CH:CQ_LO + (k + 1) * CH], k == 0, k == QT - 1)
                ins.then_inc(ql_mm, 1)

            def rope(m, c, g, n, ropes, latents):
                pe.wait_ge(cq_in[c], 16 * (g + 1))
                pe.wait_ge(weights_lo, LOADS * m + WQR + 1)
                if ropes is not None:
                    pe.wait_ge(rope_cs, ropes)
                if latents is not None:
                    pe.wait_ge(ql_lo, latents)
                for half in range(2):
                    for k in range(QT):
                        cols = slice((2 * k + half) * P, (2 * k + half + 1) * P)
                        ins = three_passes(pe, qbank[(n + half) % 2][:], wqr[:, 0, cols], wqr[:, 1, cols],
                                           tok[:, c, CQ_HI + k * CH:CQ_HI + (k + 1) * CH],
                                           tok[:, c, CQ_LO + k * CH:CQ_LO + (k + 1) * CH], k == 0, k == QT - 1)
                ins.then_inc(rope_mm, 1)

            def scores(m, s, g):
                pair, c = place(s)
                u = s // 2
                if not (isinstance(m, int) and STEPS * m + s == 0):
                    pe.wait_ge(score_taken, STEPS * m + s)
                pe.wait_ge(ql_lo, PAIR * (UNITS * m + u + 1))
                if pair == 0 and s % 2 == 0:
                    pe.wait_ge(key_in[c], 2 * 16 * (g + 1))
                    pe.wait_ge(qrope_in[c], 16 * 16 * (m + s // STEPS + 1))
                keys = tok[:, c, KT_HI:KT_HI + 2 * CH].rearrange("p (part t) -> p part t", part=2)
                rope_keys = tok[:, c, KR_HI:KR_HI + 2 * CH].rearrange("p (part t) -> p part t", part=2)
                for bl in range(2):
                    cols = batch_cols(s, bl)
                    for h in range(PAIR):
                        j = bl * PAIR + h
                        q_hi, q_lo = (qlat[u % 2][:, i, h, cols] for i in range(2))
                        pe.matmul(score[:, j], q_hi, keys[:, :, cols], start=True, stop=False)
                        pe.matmul(score[:, j, 0], q_lo, keys[:, 0, cols], start=False, stop=False)
                        ins = pe.matmul(score[:, j], qrope[c][:, pair * PAIR + h, cols], rope_keys[:, :, cols],
                                        start=False, stop=True)
                ins.then_inc(score_ready, 1)

            def turn(m, s):
                pe.wait_ge(probs_ready, STEPS * m + s + 1)
                for j in range(PARTS):
                    ins = pe.transpose(turned[:, j * SEQ:(j + 1) * SEQ], probs[s % 2][:, j, :], ident[:])
                ins.then_inc(turn_ready, 1)

            def values(m, s, g):
                _, c = place(s)
                pe.wait_ge(kv_in[c], 16 * (g + 1))
                pe.wait_ge(pT_lo_done, STEPS * m + s + 1)
                for bl in range(2):
                    cols = batch_cols(s, bl)
                    at = slice(bl * PAIR * SEQ, (bl + 1) * PAIR * SEQ)
                    ins = three_passes(pe, value[:, at], tok[:, c, KV_HI + cols.start:KV_HI + cols.stop],
                                       tok[:, c, KV_LO + cols.start:KV_LO + cols.stop],
                                       pT_hi[:, at], pT_lo[:, at], True, True)
                ins.then_inc(value_ready, 1)

            def output(m, s, bl):
                pair, _ = place(s)
                if bl == 0:
                    pe.wait_ge(val_lo_done, STEPS * m + s + 1)
                    pe.wait_ge(weights_lo, LOADS * m + WVO + pair + 1)
                for n in range(2):
                    pe.wait_ge(added, 4 * (STEPS * m + s) + 2 * bl + n + 1)
                    for h in range(PAIR):
                        at = slice((bl * PAIR + h) * SEQ, (bl * PAIR + h + 1) * SEQ)
                        cols = slice(h * D + n * CH, h * D + (n + 1) * CH)
                        ins = three_passes(pe, outb[n][:], val_hi[s % 2][:, at], val_lo[s % 2][:, at],
                                           wvo[pair][:, 0, cols], wvo[pair][:, 1, cols],
                                           h == 0, h == PAIR - 1)
                    ins.then_inc(out_ready, 1)

            def opening():
                for u in range(2):
                    rope(0, u, 0, 0, u or None, PAIR * u or None)
                    for h in range(PAIR):
                        latent(0, u, h, 0, h, u + 1, PAIR * u or None)
                scores(0, 0, 0)
                scores(0, 1, 0)
                turn(0, 0)
                values(0, 0, 0)

            def slot(m, s, end, of):
                if s + 1 < end:
                    turn(m, s + 1)
                if s + 2 < end:
                    scores(m, s + 2, of(s + 2))
                output(m, s, 0)
                u = s // 2 + 2
                latents = PAIR * (UNITS * m + u) + s % 2
                more = end > STEPS
                if u < end // 2:
                    ropes = ROPES * (m + 1) + (sum(t < s for t in ROPE_CHUNK) if more else 0)
                    latent(m, u, s % 2, of(2 * u), USE[s], ropes, latents)
                if s + 1 < end:
                    values(m, s + 1, of(s + 1))
                output(m, s, 1)
                if s in ROPE_CHUNK and more:
                    c = ROPE_CHUNK[s]
                    rope(m + 1, c, of(STEPS), USE[s] + 1, ROPES * (m + 1) + c, latents + 1)

            quads(pe, opening, slot)

        @block.scalar
        def _(act):
            def latent(m, u, h, n):
                act.wait_ge(ql_mm, PAIR * (UNITS * m + u) + h + 1)
                act.activation(qlat[u % 2][:, 0, h, :], qbank[n % 2][:], ACT.Copy).then_inc(ql_hi, 1)

            def rope(m, c, moved):
                at = ROPES * m + c
                if moved is not None:
                    act.wait_ge(qrope_in[1 - c], moved)
                for half in range(2):
                    act.wait_ge(rope_sum, 2 * at + half + 1)
                    act.activation(rope_parts[:, half, :], rope_tmp[:, 2 * half, :], ACT.Copy).then_inc(rope_hi, 1)

            def cut(k, m):
                act.wait_ge(weights_in, 16 * (LOADS * m + k + 1))
                width = weights[k].shape[2]
                act.activation(weights[k][:, 0], w_raw[:, 0:width], ACT.Copy).then_inc(weights_hi, 1)

            def exps(m, s):
                i = s % 2
                act.wait_ge(max_ready, STEPS * m + s + 1)
                for j in range(PARTS):
                    ins = act.activation(probs[i][:, j, :], probs[i][:, j, :], ACT.Exp,
                                         bias=nmax[i][:, j:j + 1], accum_out=sums[i][:, j:j + 1])
                ins.then_inc(exp_ready, 1)

            def turn(m, s):
                act.wait_ge(turn_ready, STEPS * m + s + 1)
                act.activation(pT_hi[:], turned[:], ACT.Copy).then_inc(pT_hi_done, 1)

            def values(m, s):
                act.wait_ge(value_ready, STEPS * m + s + 1)
                act.activation(val_hi[s % 2][:], value[:], ACT.Copy).then_inc(val_hi_done, 1)

            def opening():
                cut(WQR, 0)
                cut(WABS, 0)
                rope(0, 0, None)
                for h in range(PAIR):
                    latent(0, 0, h, h)
                cut(WABS + 1, 0)
                for h in range(PAIR):
                    latent(0, 1, h, h)
                rope(0, 1, 256)
                exps(0, 0)
                exps(0, 1)
                cut(WVO, 0)
                turn(0, 0)
                values(0, 0)

            def slot(m, s, end, of):
                if s + 1 < end:
                    turn(m, s + 1)
                if s + 2 < end:
                    exps(m, s + 2)
                if s // 2 + 2 < end // 2:
                    latent(m, s // 2 + 2, s % 2, USE[s])
                if s + 1 < end:
                    values(m, s + 1)
                if s - 1 in ROPE_CHUNK and end > STEPS:
                    c = ROPE_CHUNK[s - 1]
                    rope(m + 1, c, 256 * (m + 1 + c))
                cuts(cut, m, s, end)

            quads(act, opening, slot)

        @block.gpsimd
        def _(pool):
            def normalise(m, s):
                i = s % 2
                pool.wait_ge(rsum_ready, STEPS * m + s + 1)
                pool.tensor_tensor(probs[i][:], probs[i][:], rsum[i][:].unsqueeze(2).to_broadcast([P, PARTS, SEQ]),
                                   ALU.mult).then_inc(probs_ready, 1)

            def cut(k, m):
                pool.wait_ge(weights_hi, LOADS * m + k + 1)
                width = weights[k].shape[2]
                pool.tensor_tensor(weights[k][:, 1], w_raw[:, 0:width], as_f32(weights[k][:, 0]),
                                   ALU.subtract).then_inc(weights_lo, 1)

            def rope_sums(m, c):
                at = ROPES * m + c
                pool.wait_ge(rope_cs, at + 1)
                for half, op in ((0, ALU.subtract), (1, ALU.add)):
                    pool.tensor_tensor(rope_tmp[:, 2 * half, :], rope_tmp[:, 2 * half, :],
                                       rope_tmp[:, 2 * half + 1, :], op).then_inc(rope_sum, 1)

            def rope_low(m, c):
                at = ROPES * m + c
                for half in range(2):
                    pool.wait_ge(rope_hi, 2 * at + half + 1)
                    pool.tensor_tensor(rope_parts[:, 2 + half, :], rope_tmp[:, 2 * half, :],
                                       as_f32(rope_parts[:, half, :]), ALU.subtract).then_inc(rope_lo, 1)

            def opening():
                cut(WQR, 0)
                cut(WABS, 0)
                rope_sums(0, 0)
                rope_low(0, 0)
                cut(WABS + 1, 0)
                rope_sums(0, 1)
                rope_low(0, 1)
                normalise(0, 0)
                normalise(0, 1)
                cut(WVO, 0)

            def slot(m, s, end, of):
                finish = s - 1 in ROPE_CHUNK and end > STEPS
                if finish:
                    rope_sums(m + 1, ROPE_CHUNK[s - 1])
                if s + 2 < end:
                    normalise(m, s + 2)
                if finish:
                    rope_low(m + 1, ROPE_CHUNK[s - 1])
                cuts(cut, m, s, end)

            quads(pool, opening, slot)

        @block.vector
        def _(dve):
            dve.sem_inc(added, 2)
            dve.wait_ge(const_in, 64)

            def latent(m, u, h, n):
                dve.wait_ge(ql_hi, PAIR * (UNITS * m + u) + h + 1)
                dve.tensor_tensor(qlat[u % 2][:, 1, h, :], qbank[n % 2][:], as_f32(qlat[u % 2][:, 0, h, :]),
                                  ALU.subtract).then_inc(ql_lo, 1)

            def rope(m, c, n, used):
                dve.wait_ge(rope_mm, ROPES * m + c + 1)
                if used is not None:
                    dve.wait_ge(rope_lo, used)

                def times(out, half, table):
                    return dve.tensor_tensor(rope_tmp[:, out, :].rearrange("p (b s) -> p b s", b=BPC),
                                             qbank[(n + half) % 2][:].rearrange("p (b s) -> p b s", b=BPC),
                                             table[:].unsqueeze(1).to_broadcast([P, BPC, SEQ]), ALU.mult)

                times(0, 0, cos)
                times(1, 1, sin)
                times(2, 0, sin)
                times(3, 1, cos).then_inc(rope_cs, 1)

            def largest(m, s):
                i, count = s % 2, STEPS * m + s + 1
                dve.wait_ge(score_ready, count)
                dve.tensor_tensor(cross_sum[:], score[:, :, 1], mask[:].unsqueeze(1).to_broadcast([P, PARTS, SEQ]),
                                  ALU.add).then_inc(crossed, 1)
                dve.wait_ge(crossed, count)
                dve.tensor_tensor(probs[i][:], score[:, :, 0], cross_sum[:], ALU.add).then_inc(score_taken, 1)
                dve.wait_ge(score_taken, count)
                dve.tensor_reduce(nmax[i][:], probs[i][:], AX_X, ALU.max, negate=True).then_inc(max_ready, 1)

            def recip(m, s):
                i = s % 2
                dve.wait_ge(exp_ready, STEPS * m + s + 1)
                dve.reciprocal(rsum[i][:], sums[i][:]).then_inc(rsum_ready, 1)

            def turn(m, s):
                dve.wait_ge(pT_hi_done, STEPS * m + s + 1)
                dve.tensor_tensor(pT_lo[:], turned[:], as_f32(pT_hi[:]), ALU.subtract).then_inc(pT_lo_done, 1)

            def values(m, s):
                dve.wait_ge(val_hi_done, STEPS * m + s + 1)
                dve.tensor_tensor(val_lo[s % 2][:], value[:], as_f32(val_hi[s % 2][:]),
                                  ALU.subtract).then_inc(val_lo_done, 1)

            def add(m, s, bl, n, g):
                _, c = place(s)
                if bl == 0 and n == 0:
                    dve.wait_ge(acc_in[c], 16 * (g + 1))
                at = acc[:, BPC * c + 2 * (s % 2) + bl, n * CH:(n + 1) * CH]
                dve.wait_ge(out_ready, 4 * (STEPS * m + s) + 2 * bl + n + 1)
                dve.tensor_tensor(at, outb[n][:], at, ALU.add).then_inc(added, 1)

            def opening():
                for u in range(2):
                    rope(0, u, 0, 2 * u or None)
                    for h in range(PAIR):
                        latent(0, u, h, h)
                largest(0, 0)
                largest(0, 1)
                recip(0, 0)
                recip(0, 1)
                turn(0, 0)
                values(0, 0)

            def slot(m, s, end, of):
                if s + 1 < end:
                    turn(m, s + 1)
                if s + 2 < end:
                    largest(m, s + 2)
                add(m, s, 0, 0, of(s))
                if s + 2 < end:
                    recip(m, s + 2)
                add(m, s, 0, 1, of(s))
                if s // 2 + 2 < end // 2:
                    latent(m, s // 2 + 2, s % 2, USE[s])
                if s + 1 < end:
                    values(m, s + 1)
                add(m, s, 1, 0, of(s))
                add(m, s, 1, 1, of(s))
                if s in ROPE_CHUNK and end > STEPS:
                    c = ROPE_CHUNK[s]
                    rope(m + 1, c, USE[s] + 1, 2 * (ROPES * (m + 1) + c))

            quads(dve, opening, slot)


def cross(nc, x1_d, context, consts, x2_d):
    SETS = 5
    ctx = ExitStack()
    with ctx:
        def sb(name, shape, dt=F32):
            return ctx.enter_context(nc.sbuf_tensor(name, shape, dt))

        def many(n, name, shape, dt=F32):
            return [sb(f"{name}{i}", shape, dt) for i in range(n)]

        def banks(name, n=2):
            return [ctx.enter_context(nc.psum_tensor(f"{name}{i}", [P, CH], F32)) for i in range(n)]

        def sem(name):
            return ctx.enter_context(nc.semaphore(name))

        CUT = ((D, 2 * D), (0, D))
        xt = many(SETS, "cr_x", [P, D])
        y = many(SETS, "cr_y", [P, D])
        ctx_raw = many(SETS, "cr_ctx_raw", [P, 2 * D])
        ctx_hi = many(SETS, "cr_ctx_hi", [P, 2 * D], F32R)
        ctx_lo = many(SETS, "cr_ctx_lo", [P, 2 * D], F32R)
        hn = sb("cr_hn", [P, D])
        qT_hi = sb("cr_qT_hi", [P, KT, P], F32R)
        qT_lo = sb("cr_qT_lo", [P, KT, P], F32R)
        probs = sb("cr_probs", [P, SEQ])
        pT_hi = many(SETS, "cr_pT_hi", [P, SEQ], F32R)
        pT_lo = many(SETS, "cr_pT_lo", [P, SEQ], F32R)
        stats = sb("cr_stats", [P, 2, 6])
        mv = many(SETS, "cr_mv", [P, 2])
        var = many(SETS, "cr_var", [P, 1])
        rstd = many(SETS, "cr_rstd", [P, 1])
        nmax = many(SETS, "cr_nmax", [P, 1])
        total = many(SETS, "cr_total", [P, 1])
        rtotal = many(SETS, "cr_rtotal", [P, 1])
        power = sb("cr_power", [P, 1])
        ident = sb("cr_ident", [P, P])
        turned, out = banks("cr_turned"), banks("cr_out")
        score, pT = banks("cr_score", 1)[0], banks("cr_pT", 1)[0]

        const_in, power_set = sem("cr_const_in"), sem("cr_power_set")
        x_in = [sem(f"cr_x_in{i}") for i in range(SETS)]
        c_in = [sem(f"cr_c_in{i}") for i in range(SETS)]
        x2_out = [sem(f"cr_x2_out{i}") for i in range(SETS)]
        names = ("mv_done", "var_done", "rstd_done", "hn_ready", "turn_ready", "turn_hi", "turn_lo",
                 "ctx_hi_done", "ctx_lo_done", "score_ready", "max_ready", "exp_ready", "rtotal_ready", "pT_ready",
                 "pT_hi_done", "pT_lo_done", "out_ready")
        s = {n: sem(f"cr_{n}") for n in names}
        summed = sem("cr_summed")
        x1_b = x1_d.rearrange("(b p) d -> b p d", p=P)
        x2_b = x2_d.rearrange("(b p) d -> b p d", p=P)
        block = ctx.enter_context(nc.Block())

        def batches(eng, opening, turn):
            opening()
            loops = (BATCHES - 1) // SETS - 1
            with eng.Fori(0, loops) as n:
                for i in range(SETS):
                    turn(SETS * n + i + 1, i + 1, n, SETS)
            for b in range(SETS * loops + 1, BATCHES):
                turn(b, b - SETS * loops, loops, BATCHES - 1 - b)

        @block.sync
        def _(sp):
            def load_x(b, i):
                sp.dma_start(xt[i % SETS][:], x1_b[b]).then_inc(x_in[i % SETS], 16)

            def load_context(b, i):
                sp.dma_start(ctx_raw[i % SETS][:], context[b]).then_inc(c_in[i % SETS], 16)

            def store(b, i):
                sp.dma_start(x2_b[b], y[i % SETS][:]).then_inc(x2_out[i % SETS], 16)

            def opening():
                for i in range(SETS):
                    sp.sem_inc(x2_out[i], 16)
                for b in range(2):
                    load_x(b, b)
                    load_context(b, b)
                    if b == 0:
                        sp.dma_start(ident[:], consts["ident"]).then_inc(const_in, 16)
                for b in range(2, SETS):
                    load_x(b, b)
                    load_context(b, b)

            def turn(b, i, n, follow):
                sp.wait_ge(summed, 2 * b + 2)
                if follow >= SETS - 1:
                    load_x(b + SETS - 1, i - 1)
                store(b - 1, i - 1)
                if follow >= SETS - 1:
                    load_context(b + SETS - 1, i - 1)

            batches(sp, opening, turn)
            sp.wait_ge(summed, 2 * BATCHES + 2)
            store(BATCHES - 1, BATCHES - 1)
            for i in range(SETS):
                sp.wait_ge(x2_out[i], 16 * len(range(i, BATCHES, SETS)) + 16)

        @block.gpsimd
        def _(pool):
            pool.memset(power[:], -0.5).then_inc(power_set, 1)
            pool.wait_ge(power_set, 1)

            def prepare(b, i):
                i %= SETS
                pool.wait_ge(s["var_done"], b + 1)
                pool.tensor_tensor(rstd[i][:], var[i][:], power[:], ALU.pow).then_inc(s["rstd_done"], 1)
                for part, (lo, hi) in enumerate(CUT):
                    pool.wait_ge(s["ctx_hi_done"], 2 * b + part + 1)
                    pool.tensor_tensor(ctx_lo[i][:, lo:hi], ctx_raw[i][:, lo:hi], as_f32(ctx_hi[i][:, lo:hi]),
                                       ALU.subtract).then_inc(s["ctx_lo_done"], 1)

            def opening():
                for b in range(3):
                    prepare(b, b)

            def turn(b, i, n, follow):
                if follow >= 2:
                    prepare(b + 2, i + 2)

            batches(pool, opening, turn)

        @block.scalar
        def _(act):
            def cut(b, i, n):
                act.wait_ge(c_in[i], 16 * n)
                for lo, hi in CUT:
                    act.activation(ctx_hi[i][:, lo:hi], ctx_raw[i][:, lo:hi],
                                   ACT.Copy).then_inc(s["ctx_hi_done"], 1)

            def turn_hi(b):
                for half in range(2):
                    act.wait_ge(s["turn_ready"], 2 * b + half + 1)
                    act.activation(qT_hi[:, half * 4:half * 4 + 4, :],
                                   turned[half][:].rearrange("p (k s) -> p k s", k=4), ACT.Copy).then_inc(s["turn_hi"], 1)

            def exps(b, i):
                act.wait_ge(s["max_ready"], b + 1)
                act.activation(probs[:], score[:, 0:SEQ], ACT.Exp, bias=nmax[i][:, 0:1],
                               accum_out=total[i][:, 0:1]).then_inc(s["exp_ready"], 1)

            def probs_hi(b, i):
                act.wait_ge(s["pT_ready"], b + 1)
                act.activation(pT_hi[i][:], pT[:, 0:SEQ], ACT.Copy).then_inc(s["pT_hi_done"], 1)

            def opening():
                cut(0, 0, 1)
                turn_hi(0)
                cut(1, 1, 1)
                exps(0, 0)
                turn_hi(1)
                probs_hi(0, 0)
                cut(2, 2, 1)

            def turn(b, i, n, follow):
                exps(b, i % SETS)
                if follow >= 1:
                    turn_hi(b + 1)
                probs_hi(b, i % SETS)
                if follow >= 2:
                    cut(b + 2, (i + 2) % SETS, n + (i + 2) // SETS + 1)

            batches(act, opening, turn)

        @block.vector
        def _(dve):
            dve.sem_inc(summed, 2)

            def moments(b, i, n):
                dve.wait_ge(x_in[i], 16 * n)
                for h in range(2):
                    dve.bn_stats(stats[:, h, :], xt[i][:, h * 512:(h + 1) * 512])
                dve.drain()
                dve.bn_aggr(mv[i][:], stats[:].rearrange("p h s -> p (h s)")).then_inc(s["mv_done"], 1)
                dve.wait_ge(s["mv_done"], b + 1)
                dve.tensor_scalar(var[i][:], mv[i][:, 1:2], EPS, None, ALU.add).then_inc(s["var_done"], 1)

            def normalise(b, i):
                dve.wait_ge(s["rstd_done"], b + 1)
                dve.tensor_scalar(hn[:], xt[i][:], mv[i][:, 0:1], rstd[i][:, 0:1],
                                  ALU.subtract, ALU.mult).then_inc(s["hn_ready"], 1)

            def turn_lo(b):
                for half in range(2):
                    ks = slice(half * 4, half * 4 + 4)
                    dve.wait_ge(s["turn_hi"], 2 * b + half + 1)
                    dve.tensor_tensor(qT_lo[:, ks, :], turned[half][:].rearrange("p (k s) -> p k s", k=4),
                                      as_f32(qT_hi[:, ks, :]), ALU.subtract).then_inc(s["turn_lo"], 1)

            def largest(b, i):
                dve.wait_ge(s["score_ready"], b + 1)
                dve.tensor_reduce(nmax[i][:], score[:, 0:SEQ], AX_X, ALU.max, negate=True).then_inc(s["max_ready"], 1)

            def probs_lo(b, i):
                dve.wait_ge(s["pT_hi_done"], b + 1)
                dve.tensor_tensor(pT_lo[i][:], pT[:, 0:SEQ], as_f32(pT_hi[i][:]), ALU.subtract).then_inc(s["pT_lo_done"], 1)
                dve.wait_ge(s["exp_ready"], b + 1)
                dve.reciprocal(rtotal[i][:], total[i][:]).then_inc(s["rtotal_ready"], 1)

            def add(b, i, stores):
                dve.wait_ge(s["rtotal_ready"], b + 1)
                dve.wait_ge(x2_out[i % SETS], 16 * stores + 16)
                for c in range(2):
                    cols = slice(c * CH, (c + 1) * CH)
                    dve.wait_ge(s["out_ready"], 2 * b + c + 1)
                    dve.scalar_tensor_tensor(out=y[i % SETS][:, cols], in0=out[c][:], scalar=rtotal[i % SETS][:, 0:1],
                                             in1=xt[i % SETS][:, cols], op0=ALU.mult, op1=ALU.add).then_inc(summed, 1)

            def opening():
                moments(0, 0, 1)
                normalise(0, 0)
                moments(1, 1, 1)
                turn_lo(0)
                normalise(1, 1)
                largest(0, 0)
                turn_lo(1)
                probs_lo(0, 0)
                moments(2, 2, 1)
                largest(1, 1)
                normalise(2, 2)

            def turn(b, i, n, follow):
                if follow >= 2:
                    moments(b + 2, (i + 2) % SETS, n + (i + 2) // SETS + 1)
                if follow >= 1:
                    turn_lo(b + 1)
                probs_lo(b, i % SETS)
                add(b - 1, i - 1, n)
                if follow >= 2:
                    normalise(b + 2, (i + 2) % SETS)
                if follow >= 1:
                    largest(b + 1, (i + 1) % SETS)

            batches(dve, opening, turn)
            add(BATCHES - 1, BATCHES - 1, (BATCHES - 1) // SETS)

        @block.tensor
        def _(pe):
            pe.wait_ge(const_in, 16)

            def turn_hn(b, free):
                pe.wait_ge(s["hn_ready"], b + 1)
                for half in range(2):
                    if free is not None:
                        pe.wait_ge(s["turn_lo"], free + half)
                    for j in range(4):
                        k = half * 4 + j
                        ins = pe.transpose(turned[half][:, j * P:(j + 1) * P], hn[:, k * P:(k + 1) * P], ident[:])
                    ins.then_inc(s["turn_ready"], 1)

            def scores(b, i):
                pe.wait_ge(s["turn_lo"], 2 * (b + 1))
                pe.wait_ge(s["ctx_lo_done"], 2 * b + 1)
                for k in range(KT):
                    cols = slice(D + k * P, D + (k + 1) * P)
                    ins = three_passes(pe, score[:, 0:SEQ], qT_hi[:, k, :], qT_lo[:, k, :],
                                       ctx_hi[i][:, cols], ctx_lo[i][:, cols], k == 0, k == KT - 1)
                ins.then_inc(s["score_ready"], 1)

            def turn_probs(b, free):
                pe.wait_ge(s["exp_ready"], b + 1)
                if free is not None:
                    pe.wait_ge(s["pT_lo_done"], free)
                pe.transpose(pT[:, 0:SEQ], probs[:], ident[:]).then_inc(s["pT_ready"], 1)

            def outputs(b, i):
                pe.wait_ge(s["pT_lo_done"], b + 1)
                pe.wait_ge(s["ctx_lo_done"], 2 * (b + 1))
                for c in range(2):
                    cols = slice(c * CH, (c + 1) * CH)
                    pe.wait_ge(summed, 2 * b + c + 1)
                    three_passes(pe, out[c][:], pT_hi[i % SETS][:], pT_lo[i % SETS][:], ctx_hi[i % SETS][:, cols],
                                 ctx_lo[i % SETS][:, cols], True, True).then_inc(s["out_ready"], 1)

            def opening():
                turn_hn(0, None)
                scores(0, 0)
                turn_hn(1, 1)
                turn_probs(0, None)
                scores(1, 1)

            def turn(b, i, n, follow):
                if follow >= 1:
                    turn_hn(b + 1, 2 * b + 1)
                turn_probs(b, b)
                outputs(b - 1, i - 1)
                if follow >= 1:
                    scores(b + 1, (i + 1) % SETS)

            batches(pe, opening, turn)
            outputs(BATCHES - 1, BATCHES - 1)


def feed(nc, x2_d, signs, scales, consts, out_d):
    LAYERS = 3
    HID = 2 * KT
    ctx = ExitStack()
    with ctx:
        def sb(name, shape, dt=F32):
            return ctx.enter_context(nc.sbuf_tensor(name, shape, dt))

        def banks(name, n=2):
            return [ctx.enter_context(nc.psum_tensor(f"{name}{i}", [P, CH], F32)) for i in range(n)]

        def sem(name):
            return ctx.enter_context(nc.semaphore(name))

        w = [sb(f"ff_w{l}", [P, KT, D], F32R) for l in range(LAYERS)]
        xt = [sb(f"ff_x{i}", [P, BPC, D]) for i in range(2)]
        hn = sb("ff_hn", [P, 2, D])
        act_hi = [sb(f"ff_act_hi{i}", [P, KT, CH], F32R) for i in range(2)]
        act_lo = [sb(f"ff_act_lo{i}", [P, KT, CH], F32R) for i in range(2)]
        hid = sb("ff_hid", [P, 2, CH])
        stats = sb("ff_stats", [P, BPC, 2, 6])
        mv = sb("ff_mv", [P, BPC, 2])
        var = sb("ff_var", [P, BPC])
        rstd = sb("ff_rstd", [P, BPC])
        power = sb("ff_power", [P, BPC])
        ident = sb("ff_ident", [P, P])
        sign_mul = sb("ff_sign_mul", [P, KT])
        sign_add = sb("ff_sign_add", [P, KT])
        scale = sb("ff_scale", [P, LAYERS])
        scale2 = sb("ff_scale2", [P, LAYERS])
        bit_words = xt[1][:].rearrange("p b d -> p (b d)").bitcast(I32).rearrange("p (l k m) -> p l k m", l=2, k=KT)
        bits = xt[1][:].rearrange("p b d -> p (b d)").bitcast(U8).rearrange("p (l k m) -> p l k m", l=2, k=KT)

        turned, lin, outb = banks("ff_turned"), banks("ff_lin"), banks("ff_out")
        const_in, power_set, last_out = sem("ff_const_in"), sem("ff_power_set"), sem("ff_last_out")
        bits_in = [sem(f"ff_bits_in{l}") for l in range(LAYERS)]
        w_ready = [sem(f"ff_w_ready{l}") for l in range(LAYERS)]
        first_in = [sem(f"ff_first_in{t}") for t in range(BPC)]
        x_in = [sem(f"ff_x_in{i}") for i in range(2)]
        y_out = [sem(f"ff_y_out{i}") for i in range(2)]
        names = ("scale2_ready", "mv_done", "var_done", "rstd_done", "hn_ready", "turn_ready", "turn_hi",
                 "turn_lo", "lin_ready", "relu_done", "hid_hi", "hid_lo", "out_ready", "summed")
        s = {n: sem(f"ff_{n}") for n in names}
        x2_c = x2_d.rearrange("(c b p) d -> c p b d", c=CHUNKS, p=P)
        out_c = out_d.rearrange("(c b p) d -> c p b d", c=CHUNKS, p=P)
        block = ctx.enter_context(nc.Block())

        def chunks(eng, body):
            with eng.Fori(0, CHUNKS // 2 - 1) as n:
                body(2 * n, 0, n, False)
                body(2 * n + 1, 1, n + 1, False)
            body(CHUNKS - 2, 0, CHUNKS // 2 - 1, False)
            body(CHUNKS - 1, 1, 0, True)

        @block.sync
        def _(sp):
            for t in range(BPC):
                sp.dma_start(xt[0][:, t, :], x2_c[0][:, t, :]).then_inc(first_in[t], 16)
            for l in range(2):
                sp.dma_start(bit_words[:, l], signs[l]).then_inc(bits_in[l], 16)
                if l == 0:
                    for to, name in ((ident, "ident"), (sign_mul, "sign_mul"), (sign_add, "sign_add")):
                        sp.dma_start(to[:], consts[name]).then_inc(const_in, 16)
                    sp.dma_start(scale[:], scales).then_inc(const_in, 16)
            sp.wait_ge(w_ready[0], 2)
            sp.dma_start(bit_words[:, 0], signs[2]).then_inc(bits_in[2], 16)
            for l in range(1, LAYERS):
                sp.wait_ge(w_ready[l], 1)
            sp.dma_start(xt[1][:], x2_c[1]).then_inc(x_in[1], 16)

            def store(c, i):
                sp.wait_ge(s["summed"], 2 * BPC * (c + 1))
                sp.dma_start(out_c[c], xt[i][:]).then_inc(y_out[i], 16)

            with sp.Fori(0, CHUNKS // 2 - 1) as n:
                for i in range(2):
                    store(2 * n + i, i)
                    sp.wait_ge(y_out[i], 16 * (n + 1))
                    sp.dma_start(xt[i][:], x2_c[2 * n + 2 + i]).then_inc(x_in[i], 16)
            store(CHUNKS - 2, 0)
            for t in range(BPC):
                sp.wait_ge(s["summed"], 2 * (BPC * (CHUNKS - 1) + t + 1))
                sp.dma_start(out_c[CHUNKS - 1][:, t, :], xt[1][:, t, :]).then_inc(last_out, 16)
            sp.wait_ge(y_out[0], 16 * (CHUNKS // 2))
            sp.wait_ge(y_out[1], 16 * (CHUNKS // 2 - 1))
            sp.wait_ge(last_out, 16 * BPC)

        @block.gpsimd
        def _(pool):
            pool.memset(power[:], -0.5).then_inc(power_set, 1)
            pool.wait_ge(power_set, 1)

            def root(c):
                pool.wait_ge(s["var_done"], c + 1)
                pool.tensor_tensor(rstd[:], var[:], power[:], ALU.pow).then_inc(s["rstd_done"], 1)

            root(0)
            pool.wait_ge(bits_in[0], 16)
            for k in range(KT // 2, KT):
                ins = pool.tensor_scalar(w[0][:, k, :], bits[:, 0, k, :], 2.0, -1.0, ALU.mult, ALU.add)
            ins.then_inc(w_ready[0], 1)
            pool.wait_ge(const_in, 64)
            for l in (1, 2):
                pool.wait_ge(bits_in[l], 16)
                for k in range(KT):
                    ins = pool.tensor_scalar(w[l][:, k, :], bits[:, l % 2, k, :], sign_mul[:, k:k + 1],
                                             sign_add[:, k:k + 1], ALU.mult, ALU.add)
                ins.then_inc(w_ready[l], 1)
            chunks(pool, lambda c, i, n_next, last: None if last else root(c + 1))

        @block.scalar
        def _(act):
            def turn(c, i, t):
                for half in range(2):
                    act.wait_ge(s["turn_ready"], 2 * BPC * c + 2 * t + half + 1)
                    act.activation(act_hi[i][:, half * 4:half * 4 + 4, t * P:(t + 1) * P],
                                   turned[half][:].rearrange("p (k s) -> p k s", k=4), ACT.Copy).then_inc(s["turn_hi"], 1)

            def hidden(c, i, layer):
                to = act_hi[1 - i] if layer == 0 else act_hi[i]
                for m in range(KT):
                    a = HID * c + KT * layer + m
                    act.wait_ge(s["lin_ready"], a + 1)
                    if layer or m >= 2:
                        act.wait_ge(s["hid_lo"], a - 1)
                    act.activation(hid[:, m % 2, :], lin[m % 2][:], ACT.Relu,
                                   scale=scale2[:, layer:layer + 1]).then_inc(s["relu_done"], 1)
                    act.wait_ge(s["relu_done"], a + 1)
                    act.activation(to[:, m, :], hid[:, m % 2, :], ACT.Copy).then_inc(s["hid_hi"], 1)

            def body(c, i, n_next, last):
                hidden(c, i, 0)
                hidden(c, i, 1)
                if not last:
                    for t in range(BPC):
                        turn(c + 1, 1 - i, t)

            act.wait_ge(bits_in[0], 16)
            for k in range(KT // 2):
                ins = act.activation(w[0][:, k, :], bits[:, 0, k, :], ACT.Copy, scale=2.0, bias=-1.0)
            ins.then_inc(w_ready[0], 1)
            act.wait_ge(s["scale2_ready"], 1)
            for t in range(BPC):
                turn(0, 0, t)
            chunks(act, body)

        @block.vector
        def _(dve):
            def moments(c, i, n, first):
                if not first:
                    dve.wait_ge(x_in[i], 16 * (n + 1))
                for t in range(BPC):
                    if first:
                        dve.wait_ge(first_in[t], 16)
                    for h in range(2):
                        dve.bn_stats(stats[:, t, h, :], xt[i][:, t, h * 512:(h + 1) * 512])
                dve.drain()
                for t in range(BPC):
                    ins = dve.bn_aggr(mv[:, t, :], stats[:, t].rearrange("p h s -> p (h s)"))
                ins.then_inc(s["mv_done"], 1)
                dve.wait_ge(s["mv_done"], c + 1)
                dve.tensor_scalar(var[:], mv[:, :, 1], EPS, None, ALU.add).then_inc(s["var_done"], 1)

            def normalise(c, i, t):
                if t == 0:
                    dve.wait_ge(s["rstd_done"], c + 1)
                dve.tensor_scalar(hn[:, t % 2, :], xt[i][:, t, :], mv[:, t, 0:1], rstd[:, t:t + 1],
                                  ALU.subtract, ALU.mult).then_inc(s["hn_ready"], 1)

            def turn(c, i, t):
                for half in range(2):
                    at = (slice(None), slice(half * 4, half * 4 + 4), slice(t * P, (t + 1) * P))
                    dve.wait_ge(s["turn_hi"], 2 * BPC * c + 2 * t + half + 1)
                    dve.tensor_tensor(act_lo[i][at], turned[half][:].rearrange("p (k s) -> p k s", k=4),
                                      as_f32(act_hi[i][at]), ALU.subtract).then_inc(s["turn_lo"], 1)

            def hidden(c, i, layer):
                at = 1 - i if layer == 0 else i
                for m in range(KT):
                    dve.wait_ge(s["hid_hi"], HID * c + KT * layer + m + 1)
                    dve.tensor_tensor(act_lo[at][:, m, :], hid[:, m % 2, :], as_f32(act_hi[at][:, m, :]),
                                      ALU.subtract).then_inc(s["hid_lo"], 1)

            def body(c, i, n_next, last):
                hidden(c, i, 0)
                if not last:
                    moments(c + 1, 1 - i, n_next, False)
                    normalise(c + 1, 1 - i, 0)
                    normalise(c + 1, 1 - i, 1)
                hidden(c, i, 1)
                for t in range(BPC):
                    for n in range(2):
                        cols = slice(n * CH, (n + 1) * CH)
                        dve.wait_ge(s["out_ready"], 2 * BPC * c + 2 * t + n + 1)
                        dve.scalar_tensor_tensor(out=xt[i][:, t, cols], in0=outb[n][:], scalar=scale[:, 2:3],
                                                 in1=xt[i][:, t, cols], op0=ALU.mult, op1=ALU.add).then_inc(s["summed"], 1)
                    if not last:
                        turn(c + 1, 1 - i, t)
                        if t + 2 < BPC:
                            normalise(c + 1, 1 - i, t + 2)

            dve.sem_inc(x_in[0], 16)
            moments(0, 0, 0, True)
            normalise(0, 0, 0)
            normalise(0, 0, 1)
            dve.wait_ge(const_in, 64)
            dve.tensor_scalar(scale2[:], scale[:], 2.0, None, ALU.mult).then_inc(s["scale2_ready"], 1)
            for t in range(BPC):
                turn(0, 0, t)
                if t + 2 < BPC:
                    normalise(0, 0, t + 2)
            chunks(dve, body)

        @block.tensor
        def _(pe):
            def turn(c, i, t):
                pe.wait_ge(s["hn_ready"], BPC * c + t + 1)
                for half in range(2):
                    if t:
                        pe.wait_ge(s["turn_lo"], 2 * BPC * c + 2 * (t - 1) + half + 1)
                    for j in range(4):
                        k = half * 4 + j
                        ins = pe.transpose(turned[half][:, j * P:(j + 1) * P], hn[:, t % 2, k * P:(k + 1) * P], ident[:])
                    ins.then_inc(s["turn_ready"], 1)

            def hidden(c, i, layer):
                at = i if layer == 0 else 1 - i
                if layer == 0:
                    pe.wait_ge(s["turn_lo"], 2 * BPC * (c + 1))
                pe.wait_ge(w_ready[layer], 1 if layer else 2)
                for m in range(KT):
                    a = HID * c + KT * layer + m
                    if layer or m >= 2:
                        pe.wait_ge(s["relu_done"], a - 1)
                    for k in range(KT):
                        if layer and m == 0:
                            pe.wait_ge(s["hid_lo"], HID * c + k + 1)
                        wk = w[layer][:, k, m * P:(m + 1) * P]
                        pe.matmul(lin[m % 2][:], wk, act_hi[at][:, k, :], start=k == 0, stop=False)
                        ins = pe.matmul(lin[m % 2][:], wk, act_lo[at][:, k, :], start=False, stop=k == KT - 1)
                    ins.then_inc(s["lin_ready"], 1)

            def body(c, i, n_next, last):
                hidden(c, i, 0)
                hidden(c, i, 1)
                pe.wait_ge(w_ready[2], 1)
                for t in range(BPC):
                    for n in range(2):
                        if t:
                            pe.wait_ge(s["summed"], 2 * BPC * c + 2 * (t - 1) + n + 1)
                        for k in range(KT):
                            if t == 0 and n == 0:
                                pe.wait_ge(s["hid_lo"], HID * c + KT + k + 1)
                            rows = slice(t * P, (t + 1) * P)
                            wk = w[2][:, k, n * CH:(n + 1) * CH]
                            pe.matmul(outb[n][:], act_hi[i][:, k, rows], wk, start=k == 0, stop=False)
                            ins = pe.matmul(outb[n][:], act_lo[i][:, k, rows], wk, start=False, stop=k == KT - 1)
                        ins.then_inc(s["out_ready"], 1)
                    if not last:
                        turn(c + 1, 1 - i, t)

            pe.wait_ge(const_in, 64)
            for t in range(BPC):
                turn(0, 0, t)
            chunks(pe, body)


def build(nc, a, out):
    def scratch(name, shape):
        return nc.dram_tensor(name, shape, F32, kind="Internal").ap()

    tok_d = scratch("tok_d", [CHUNKS, P, PACK])
    wh_d = scratch("wh_d", [PAIRS, P, PAIR, WH])
    x1_d = scratch("x1_d", [TOKENS, D])
    x2_d = scratch("x2_d", [TOKENS, D])
    prepare(nc, a["x"], a["w_down"], a["w_heads"], a, tok_d, wh_d)
    attend(nc, a["x"], tok_d, wh_d, a["w_rope"], a, x1_d)
    cross(nc, x1_d, a["context"], a, x2_d)
    feed(nc, x2_d, a["signs"], a["scales"], a, out)


def constants():
    half = np.arange(0, DR, 2, dtype=np.float32) / np.float32(DR)
    freqs = np.float32(1.0) / np.power(np.float32(10000.0), half)
    wave = np.float32(2.0 * np.pi) / freqs
    ramp = np.clip((wave / np.float32(4096.0) - np.float32(1.0)) / np.float32(31.0), 0, 1).astype(np.float32)
    inv = freqs / (np.float32(1.0) - ramp + ramp * np.float32(40.0))
    angle = (np.arange(SEQ, dtype=np.float32)[None, :] * inv[:, None]).astype(np.float32)
    cos, sin = np.cos(angle).astype(np.float32), np.sin(angle).astype(np.float32)
    sc = np.float32(SCORE_SCALE)
    row = np.arange(KT * P).reshape(KT, P).T
    inhibitory = row >= round(D * 0.8)
    return {
        "ident": np.eye(P, dtype=np.float32),
        "mask": np.where(np.tril(np.ones((SEQ, SEQ), bool)), 0, MASKED).astype(np.float32),
        "cos": np.tile(cos, (QUAD, 1)),
        "sin": np.tile(sin, (QUAD, 1)),
        "k_tab": np.concatenate([cos * sc, cos * sc, -sin * sc, sin * sc]),
        "sign_mul": np.where(inhibitory, -8, 2).astype(np.float32),
        "sign_add": np.where(inhibitory, 4, -1).astype(np.float32),
    }


def kernel(x, ctx_4096, L0_attn_w_q_down, L0_attn_w_q_up_nope, L0_attn_w_q_up_rope, L0_attn_w_kv_down,
           L0_attn_w_k_rope, L0_attn_w_uk, L0_attn_w_uv, L0_attn_w_out, L0_ffn_k0, L0_ffn_s0, L0_ffn_k1,
           L0_ffn_s1, L0_ffn_k2, L0_ffn_s2):
    import concourse.bacc as bacc
    from concourse.bass_utils import run_bass_kernel_spmd

    x, ctx_4096 = np.asarray(x), np.asarray(ctx_4096)
    wkr = np.asarray(L0_attn_w_k_rope)
    w_down = np.concatenate([np.asarray(L0_attn_w_q_down), np.asarray(L0_attn_w_kv_down), wkr,
                             wkr[:, HALF:], wkr[:, :HALF]], axis=1)
    w_down = w_down.reshape(KT, P, 5 * P).transpose(1, 0, 2)
    nope_t = np.asarray(L0_attn_w_q_up_nope).reshape(QL, HEADS, DN).transpose(1, 2, 0)
    heads = np.concatenate([nope_t, np.asarray(L0_attn_w_uk).reshape(HEADS, DN, KVL),
                            np.asarray(L0_attn_w_uv).reshape(HEADS, DV, KVL),
                            np.asarray(L0_attn_w_out).reshape(HEADS, DV, D)], axis=2)
    w_rope = np.asarray(L0_attn_w_q_up_rope).reshape(QT, P, QUADS, QUAD, 2, HALF).transpose(2, 1, 0, 4, 3, 5)
    w_rope = w_rope.reshape(QUADS, P, QT, 2, P)
    ctx_t = ctx_4096.reshape(BATCHES, SEQ, KT, P).transpose(0, 3, 2, 1).reshape(BATCHES, P, KT * SEQ)
    context = np.concatenate([ctx_4096, ctx_t], axis=2)
    signs = np.stack([np.asarray(k).reshape(KT, P, D).transpose(1, 0, 2)
                      for k in (L0_ffn_k0, L0_ffn_k1, L0_ffn_k2)]).view(np.int32)
    scales = np.broadcast_to(np.stack([np.asarray(s).reshape(()) for s in (L0_ffn_s0, L0_ffn_s1, L0_ffn_s2)]), (P, 3))
    arrays = {"x": x.reshape(TOKENS, D), "w_down": w_down, "w_heads": heads, "w_rope": w_rope, "context": context,
              "signs": signs, "scales": scales, **constants()}
    arrays = {name: np.ascontiguousarray(v) for name, v in arrays.items()}

    nc = bacc.Bacc("TRN2", target_bir_lowering=False, num_devices=1)
    a = {name: nc.dram_tensor(f"in_{name}", v.shape, mybir.dt.from_np(v.dtype), kind="ExternalInput").ap()
         for name, v in arrays.items()}
    out = nc.dram_tensor("out", [TOKENS, D], F32, kind="ExternalOutput").ap()
    build(nc, a, out)
    r = run_bass_kernel_spmd(nc, [{f"in_{name}": v for name, v in arrays.items()}], core_ids=[0])
    return r.results[0]["out"].reshape(BATCHES, SEQ, D)
```
